# Optimizing a Trainium2 kernel written in Bass

```python
import numpy as np
import jax
import jax.numpy as jnp

def _softmax(x, axis=-1):
    return jax.nn.softmax(x, axis=axis)

def _gelu(x):
    return jax.nn.gelu(x, approximate=True)

def _silu(x):
    return jax.nn.silu(x)

def _sigmoid(x):
    return jax.nn.sigmoid(x)

def _layernorm(x, axis=-1, eps=1e-05):
    m = jnp.mean(x, axis=axis, keepdims=True)
    v = jnp.var(x, axis=axis, keepdims=True)
    return (x - m) / jnp.sqrt(v + eps)

def _scatter_add(tgt, idx, src, axis=0):
    return tgt.at[idx].add(src)

def _segment_sum(src, seg, n):
    return jax.ops.segment_sum(src, seg, n)
kernel_name = 'mk_xattn_ffn_d1_seqx_r4_6b61cf'

def setup_inputs(seed: int=0):
    np.random.seed(seed)
    _w = jnp.asarray

    def _rec_inputs():
        import jax
        import jax.numpy as jnp
        _rk = jax.random.key(seed)
        x = -0.0003929 + 0.9999 * jax.random.normal(jax.random.fold_in(_rk, 1), (16, 512, 256), jnp.float32)
        _lenS = 512 - jax.random.randint(jax.random.fold_in(_rk, 7), (16,), 0, max(1, 512 // 4) + 1, jnp.int32)
        _lenS2 = 1601 - jax.random.randint(jax.random.fold_in(_rk, 8), (16,), 0, max(1, 1601 // 4) + 1, jnp.int32)
        _ctx_1024P = jax.random.normal(jax.random.fold_in(_rk, 11), (16, 16, 256), jnp.float32)
        _ctx_1024c = jax.random.dirichlet(jax.random.fold_in(_rk, 511), 0.3 * jnp.ones((16,), jnp.float32), (16, 1601))
        _ctx_1024t = jnp.einsum('bsk,bkd->bsd', _ctx_1024c, _ctx_1024P)
        _ctx_1024t = _ctx_1024t * jax.lax.rsqrt(jnp.mean(jnp.square(_ctx_1024t)) + 1e-12) * 0.953939
        ctx_1024 = 2.81802e-05 + 1.00001 * (_ctx_1024t + 0.3 * jax.random.normal(jax.random.fold_in(_rk, 611), (16, 1601, 256), jnp.float32))
        _validS = jnp.arange(512)[None, :] < _lenS[:, None]
        _validS2 = jnp.arange(1601)[None, :] < _lenS2[:, None]
        _causal = jnp.tril(jnp.ones((512, 512), dtype=bool))
        mask_BxSxS2_ik1 = jnp.where(jnp.broadcast_to(_validS2[:, None, :], (16, 512, 1601)), 1, 0).astype(jnp.int32)
        return (x, ctx_1024, mask_BxSxS2_ik1)
    x, ctx_1024, mask_BxSxS2_ik1 = _rec_inputs()

    def _L0_xattn_setup():
        import jax, jax.numpy as jnp
        import numpy as np
        B, L, H = (8, 512, 256)
        SCALE = float(np.sqrt(H))
        EPS = 1e-05
        key = jax.random.key(seed)
        ks = jax.random.split(key, 12)
        s = 1.0 / np.sqrt(H)
        return {'queries': jax.random.normal(ks[0], (B, L, H), jnp.float32), 'keys': jax.random.normal(ks[1], (B, L, H), jnp.float32), 'values': jax.random.normal(ks[2], (B, L, H), jnp.float32), 'mask': jax.random.randint(ks[3], (B, L, L), 0, 2, jnp.int32), 'Wq': jax.random.normal(ks[4], (H, H), jnp.float32) * s, 'bq': jnp.zeros((H,), jnp.float32), 'Wk': jax.random.normal(ks[5], (H, H), jnp.float32) * s, 'bk': jnp.zeros((H,), jnp.float32), 'Wv': jax.random.normal(ks[6], (H, H), jnp.float32) * s, 'bv': jnp.zeros((H,), jnp.float32), 'ln_gamma': jnp.ones((H,), jnp.float32), 'ln_beta': jnp.zeros((H,), jnp.float32)}
    _L0_xattn_all = _L0_xattn_setup()
    _L0_xattn_in = {k: v for k, v in _L0_xattn_all.items() if k in ('Wq', 'bq', 'Wk', 'bk', 'Wv', 'bv', 'ln_gamma', 'ln_beta')}
    del _L0_xattn_all

    def _L0_ffn_setup():
        import jax, jax.numpy as jnp
        import numpy as np
        key = jax.random.key(seed)
        ks = jax.random.split(key, 5)
        B, Sq, M, E, H = (4, 512, 256, 8, 1024)
        x = jax.random.normal(ks[0], (B, Sq, M), dtype=jnp.float32)
        wg = jax.random.normal(ks[1], (M, E), dtype=jnp.float32) * (1.0 / np.sqrt(M))
        w1 = jax.random.normal(ks[2], (E, M, H), dtype=jnp.float32) * (1.0 / np.sqrt(M))
        b1 = jnp.zeros((E, H), dtype=jnp.float32)
        w2 = jax.random.normal(ks[3], (E, H, M), dtype=jnp.float32) * (1.0 / np.sqrt(H))
        b2 = jnp.zeros((E, M), dtype=jnp.float32)
        return {'x': x, 'wg': wg, 'w1': w1, 'b1': b1, 'w2': w2, 'b2': b2}
    _L0_ffn_all = _L0_ffn_setup()
    _L0_ffn_in = {k: v for k, v in _L0_ffn_all.items() if k in ('wg', 'w1', 'b1', 'w2', 'b2')}
    del _L0_ffn_all
    return {'x': x, 'ctx_1024': ctx_1024, 'mask_BxSxS2_ik1': mask_BxSxS2_ik1, 'L0_xattn_Wq': _L0_xattn_in['Wq'], 'L0_xattn_bq': _L0_xattn_in['bq'], 'L0_xattn_Wk': _L0_xattn_in['Wk'], 'L0_xattn_bk': _L0_xattn_in['bk'], 'L0_xattn_Wv': _L0_xattn_in['Wv'], 'L0_xattn_bv': _L0_xattn_in['bv'], 'L0_xattn_ln_gamma': _L0_xattn_in['ln_gamma'], 'L0_xattn_ln_beta': _L0_xattn_in['ln_beta'], 'L0_ffn_wg': _L0_ffn_in['wg'], 'L0_ffn_w1': _L0_ffn_in['w1'], 'L0_ffn_b1': _L0_ffn_in['b1'], 'L0_ffn_w2': _L0_ffn_in['w2'], 'L0_ffn_b2': _L0_ffn_in['b2']}

def reference(x, ctx_1024, mask_BxSxS2_ik1, L0_xattn_Wq, L0_xattn_bq, L0_xattn_Wk, L0_xattn_bk, L0_xattn_Wv, L0_xattn_bv, L0_xattn_ln_gamma, L0_xattn_ln_beta, L0_ffn_wg, L0_ffn_w1, L0_ffn_b1, L0_ffn_w2, L0_ffn_b2):
    import jax
    import jax.numpy as jnp

    def _L0_xattn_ref(queries, keys, values, mask, Wq, bq, Wk, bk, Wv, bv, ln_gamma, ln_beta):
        import jax, jax.numpy as jnp
        import numpy as np
        B, L, H = (8, 512, 256)
        SCALE = float(np.sqrt(H))
        EPS = 1e-05
        Q = queries @ Wq + bq
        K = keys @ Wk + bk
        V = values @ Wv + bv
        scores = jnp.einsum('bik,bjk->bij', Q, K) / SCALE
        scores = jnp.where(mask == 0, -jnp.inf, scores)
        probs = jax.nn.softmax(scores, axis=-1)
        context = jnp.einsum('bij,bjk->bik', probs, V)
        mu = jnp.mean(context, axis=-1, keepdims=True)
        var = jnp.var(context, axis=-1, keepdims=True)
        normed = (context - mu) * jax.lax.rsqrt(var + EPS)
        return normed * ln_gamma + ln_beta

    def _L0_ffn_ref(x, wg, w1, b1, w2, b2):
        import jax, jax.numpy as jnp
        import numpy as np
        B, Sq, M = x.shape
        E = wg.shape[1]
        S = B * Sq
        C = S // E
        xt = x.reshape(S, M)
        gates = jax.nn.softmax(xt @ wg, axis=-1)
        expert_idx = jnp.argmax(gates, axis=-1)
        mask1 = jax.nn.one_hot(expert_idx, E, dtype=xt.dtype)
        locations = jnp.cumsum(mask1, axis=0) - 1.0
        pos = jnp.sum(locations * mask1, axis=1).astype(jnp.int32)
        keep = (pos < C).astype(xt.dtype)
        gate_val = jnp.sum(gates * mask1, axis=1) * keep
        slot = expert_idx.astype(jnp.int32) * C + jnp.clip(pos, 0, C - 1)
        disp = jnp.zeros((E * C, M), dtype=xt.dtype).at[slot].add(xt * keep[:, None])
        disp = disp.reshape(E, C, M)
        h = jax.nn.relu(jnp.einsum('ecm,emh->ech', disp, w1) + b1[:, None, :])
        eo = jnp.einsum('ech,ehm->ecm', h, w2) + b2[:, None, :]
        out = eo.reshape(E * C, M)[slot] * gate_val[:, None]
        return out.reshape(B, Sq, M)
    x = x + _L0_xattn_ref(_layernorm(x, axis=-1), ctx_1024, ctx_1024, mask_BxSxS2_ik1, L0_xattn_Wq, L0_xattn_bq, L0_xattn_Wk, L0_xattn_bk, L0_xattn_Wv, L0_xattn_bv, L0_xattn_ln_gamma, L0_xattn_ln_beta)
    x = x + _L0_ffn_ref(_layernorm(x, axis=-1), L0_ffn_wg, L0_ffn_w1, L0_ffn_b1, L0_ffn_w2, L0_ffn_b2)
    return x

_drawn_inputs = setup_inputs


def setup_inputs(seed=0):
    import zlib

    import numpy as np

    out = dict(_drawn_inputs(seed))
    spreads = {'L0_xattn_bq': (0.0, 0.1),
     'L0_xattn_bk': (0.0, 0.8),
     'L0_xattn_bv': (0.0, 0.1),
     'L0_xattn_ln_gamma': (1.0, 0.2),
     'L0_xattn_ln_beta': (0.0, 0.1),
     'L0_ffn_b1': (0.0, 0.481),
     'L0_ffn_b2': (0.0, 0.341)}
    factors = {}
    for name, (base, spread) in spreads.items():
        noise = np.random.default_rng([zlib.crc32(name.encode()), seed]).standard_normal(out[name].shape)
        drawn = base * np.exp(spread * noise) if base else spread * noise
        out[name] = jnp.asarray(drawn.astype(out[name].dtype))
    for name, factor in factors.items():
        out[name] = (out[name] * factor).astype(out[name].dtype)
    return out
```

```python
from contextlib import ExitStack

import concourse.bass as bass
from concourse import mybir

ALU = mybir.AluOpType
ACT = mybir.ActivationFunctionType
AX = mybir.AxisListType
F32 = mybir.dt.float32
F32R = mybir.dt.float32r
BF16 = mybir.dt.bfloat16
I32 = mybir.dt.int32
U32 = mybir.dt.uint32

P = 128
NB, SQ, D = 16, 512, 256
SK = 1601
KT = D // P
QT = SQ // P
NT = NB * QT
JF = SK // P
JR = SK - JF * P
JT = JF + 1
CH = 512
NC = (SK + CH - 1) // CH
CW = 2 * ((SK + 2 * NC - 1) // (2 * NC))
SKP = NC * CW
EXPERTS, HID = 8, 1024
TOKENS = NB * SQ
CAP = TOKENS // EXPERTS
ROW = D + 4
SCALE = 1.0 / float(D) ** 0.5
EPS = 1e-5
MASKED = -1e30
NOWHERE = 65536.0
FIRST_STEP, LAST_STEP = -QT, NT + QT


class Pipeline:

    def __init__(self, name, first, loop_from, period, loops, last):
        self.name = name
        self.first, self.loop_from, self.period, self.loops, self.last = first, loop_from, period, loops, last

    def run(self, eng, step):
        counts = [eng.alloc_register(f"{self.name}{n}") for n in range(3)]
        for t in range(self.first, self.loop_from):
            step(At(self, t))
        with eng.Fori(0, self.loops) as it:
            for u in range(self.period):
                step(At(self, self.loop_from + u, it, counts))
        for t in range(self.loop_from + self.loops * self.period, self.last + 1):
            step(At(self, t))


class At:

    def __init__(self, pipe, t, it=None, counts=()):
        self.pipe, self.t, self.it, self.counts = pipe, t, it, counts
        self.batch, self.quarter = t // QT, t % QT

    def value(self, f):
        v = f(self.t)
        if self.it is None:
            return v
        by = f(self.t + self.pipe.period) - v
        assert all(f(self.t + n * self.pipe.period) == v + n * by for n in range(self.pipe.loops))
        return v + self.it * by

    def wait(self, eng, sem, f):
        v = self.value(f)
        if not isinstance(v, int) or v > 0:
            eng.wait_ge(sem, v)

    def wait_apart(self, eng, met, *waits):
        values = [(sem, self.value(f)) for sem, f in waits]
        for n, (sem, v) in enumerate(values):
            if not isinstance(v, int):
                eng.reg_mov(self.counts[n], v)
                values[n] = (sem, self.counts[n])
        if self.it is not None:
            eng.wait_ge(*met)
        for sem, v in values:
            if not isinstance(v, int) or v > 0:
                eng.wait_ge(sem, v)


ATTENTION = Pipeline("attention", FIRST_STEP, 2 * QT, 2 * QT, NB // 2 - 2, LAST_STEP)


def tile_ok(t):
    return 0 <= t < NT


def batch_ok(b):
    return 0 <= b < NB


def turn_groups(t):
    out = []
    if tile_ok(t - 1):
        out += [("probs", t - 1, c) for c in range(NC)]
    if tile_ok(t - 3):
        out.append(("xn2", t - 3, 0))
    if tile_ok(t - 2):
        out.append(("attn", t - 2, 0))
    b, r = t // QT + 1, t % QT
    if batch_ok(b):
        out += [("ctx", b, 2 * r), ("ctx", b, 2 * r + 1)]
        if r == 1:
            out += [("xn", b, 0), ("xn", b, 1)]
        if r == 2:
            out += [("qk", b, 0), ("qk", b, 1)]
    return out


def small_groups(t):
    out = []
    if tile_ok(t - 3):
        out.append(("logits", t - 3))
    if tile_ok(t - 2):
        out.append(("value", t - 2))
    b, r = t // QT + 1, t % QT
    if batch_ok(b) and r == 2:
        out.append(("keybias", b))
    if batch_ok(b - 2) and r == 3:
        out.append(("places", b - 2))
    return out


SETUP_TURNS = [("setup", 0, n) for n in range(3)]
SPLIT_KINDS = ("probs", "ctx", "qk")
TURNS = SETUP_TURNS + [g for t in range(FIRST_STEP, LAST_STEP + 1) for g in turn_groups(t)]
TURN_NO = {g: n for n, g in enumerate(TURNS)}
SPLITS = {g: n for n, g in enumerate(g for g in TURNS if g[0] in SPLIT_KINDS)}
SETUP_SMALL = [("setup", 0)]
READ_BY_ACT = ("logits",)
SMALLS = SETUP_SMALL + [g for t in range(FIRST_STEP, LAST_STEP + 1) for g in small_groups(t)]
SMALL_NO = {g: n for n, g in enumerate(SMALLS)}
SMALL_READ = {g: n for n, g in enumerate(g for g in SMALLS if g[0] not in READ_BY_ACT)}


def nth(table, group, t0, per=1):
    kind, of, *rest = group

    def f(t):
        shift = (t - t0) // per
        return table[(kind, of + shift, *rest)] + 1
    return f


def attention(nc, dram, keep):
    with ExitStack() as ctx:
        def sb(name, shape, dt=F32):
            return ctx.enter_context(nc.sbuf_tensor(name, shape, dt))

        def sem(name):
            return ctx.enter_context(nc.semaphore(name))

        ident = keep["ident"]
        tri = sb("tri", [P, P], BF16)
        ones = sb("ones", [P, P], BF16)
        halves = sb("halves", [P, QT])
        rank = sb("rank", [P, QT, EXPERTS])
        token = sb("token", [P, QT])
        wv = sb("wv", [P, KT, D])
        wg = sb("wg", [P, KT, EXPERTS])
        bq = sb("bq", [P, KT])
        bk = sb("bk", [P, KT])
        mqk = sb("mqk", [P, KT, D])
        qbias = sb("qbias", [P, KT])
        kbias = sb("kbias", [P, KT])
        bqk = sb("bqk", [P, 1])
        bqw = sb("bqw", [P, KT, P])
        bv_all = sb("bv_all", [P, D])
        gamma_all = sb("gamma_all", [P, D])
        beta_all = sb("beta_all", [P, D])

        ctx_in = sb("ctx_in", [P, JT, D])
        ctx_hi = [sb(f"ctx_hi{n}", [P, JT, D], F32R) for n in range(2)]
        ctx_lo = [sb(f"ctx_lo{n}", [P, JT, D], F32R) for n in range(2)]
        ctxT_hi = [sb(f"ctxT_hi{n}", [P, KT, SKP], F32R) for n in range(2)]
        ctxT_lo = [sb(f"ctxT_lo{n}", [P, KT, SKP], F32R) for n in range(2)]
        xb = sb("xb", [P, QT, D])
        xnT = sb("xnT", [P, KT, SQ])
        qkT_hi = [sb(f"qkT_hi{n}", [P, KT, SQ], F32R) for n in range(2)]
        qkT_lo = [sb(f"qkT_lo{n}", [P, KT, SQ], F32R) for n in range(2)]
        kb16 = [sb(f"kb16_{n}", [P, QT]) for n in range(2)]
        mask_in = sb("mask_in", [P, SK], I32)
        mask_add = [sb(f"mask_add{n}", [P, SKP], BF16) for n in range(2)]
        probs = sb("probs", [P, SKP])
        probsT_hi = sb("probsT_hi", [P, JT, P], F32R)
        probsT_lo = sb("probsT_lo", [P, JT, P], F32R)
        wq, wk = (probs[:, n * KT * D:(n + 1) * KT * D].rearrange("p (k n) -> p k n", k=KT) for n in range(2))
        wq_t, wk_t = (xnT[:, n, :].rearrange("p (k n) -> p k n", k=KT) for n in range(2))
        rowmax = sb("rowmax", [P, 2])
        fullmax = sb("fullmax", [P, 2])
        negmax = sb("negmax", [P, 2])
        rowsum = sb("rowsum", [P, 2])
        rsum = sb("rsum", [P, 2])
        attn = sb("attn", [P, D])
        attnT = sb("attnT", [P, KT, P])
        xres = [sb(f"xres{n}", [P, D]) for n in range(4)]
        value = sb("value", [P, D])
        scaled = sb("scaled", [P, D])
        bn1 = sb("bn1", [P, 6])
        mv1 = sb("mv1", [P, 2])
        ve1 = sb("ve1", [P, 1])
        rstd1 = sb("rstd1", [P, 1])
        bn2 = sb("bn2", [P, 6])
        mv2 = sb("mv2", [P, 2])
        ve2 = sb("ve2", [P, 1])
        bnx = sb("bnx", [P, QT, 6])
        mvx = sb("mvx", [P, QT, 2])
        vex = sb("vex", [P, QT])
        rstdx = sb("rstdx", [P, QT])
        row = [sb(f"row{n}", [P, QT, ROW]) for n in range(2)]
        xn2 = sb("xn2", [P, D])
        xn2T = sb("xn2T", [P, KT, P])
        logits = sb("logits", [P, QT, EXPERTS])
        best = sb("best", [P, QT])
        below = sb("below", [P, QT, EXPERTS])
        gates = sb("gates", [P, QT, EXPERTS])
        gsum = sb("gsum", [P, QT])
        tied = sb("tied", [P, QT, EXPERTS])
        pick = sb("pick", [P, QT])
        onehot = sb("onehot", [P, QT, EXPERTS], BF16)
        added = sb("added", [P, EXPERTS])
        count = sb("count", [P, EXPERTS])
        countb = sb("countb", [P, EXPERTS], BF16)
        placed = sb("placed", [P, QT, EXPERTS])
        place = sb("place", [P, QT])
        base = sb("base", [P, QT])
        over = sb("over", [P, QT])
        slotf = sb("slotf", [P, QT])
        slot = [sb(f"slot{n}", [P, QT], U32) for n in range(2)]
        blank = sb("blank", [P, ROW])

        scores = ctx.enter_context(nc.psum_tensor("scores", [P, NC, CH], F32))
        turn = [ctx.enter_context(nc.psum_tensor(f"turn{n}", [P, CH], F32)) for n in range(2)]
        outp = ctx.enter_context(nc.psum_tensor("outp", [P, CH], F32))
        small = ctx.enter_context(nc.psum_tensor("small", [P, CH], F32))

        S = {}
        for name in ("consts weights_in bcast_in blank_set blanks_out "
                     "turn_full turn_evac turn_low small_full small_read logits_read setup_done "
                     "x_in ctx_in_a mask_in xres_in0 xres_in1 xres_in2 xres_in3 "
                     "scores_full mask_ready max_raw max_full max_neg exp_done sum_inv "
                     "out_full attn_ready ctx_hi_done ctx_lo_done xres_beta "
                     "value_set bn1_set mv1_set var1 rstd1 scaled_set x1_done bn2_set mv2_set var2 rstd2 xn2_done "
                     "bnx_set mvx_set varx rstdx xnorm_done "
                     "best_set below_set gates_done tied_set pick_set onehot_done added_set count_set countb_set "
                     "placed_set place_set base_set over_set part_set slot_ready gsum_set gate_done token_set token_next "
                     "store0 store1 scatter0 scatter1").split():
            S[name] = sem(name)
        MET = (S["consts"], 14)
        store_done = [S["store0"], S["store1"]]
        scatter_done = [S["scatter0"], S["scatter1"]]
        xres_in = [S[f"xres_in{n}"] for n in range(4)]

        x_v = dram["x"].rearrange("b (i p) d -> b p i d", p=P)
        ctx_v = dram["ctx"]
        mask_v = dram["mask"].rearrange("b (i p) k -> (b i) p k", p=P)
        x_t = dram["x"].rearrange("b (i p) d -> (b i) p d", p=P)
        out_t = dram["out"].rearrange("b (i p) d -> (b i) p d", p=P)
        slots = dram["slots"]

        block = ctx.enter_context(nc.Block())

        @block.sync
        def _(sp):
            for dst, src in ((wq, "wq"), (wk, "wk"), (wv, "wv"), (wg, "wg")):
                sp.dma_start(dst[:], dram[src].rearrange("(k p) n -> p k n", p=P)).then_inc(S["weights_in"], 16)
            for dst, src in ((bq, "bq"), (bk, "bk")):
                sp.dma_start(dst[:], dram[src].rearrange("(k p) -> p k", p=P), allow_slow_non_contiguous=True).then_inc(S["weights_in"], 16)
            for dst, src in ((bv_all, "bv"), (gamma_all, "gamma"), (beta_all, "beta")):
                sp.dma_start(dst[:], dram[src].partition_broadcast(P)).then_inc(S["bcast_in"], 16)

            def step(at):
                t, b, r = at.t, at.batch, at.quarter
                if batch_ok(b + 1) and r == 0:
                    nb = at.value(lambda t: t // QT + 1)
                    if batch_ok(b):
                        at.wait_apart(sp, MET, (S["turn_full"], nth(TURN_NO, ("xn", b, 1), t, QT)))
                    sp.dma_start(xb[:], x_v[nb]).then_inc(S["x_in"], 16)
                    if batch_ok(b):
                        at.wait_apart(sp, MET, (S["turn_full"], nth(TURN_NO, ("ctx", b, 7), t, QT)),
                                      (S["ctx_hi_done"], lambda t: t + QT), (S["ctx_lo_done"], lambda t: t + QT))
                    sp.dma_start(ctx_in[:, 0:JF, :], ctx_v[nb, 0:JF * P, :].rearrange("(j p) d -> p j d", p=P)) \
                        .then_inc(S["ctx_in_a"], 16)
                    sp.dma_start(ctx_in[0:JR, JF, :], ctx_v[nb, JF * P:SK, :]).then_inc(S["ctx_in_a"], 16)
                if tile_ok(t):
                    if tile_ok(t - 4):
                        at.wait_apart(sp, MET, (S["x1_done"], lambda t: t - 3))
                    sp.dma_start(xres[t % 4][:], x_t[at.value(lambda t: t)]).then_inc(xres_in[t % 4], 16)
                if tile_ok(t + 1):
                    if tile_ok(t):
                        at.wait_apart(sp, MET, (S["mask_ready"], lambda t: t + 1))
                    sp.dma_start(mask_in[:], mask_v[at.value(lambda t: t + 1)]).then_inc(S["mask_in"], 16)
                if t == -1:
                    sp.wait_ge(S["blank_set"], 3)
                    sp.dma_start(slots.rearrange("(p n) w -> p n w", p=P),
                                 blank[:].unsqueeze(1).broadcast_to([P, TOKENS // P, ROW])) \
                        .then_inc(S["blanks_out"], 16)
                if tile_ok(t - 3):
                    at.wait_apart(sp, MET, (S["x1_done"], lambda t: t - 2))
                    sp.dma_start(out_t[at.value(lambda t: t - 3)],
                                 row[(t - 3) // QT % 2][:, (t - 3) % QT, 0:D]).then_inc(store_done[(t - 3) // QT % 2], 16)

            ATTENTION.run(sp, step)
            for n in range(2):
                sp.wait_ge(store_done[n], 16 * NT // 2)
                sp.wait_ge(scatter_done[n], 16 * NT // 2)

        @block.gpsimd
        def _(pool):
            g = nc.gpsimd
            g.memset(ident[:], 0.0).then_inc(S["consts"], 1)
            g.memset(tri[:], 0.0).then_inc(S["consts"], 1)
            g.memset(ones[:], 1.0).then_inc(S["consts"], 1)
            g.memset(halves[:], -0.5).then_inc(S["consts"], 1)
            for n in range(2):
                g.memset(mask_add[n][:, SK:SKP], MASKED).then_inc(S["consts"], 1)
                for part in (ctxT_hi[n], ctxT_lo[n]):
                    g.memset(part[:, :, SK:SKP].bitcast(F32), 0.0).then_inc(S["consts"], 1)
            g.iota(rank[:], pattern=[[0, QT], [-1, EXPERTS]], base=EXPERTS, channel_multiplier=0,
                   allow_small_or_imprecise_dtypes=True).then_inc(S["consts"], 1)
            g.iota(token[:], pattern=[[P, QT]], base=0, channel_multiplier=1,
                   allow_small_or_imprecise_dtypes=True).then_inc(S["consts"], 1)
            pool.wait_ge(S["consts"], 12)
            g.affine_select(out=ident[:], in_=ident[:], compare_op=ALU.not_equal, fill=1.0, base=0,
                            pattern=[[-1, P]], channel_multiplier=1).then_inc(S["consts"], 1)
            g.affine_select(out=tri[:], in_=tri[:], compare_op=ALU.is_ge, fill=1.0, base=0,
                            pattern=[[-1, P]], channel_multiplier=1).then_inc(S["consts"], 1)
            g.memset(blank[:, 0:D + 3], 0.0).then_inc(S["blank_set"], 1)
            g.memset(blank[:, D + 3:ROW], NOWHERE).then_inc(S["blank_set"], 1)
            g.memset(countb[:], 0.0).then_inc(S["blank_set"], 1)
            pool.wait_ge(S["bcast_in"], 48)

            def low_part(at, b, r):
                j0, j1 = 3 * r, 3 * r + 3
                par = b % 2
                at.wait(pool, S["ctx_hi_done"], lambda t: t + QT + 1)
                src, hi, lo = ctx_in[:, j0:j1, :], ctx_hi[par][:, j0:j1, :], ctx_lo[par][:, j0:j1, :]
                last = g.tensor_tensor(out=lo, in0=src, in1=hi.bitcast(F32), op=ALU.subtract)
                if r == QT - 1:
                    last = g.tensor_tensor(out=ctx_lo[par][0:JR, JF, :], in0=ctx_in[0:JR, JF, :],
                                           in1=ctx_hi[par][0:JR, JF, :].bitcast(F32), op=ALU.subtract)
                last.then_inc(S["ctx_lo_done"], 1)

            def step(at):
                t, b, r = at.t, at.batch, at.quarter
                if tile_ok(t - 1):
                    at.wait(pool, xres_in[(t - 1) % 4], lambda t: 16 * ((t - 1) // 4 + 1))
                    g.tensor_tensor(out=xres[(t - 1) % 4][:], in0=xres[(t - 1) % 4][:], in1=beta_all[:],
                                    op=ALU.add).then_inc(S["xres_beta"], 1)
                if tile_ok(t - 2):
                    at.wait(pool, S["var1"], lambda t: t - 1)
                    g.tensor_tensor(out=rstd1[:], in0=ve1[:], in1=halves[:, 0:1], op=ALU.pow).then_inc(S["rstd1"], 1)
                if batch_ok(b + 1) and r == 0:
                    at.wait(pool, S["varx"], lambda t: t // QT + 2)
                    g.tensor_tensor(out=rstdx[:], in0=vex[:], in1=halves[:], op=ALU.pow).then_inc(S["rstdx"], 1)
                if batch_ok(b + 1):
                    low_part(at, b + 1, r)
                if tile_ok(t - 2):
                    at.wait(pool, S["var2"], lambda t: t - 1)
                    k = (t - 2) // QT % 2
                    g.tensor_tensor(out=row[k][:, (t - 2) % QT, D + 1:D + 2], in0=ve2[:], in1=halves[:, 0:1],
                                    op=ALU.pow).then_inc(S["rstd2"], 1)
                if batch_ok(b - 2) and r == 0:
                    k = b % 2
                    at.wait_apart(pool, MET, *((S[s], lambda t: t // QT - 1) for s in ("slot_ready", "gate_done", "token_set")))
                    if b == 2:
                        pool.wait_ge(S["blanks_out"], 16)
                    for i in range(QT):
                        g.indirect_dma_start(
                            out=slots, out_offset=bass.IndirectOffsetOnAxis(ap=slot[k][:, i:i + 1], axis=0),
                            in_=row[k][:, i, :], in_offset=None, bounds_check=TOKENS - 1, oob_is_err=False) \
                            .then_inc(scatter_done[k], 16)

            ATTENTION.run(pool, step)

        @block.scalar
        def _(act):
            a = nc.scalar

            def evac(at, group, t0, per, out, in_, **kw):
                at.wait(act, S["turn_full"], nth(TURN_NO, group, t0, per))
                a.activation(out, in_, kw.pop("func", ACT.Copy), **kw).then_inc(S["turn_evac"], 1)

            def ctx_high(at, i):
                par = (at.batch + 1) % 2
                g = ("ctx", at.batch + 1, i)
                c, k = i // 2, i % 2
                w = min(CH, SK - c * CH)
                evac(at, g, at.t, QT, ctxT_hi[par][:, k, c * CH:c * CH + w], turn[TURN_NO[g] % 2][:, 0:w])

            for n, dst in enumerate((wq_t, wk_t, mqk)):
                act.wait_ge(S["turn_full"], n + 1)
                a.activation(dst[:].rearrange("p k n -> p (k n)"), turn[n % 2][:], ACT.Copy).then_inc(S["turn_evac"], 1)

            def step(at):
                t, b, r = at.t, at.batch, at.quarter
                if tile_ok(t - 1):
                    for c in range(NC):
                        g = ("probs", t - 1, c)
                        bank = turn[TURN_NO[g] % 2]
                        if c < NC - 1:
                            dst, src = probsT_hi[:, 4 * c:4 * c + 4, :].rearrange("p j q -> p (j q)"), bank[:]
                        else:
                            dst, src = probsT_hi[0:JR, JF, :], bank[0:JR, 0:P]
                        evac(at, g, t, 1, dst, src)
                if tile_ok(t - 3):
                    g = ("xn2", t - 3, 0)
                    evac(at, g, t, 1, xn2T[:].rearrange("p k q -> p (k q)"), turn[TURN_NO[g] % 2][:, 0:KT * P])
                if tile_ok(t - 2):
                    g = ("attn", t - 2, 0)
                    evac(at, g, t, 1, attnT[:].rearrange("p k q -> p (k q)"), turn[TURN_NO[g] % 2][:, 0:KT * P])
                if tile_ok(t):
                    at.wait(act, S["max_neg"], lambda t: t + 1)
                    a.activation(probs[:], probs[:], ACT.Exp, bias=negmax[:, t % 2:t % 2 + 1], scale=SCALE,
                                 accum_out=rowsum[:, t % 2:t % 2 + 1]).then_inc(S["exp_done"], 1)
                if tile_ok(t - 3):
                    at.wait(act, S["small_full"], nth(SMALL_NO, ("logits", t - 3), t))
                    if (t - 3) % QT == 0 and t - 3 > 0:
                        at.wait(act, S["below_set"], lambda t: (t - 3) // QT)
                    a.activation(logits[:, (t - 3) % QT, :], small[:, 0:EXPERTS], ACT.Copy) \
                        .then_inc(S["logits_read"], 1)
                if batch_ok(b + 1):
                    par = (b + 1) % 2
                    ctx_high(at, 2 * r)
                    if r == 0:
                        at.wait(act, S["ctx_in_a"], lambda t: 32 * (t // QT + 2))
                    j0, j1 = 3 * r, 3 * r + 3
                    last = a.activation(ctx_hi[par][:, j0:j1, :], ctx_in[:, j0:j1, :], ACT.Copy)
                    if r == QT - 1:
                        last = a.activation(ctx_hi[par][0:JR, JF, :], ctx_in[0:JR, JF, :], ACT.Copy)
                    last.then_inc(S["ctx_hi_done"], 1)
                    ctx_high(at, 2 * r + 1)
                if tile_ok(t - 1):
                    at.wait(act, S["sum_inv"], lambda t: t)
                    at.wait(act, S["out_full"], lambda t: t)
                    a.activation(attn[:], outp[:, 0:D], ACT.Copy, scale=rsum[:, (t - 1) % 2:(t - 1) % 2 + 1]) \
                        .then_inc(S["attn_ready"], 1)
                if batch_ok(b + 1):
                    if r == 1:
                        for k in range(KT):
                            g = ("xn", b + 1, k)
                            evac(at, g, t, QT, xnT[:, k, :], turn[TURN_NO[g] % 2][:])
                    if r == 2:
                        for m in range(KT):
                            g = ("qk", b + 1, m)
                            evac(at, g, t, QT, qkT_hi[par][:, m, :], turn[TURN_NO[g] % 2][:],
                                 func=ACT.Identity, bias=qbias[:, m:m + 1])
                if batch_ok(b - 1) and r == 2:
                    at.wait(act, S["below_set"], lambda t: t // QT)
                    a.activation(gates[:].rearrange("p i e -> p (i e)"), below[:].rearrange("p i e -> p (i e)"),
                                 ACT.Exp).then_inc(S["gates_done"], 1)

            ATTENTION.run(act, step)

        @block.vector
        def _(dve):
            v = nc.vector
            TT, TS, STT = v.tensor_tensor, v.tensor_scalar, v.scalar_tensor_tensor

            dve.wait_ge(S["consts"], 14)
            dve.wait_ge(S["blank_set"], 3)
            v.memset(count[:], 0.0).then_inc(S["count_set"], 1)
            dve.wait_ge(S["weights_in"], 96)
            for k in range(KT):
                last = v.tensor_copy(bqw[:, k, :], bq[:, k:k + 1].broadcast_to([P, P]))
            last.then_inc(S["setup_done"], 1)
            dve.wait_ge(S["small_full"], 1)
            v.tensor_copy(qbias[:], small[:, 0:KT])
            v.tensor_copy(kbias[:], small[:, KT:2 * KT])
            v.tensor_copy(bqk[:], small[:, 2 * KT:2 * KT + 1]).then_inc(S["small_read"], 1)
            dve.wait_ge(S["small_read"], 1)
            dve.wait_ge(S["bcast_in"], 48)

            def low(at, group, t0, per, out, psum, hi, bias=None):
                at.wait(dve, S["turn_evac"], nth(TURN_NO, group, t0, per))
                if bias is None:
                    ins = TT(out=out, in0=psum, in1=hi.bitcast(F32), op=ALU.subtract)
                else:
                    ins = STT(out=out, in0=psum, scalar=bias, in1=hi.bitcast(F32), op0=ALU.add, op1=ALU.subtract)
                ins.then_inc(S["turn_low"], 1)

            def mask_prep(at):
                at.wait(dve, S["mask_in"], lambda t: 16 * (t + 2))
                TS(mask_add[(at.t + 1) % 2][:, 0:SK], mask_in[:], 0.0, MASKED, ALU.is_equal, ALU.mult) \
                    .then_inc(S["mask_ready"], 1)

            def ctx_low(at, i):
                par = (at.batch + 1) % 2
                g = ("ctx", at.batch + 1, i)
                c, k = i // 2, i % 2
                w = min(CH, SK - c * CH)
                low(at, g, at.t, QT, ctxT_lo[par][:, k, c * CH:c * CH + w], turn[TURN_NO[g] % 2][:, 0:w],
                    ctxT_hi[par][:, k, c * CH:c * CH + w])

            def norm_tail(at):
                t = at.t
                k, i = (t - 2) // QT % 2, (t - 2) % QT
                at.wait(dve, S["rstd1"], lambda t: t - 1)
                at.wait(dve, S["xres_beta"], lambda t: t - 1)
                at.wait(dve, S["scaled_set"], lambda t: t - 1)
                if i == 0 and (t - 2) // QT >= 2:
                    at.wait(dve, store_done[k], lambda t: 16 * QT * ((t - 2) // QT // 2))
                    at.wait(dve, scatter_done[k], lambda t: 16 * QT * ((t - 2) // QT // 2))
                x1 = row[k][:, i, 0:D]
                STT(out=x1, in0=scaled[:], scalar=rstd1[:], in1=xres[(t - 2) % 4][:],
                    op0=ALU.mult, op1=ALU.add).then_inc(S["x1_done"], 1)
                at.wait(dve, S["x1_done"], lambda t: t - 1)
                v.bn_stats(bn2[:], x1).then_inc(S["bn2_set"], 1)
                at.wait_apart(dve, MET, (S["bn2_set"], lambda t: t - 1))
                v.bn_aggr(mv2[:], bn2[:]).then_inc(S["mv2_set"], 1)
                at.wait(dve, S["mv2_set"], lambda t: t - 1)
                v.tensor_copy(row[k][:, i, D:D + 1], mv2[:, 0:1])
                v.tensor_scalar_add(ve2[:], mv2[:, 1:2], EPS).then_inc(S["var2"], 1)

            def step(at):
                t, b, r = at.t, at.batch, at.quarter
                if tile_ok(t - 1):
                    at.wait(dve, S["exp_done"], lambda t: t)
                    v.reciprocal(rsum[:, (t - 1) % 2:(t - 1) % 2 + 1], rowsum[:, (t - 1) % 2:(t - 1) % 2 + 1]) \
                        .then_inc(S["sum_inv"], 1)
                    for c in range(NC):
                        g = ("probs", t - 1, c)
                        bank = turn[TURN_NO[g] % 2]
                        if c < NC - 1:
                            sl = lambda a: a[:, 4 * c:4 * c + 4, :].rearrange("p j q -> p (j q)")
                            low(at, g, t, 1, sl(probsT_lo), bank[:], sl(probsT_hi))
                        else:
                            low(at, g, t, 1, probsT_lo[0:JR, JF, :], bank[0:JR, 0:P], probsT_hi[0:JR, JF, :])
                if tile_ok(t):
                    o = t % 2
                    at.wait_apart(dve, MET, (S["scores_full"], lambda t: t + 1), (S["mask_ready"], lambda t: t + 1))
                    v.tensor_tensor_reduce(out=probs[:].rearrange("p (c w) -> p c w", c=NC), in0=scores[:, :, 0:CW],
                                           in1=mask_add[o][:].rearrange("p (c w) -> p c w", c=NC), scale=1.0,
                                           scalar=-3e38, op0=ALU.add, op1=ALU.max,
                                           accum_out=rowmax[:, o:o + 1]).then_inc(S["max_raw"], 1)
                    kb = kb16[b % 2][:, r:r + 1]
                    at.wait(dve, S["max_raw"], lambda t: t + 1)
                    STT(out=fullmax[:, o:o + 1], in0=rowmax[:, o:o + 1], scalar=SCALE, in1=kb,
                        op0=ALU.mult, op1=ALU.add).then_inc(S["max_full"], 1)
                    at.wait(dve, S["max_full"], lambda t: t + 1)
                    TT(out=negmax[:, o:o + 1], in0=kb, in1=fullmax[:, o:o + 1], op=ALU.subtract) \
                        .then_inc(S["max_neg"], 1)
                if tile_ok(t + 1):
                    mask_prep(at)
                if batch_ok(b + 1):
                    ctx_low(at, 2 * r)
                if tile_ok(t - 2):
                    at.wait(dve, S["small_full"], nth(SMALL_NO, ("value", t - 2), t))
                    TT(out=value[:], in0=small[:, D:2 * D], in1=bv_all[:], op=ALU.add).then_inc(S["small_read"], 1)
                    at.wait(dve, S["small_read"], nth(SMALL_READ, ("value", t - 2), t))
                    v.bn_stats(bn1[:], value[:]).then_inc(S["bn1_set"], 1)
                    at.wait_apart(dve, MET, (S["bn1_set"], lambda t: t - 1))
                    v.bn_aggr(mv1[:], bn1[:]).then_inc(S["mv1_set"], 1)
                    at.wait(dve, S["mv1_set"], lambda t: t - 1)
                    v.tensor_scalar_add(ve1[:], mv1[:, 1:2], EPS).then_inc(S["var1"], 1)
                    STT(out=scaled[:], in0=value[:], scalar=mv1[:, 0:1], in1=gamma_all[:],
                        op0=ALU.subtract, op1=ALU.mult).then_inc(S["scaled_set"], 1)
                if batch_ok(b + 1):
                    ctx_low(at, 2 * r + 1)
                    par = (b + 1) % 2
                    if r == 0:
                        at.wait(dve, S["x_in"], lambda t: 16 * (t // QT + 2))
                        for i in range(QT):
                            last = v.bn_stats(bnx[:, i, :], xb[:, i, :])
                        last.then_inc(S["bnx_set"], 1)
                        at.wait_apart(dve, MET, (S["bnx_set"], lambda t: t // QT + 2))
                        for i in range(QT):
                            last = v.bn_aggr(mvx[:, i, :], bnx[:, i, :])
                        last.then_inc(S["mvx_set"], 1)
                        at.wait(dve, S["mvx_set"], lambda t: t // QT + 2)
                        v.tensor_scalar_add(vex[:], mvx[:, :, 1], EPS).then_inc(S["varx"], 1)
                    if r == 1:
                        at.wait(dve, S["rstdx"], lambda t: t // QT + 2)
                        for i in range(QT):
                            last = TS(xb[:, i, :], xb[:, i, :], mvx[:, i, 0:1], rstdx[:, i:i + 1],
                                      ALU.subtract, ALU.mult)
                        last.then_inc(S["xnorm_done"], 1)
                if tile_ok(t - 2):
                    norm_tail(at)
                if batch_ok(b + 1):
                    if r == 2:
                        for m in range(KT):
                            g = ("qk", b + 1, m)
                            low(at, g, t, QT, qkT_lo[par][:, m, :], turn[TURN_NO[g] % 2][:], qkT_hi[par][:, m, :],
                                bias=qbias[:, m:m + 1])
                        at.wait(dve, S["small_full"], nth(SMALL_NO, ("keybias", b + 1), t, QT))
                        TS(kb16[par][:], small[:, 16:16 + QT], bqk[:], SCALE, ALU.add, ALU.mult) \
                            .then_inc(S["small_read"], 1)
                if tile_ok(t - 2):
                    k, i = (t - 2) // QT % 2, (t - 2) % QT
                    at.wait(dve, S["rstd2"], lambda t: t - 1)
                    TS(xn2[:], row[k][:, i, 0:D], mv2[:, 0:1], row[k][:, i, D + 1:D + 2], ALU.subtract, ALU.mult) \
                        .then_inc(S["xn2_done"], 1)
                if batch_ok(b - 1) and r == 2:
                    router(at)
                if batch_ok(b - 1) and r == 3:
                    places(at)

            nbatch = lambda t: t // QT

            def router(at):
                k = (at.batch - 1) % 2
                wide = lambda a: a.unsqueeze(2).broadcast_to([P, QT, EXPERTS])
                at.wait(dve, S["logits_read"], lambda t: t - 2)
                v.tensor_reduce(best[:], logits[:], AX.X, ALU.max).then_inc(S["best_set"], 1)
                at.wait(dve, S["best_set"], nbatch)
                TT(out=below[:], in0=logits[:], in1=wide(best[:]), op=ALU.subtract).then_inc(S["below_set"], 1)
                at.wait(dve, S["below_set"], nbatch)
                STT(out=tied[:], in0=below[:], scalar=0.0, in1=rank[:], op0=ALU.is_equal, op1=ALU.mult) \
                    .then_inc(S["tied_set"], 1)
                at.wait(dve, S["tied_set"], nbatch)
                v.tensor_reduce(pick[:], tied[:], AX.X, ALU.max).then_inc(S["pick_set"], 1)
                at.wait(dve, S["pick_set"], nbatch)
                TT(out=onehot[:], in0=tied[:], in1=wide(pick[:]), op=ALU.is_equal).then_inc(S["onehot_done"], 1)
                at.wait(dve, S["token_next"], lambda t: t // QT - 1)
                v.tensor_copy(row[k][:, :, D + 3], token[:]).then_inc(S["token_set"], 1)
                at.wait(dve, S["token_set"], nbatch)
                v.tensor_scalar_add(token[:], token[:], float(SQ)).then_inc(S["token_next"], 1)

            def places(at):
                k = (at.batch - 1) % 2
                at.wait(dve, S["small_full"], nth(SMALL_NO, ("places", at.batch - 1), at.t, QT))
                TT(out=placed[:], in0=small[:, 32:32 + QT * EXPERTS].rearrange("p (i e) -> p i e", e=EXPERTS),
                   in1=onehot[:], op=ALU.mult).then_inc(S["small_read"], 1)
                v.tensor_reduce(added[:], onehot[:].rearrange("p i e -> p e i"), AX.X, ALU.add) \
                    .then_inc(S["added_set"], 1)
                at.wait(dve, S["small_read"], nth(SMALL_READ, ("places", at.batch - 1), at.t, QT))
                v.tensor_reduce(place[:], placed[:], AX.X, ALU.add).then_inc(S["place_set"], 1)
                at.wait(dve, S["added_set"], nbatch)
                TT(out=count[:], in0=count[:], in1=added[:], op=ALU.add).then_inc(S["count_set"], 1)
                at.wait(dve, S["place_set"], nbatch)
                TS(base[:], pick[:], -float(CAP), float(EXPERTS * CAP), ALU.mult, ALU.add).then_inc(S["base_set"], 1)
                TS(over[:], place[:], float(CAP), NOWHERE, ALU.is_ge, ALU.mult).then_inc(S["over_set"], 1)
                at.wait(dve, S["count_set"], lambda t: t // QT + 1)
                v.tensor_copy(countb[:], count[:]).then_inc(S["countb_set"], 1)
                at.wait(dve, S["base_set"], nbatch)
                TT(out=slotf[:], in0=base[:], in1=place[:], op=ALU.add).then_inc(S["part_set"], 1)
                at.wait(dve, S["over_set"], nbatch)
                at.wait(dve, S["part_set"], nbatch)
                TT(out=slot[k][:], in0=slotf[:], in1=over[:], op=ALU.add).then_inc(S["slot_ready"], 1)
                at.wait(dve, S["gates_done"], nbatch)
                v.tensor_reduce(gsum[:], gates[:], AX.X, ALU.add).then_inc(S["gsum_set"], 1)
                at.wait(dve, S["gsum_set"], nbatch)
                v.reciprocal(row[k][:, :, D + 2], gsum[:]).then_inc(S["gate_done"], 1)

            ATTENTION.run(dve, step)

        @block.tensor
        def _(pe):
            mm = nc.tensor.matmul

            def turn_bank(at, group, t0, per):
                n = TURN_NO[group]
                before = TURNS[n - 2]

                def shifted(table):
                    def f(t):
                        kind, of, *rest = group
                        return table(TURNS[TURN_NO[(kind, of + (t - t0) // per, *rest)] - 2])
                    return f
                if before[0] in SPLIT_KINDS:
                    at.wait(pe, S["turn_low"], shifted(lambda g: SPLITS[g] + 1))
                else:
                    at.wait(pe, S["turn_evac"], shifted(lambda g: TURN_NO[g] + 1))
                return turn[n % 2]

            def small_free(at, group, t0, per=1):
                before = SMALLS[SMALL_NO[group] - 1]

                def prior(t):
                    g = SMALLS[nth(SMALL_NO, group, t0, per)(t) - 2]
                    assert g[0] == before[0]
                    return g[1] + 1 if g[0] in READ_BY_ACT else SMALL_READ[g] + 1
                at.wait(pe, S["logits_read" if before[0] in READ_BY_ACT else "small_read"], prior)

            def three(out, w_hi, w_lo, m_hi, m_lo, first, last):
                mm(out, w_hi, m_hi, start=first, stop=False)
                mm(out, w_hi, m_lo, start=False, stop=False)
                return mm(out, w_lo, m_hi, start=False, stop=last)

            pe.wait_ge(S["consts"], 14)
            pe.wait_ge(S["weights_in"], 96)
            for n, w in enumerate((wq, wk)):
                for k in range(KT):
                    for m in range(KT):
                        last = nc.tensor.transpose(turn[n][:, k * D + m * P:k * D + m * P + P],
                                                   w[:, m, k * P:k * P + P], ident[:])
                last.then_inc(S["turn_full"], 1)
            pe.wait_ge(S["turn_evac"], 2)
            for m in range(KT):
                for k in range(KT):
                    last = mm(turn[0][:, m * D:m * D + D], wq_t[:, k, m * P:m * P + P], wk_t[:, k, :],
                              start=(k == 0), stop=(k == KT - 1))
            last.then_inc(S["turn_full"], 1)
            pe.wait_ge(S["setup_done"], 1)
            for w, vec, at0 in ((wk_t, bq, 0), (wq_t, bk, KT)):
                for m in range(KT):
                    for k in range(KT):
                        mm(small[:, at0 + m:at0 + m + 1], w[:, k, m * P:m * P + P], vec[:, k:k + 1],
                           start=(k == 0), stop=(k == KT - 1))
            for k in range(KT):
                last = mm(small[:, 2 * KT:2 * KT + 1], bqw[:, k, :], bk[:, k:k + 1],
                          start=(k == 0), stop=(k == KT - 1))
            last.then_inc(S["small_full"], 1)

            def score_chunk(at, c):
                t, b, r = at.t, at.batch, at.quarter
                par = b % 2
                if c == 0:
                    if tile_ok(t - 1):
                        at.wait(pe, S["max_raw"], lambda t: t)
                    if r == 0:
                        at.wait(pe, S["turn_low"], nth(SPLITS, ("qk", b, 1), t, QT))
                if r == 0 and c == NC - 1:
                    at.wait(pe, S["turn_low"], nth(SPLITS, ("ctx", b, 2 * c + 1), t, QT))
                sl = slice(c * CW, c * CW + CW)
                q = slice(r * P, r * P + P)
                for k in range(KT):
                    last = three(scores[:, c, 0:CW], qkT_hi[par][:, k, q], qkT_lo[par][:, k, q],
                                 ctxT_hi[par][:, k, sl], ctxT_lo[par][:, k, sl], k == 0, k == KT - 1)
                if c == NC - 1:
                    last.then_inc(S["scores_full"], 1)

            def probs_turn(at, c):
                t = at.t
                if c == 0:
                    at.wait(pe, S["exp_done"], lambda t: t)
                bank = turn_bank(at, ("probs", t - 1, c), t, 1)
                for j in range(4 * c, min(4 * c + 4, JT)):
                    n = P if j < JF else JR
                    o = (j - 4 * c) * P
                    last = nc.tensor.transpose(bank[0:n, o:o + P], probs[:, j * P:j * P + n], ident[:])
                last.then_inc(S["turn_full"], 1)

            def attend(at, j0, j1):
                t = at.t
                par = (t - 1) // QT % 2
                if j0 == 0:
                    if tile_ok(t - 2):
                        at.wait(pe, S["attn_ready"], lambda t: t - 1)
                    if (t - 1) % QT == 0:
                        at.wait(pe, S["ctx_lo_done"], lambda t: (t - 1) + QT)
                for j in range(j0, j1):
                    n = P if j < JF else JR
                    if j % 4 == 0:
                        at.wait(pe, S["turn_low"], nth(SPLITS, ("probs", t - 1, j // 4), t))
                    last = three(outp[:, 0:D], probsT_hi[0:n, j, :], probsT_lo[0:n, j, :],
                                 ctx_hi[par][0:n, j, :], ctx_lo[par][0:n, j, :], j == 0, j == JT - 1)
                if j1 == JT:
                    last.then_inc(S["out_full"], 1)

            def ctx_turn(at, i):
                bank = turn_bank(at, ("ctx", at.batch + 1, i), at.t, QT)
                c, k = i // 2, i % 2
                for j in range(4 * c, min(4 * c + 4, JT)):
                    n = P if j < JF else JR
                    o = (j - 4 * c) * P
                    last = nc.tensor.transpose(bank[:, o:o + n], ctx_in[0:n, j, k * P:k * P + P], ident[0:n, 0:n])
                last.then_inc(S["turn_full"], 1)

            def step(at):
                t, b, r = at.t, at.batch, at.quarter
                for c in range(NC):
                    if tile_ok(t):
                        score_chunk(at, c)
                    if tile_ok(t - 1):
                        probs_turn(at, c)
                if tile_ok(t - 1):
                    attend(at, 0, 4)
                if tile_ok(t - 3):
                    at.wait(pe, S["xn2_done"], lambda t: t - 2)
                    bank = turn_bank(at, ("xn2", t - 3, 0), t, 1)
                    for k in range(KT):
                        last = nc.tensor.transpose(bank[:, k * P:k * P + P], xn2[:, k * P:k * P + P], ident[:])
                    last.then_inc(S["turn_full"], 1)
                if tile_ok(t - 2):
                    at.wait(pe, S["attn_ready"], lambda t: t - 1)
                    bank = turn_bank(at, ("attn", t - 2, 0), t, 1)
                    for k in range(KT):
                        last = nc.tensor.transpose(bank[:, k * P:k * P + P], attn[:, k * P:k * P + P], ident[:])
                    last.then_inc(S["turn_full"], 1)
                if tile_ok(t - 1):
                    attend(at, 4, 6)
                if tile_ok(t - 3):
                    at.wait(pe, S["turn_evac"], nth(TURN_NO, ("xn2", t - 3, 0), t))
                    small_free(at, ("logits", t - 3), t)
                    for k in range(KT):
                        last = mm(small[:, 0:EXPERTS], xn2T[:, k, :], wg[:, k, :], start=(k == 0), stop=(k == KT - 1))
                    last.then_inc(S["small_full"], 1)
                if batch_ok(b + 1):
                    if r == 0:
                        at.wait(pe, S["ctx_in_a"], lambda t: 32 * (t // QT + 2))
                    ctx_turn(at, 2 * r)
                if tile_ok(t - 1):
                    attend(at, 6, 8)
                if tile_ok(t - 2):
                    at.wait(pe, S["turn_evac"], nth(TURN_NO, ("attn", t - 2, 0), t))
                    small_free(at, ("value", t - 2), t)
                    for k in range(KT):
                        last = mm(small[:, D:2 * D], attnT[:, k, :], wv[:, k, :], start=(k == 0), stop=(k == KT - 1))
                    last.then_inc(S["small_full"], 1)
                if tile_ok(t - 1):
                    attend(at, 8, 10)
                if batch_ok(b + 1):
                    ctx_turn(at, 2 * r + 1)
                if tile_ok(t - 1):
                    attend(at, 10, JT)
                if batch_ok(b + 1):
                    if r == 1:
                        at.wait(pe, S["xnorm_done"], lambda t: t // QT + 2)
                        for k in range(KT):
                            bank = turn_bank(at, ("xn", b + 1, k), t, QT)
                            for i in range(QT):
                                last = nc.tensor.transpose(bank[:, i * P:i * P + P], xb[:, i, k * P:k * P + P],
                                                           ident[:])
                            last.then_inc(S["turn_full"], 1)
                    if r == 2:
                        at.wait(pe, S["turn_evac"], nth(TURN_NO, ("xn", b + 1, 1), t, QT))
                        for m in range(KT):
                            bank = turn_bank(at, ("qk", b + 1, m), t, QT)
                            for k in range(KT):
                                last = mm(bank[:], mqk[:, k, m * P:m * P + P], xnT[:, k, :],
                                          start=(k == 0), stop=(k == KT - 1))
                            last.then_inc(S["turn_full"], 1)
                        small_free(at, ("keybias", b + 1), t, QT)
                        for i in range(QT):
                            for k in range(KT):
                                last = mm(small[:, 16 + i:17 + i], xnT[:, k, i * P:i * P + P], kbias[:, k:k + 1],
                                          start=(k == 0), stop=(k == KT - 1))
                        last.then_inc(S["small_full"], 1)
                if batch_ok(b - 1) and r == 3:
                    at.wait(pe, S["onehot_done"], lambda t: t // QT)
                    if b - 1 > 0:
                        at.wait(pe, S["countb_set"], lambda t: t // QT - 1)
                    small_free(at, ("places", b - 1), t, QT)
                    flat = lambda a: a.rearrange("p i e -> p (i e)")
                    region = small[:, 32:32 + QT * EXPERTS]
                    mm(region, tri[:], flat(onehot[:]), start=True, stop=False)
                    for back in range(1, QT):
                        mm(region[:, back * EXPERTS:], ones[:], flat(onehot[:, 0:QT - back, :]),
                           start=False, stop=False)
                    mm(region, ones[:], countb[:].unsqueeze(1).broadcast_to([P, QT, EXPERTS]), start=False, stop=True) \
                        .then_inc(S["small_full"], 1)

            ATTENTION.run(pe, step)


LAG = 2
HB = HID // P
SG = 512
GROUPS = CAP // SG
ST = SG // P
UNITS = EXPERTS * GROUPS * HB
PER = GROUPS * HB
EXPERT_PIPE = Pipeline("experts", -HB, PER, PER, EXPERTS - 2, UNITS + LAG)


def experts(nc, dram, keep):
    with ExitStack() as ctx:
        def sb(name, shape, dt=F32):
            return ctx.enter_context(nc.sbuf_tensor(name, shape, dt))

        def sem(name):
            return ctx.enter_context(nc.semaphore(name))

        ident = keep["ident"]
        w1_in = sb("w1_in", [P, KT, HID])
        w2_in = sb("w2_in", [P, HB, D])
        w1_hi = sb("w1_hi", [P, KT, HID], F32R)
        w1_lo = sb("w1_lo", [P, KT, HID], F32R)
        w2_hi = sb("w2_hi", [P, HB, D], F32R)
        w2_lo = sb("w2_lo", [P, HB, D], F32R)
        b1_in = sb("b1_in", [EXPERTS * HB, P])
        b1_t = sb("b1_t", [P, EXPERTS * HB])
        b2_all = sb("b2_all", [P, EXPERTS, D])
        rows = [sb(f"rows{n}", [P, ST, ROW]) for n in range(2)]
        token_of = [sb(f"token_of{n}", [P, ST], U32) for n in range(2)]
        xn = sb("xn", [P, ST, D])
        xT_hi = [sb(f"xT_hi{n}", [P, KT, SG], F32R) for n in range(2)]
        xT_lo = [sb(f"xT_lo{n}", [P, KT, SG], F32R) for n in range(2)]
        hid = [sb(f"hid{n}", [P, SG]) for n in range(4)]
        hid_hi = [sb(f"hid_hi{n}", [P, SG], F32R) for n in range(4)]
        hid_lo = [sb(f"hid_lo{n}", [P, SG], F32R) for n in range(4)]
        biased = [sb(f"biased{n}", [P, D]) for n in range(ST)]
        result = [sb(f"result{n}", [P, ST, D]) for n in range(2)]

        hps = [ctx.enter_context(nc.psum_tensor(f"hps{n}", [P, SG], F32)) for n in range(2)]
        xps = [ctx.enter_context(nc.psum_tensor(f"xps{n}", [P, SG], F32)) for n in range(KT)]
        acc = [ctx.enter_context(nc.psum_tensor(f"acc{n}", [P, SG], F32)) for n in range(ST)]

        S = {}
        for name in ("w1_arrived w2_arrived bias_in b1_full b1_set rows_in0 rows_in1 xn_set token_of_set "
                     "w1_hi_set w1_lo_set w2_hi_set w2_lo_set x_turned x_hi x_lo hid_full hid_set hid_hi_set hid_lo_set "
                     "hid_used acc_full0 acc_full1 acc_full2 acc_full3 biased_set result_set out0 out1").split():
            S[name] = sem("e_" + name)
        MET = (S["bias_in"], 32)
        rows_in = [S["rows_in0"], S["rows_in1"]]
        acc_full = [S[f"acc_full{n}"] for n in range(ST)]
        out_done = [S["out0"], S["out1"]]
        slots_v = dram["slots"].rearrange("(g p n) w -> g p n w", g=EXPERTS * GROUPS, p=P)
        w1_v = dram["w1"].rearrange("e (k p) h -> e p k h", p=P)
        w2_v = dram["w2"].rearrange("e (h p) n -> e p h n", p=P)
        out_rows = dram["out"].rearrange("b q d -> (b q) d")

        unit_ok = lambda n: 0 <= n < UNITS
        group_ok = lambda g: 0 <= g < EXPERTS * GROUPS
        refresh_ok = lambda n: n >= -HB and n // HB % 2 == 1 and 0 <= n // PER + 1 < EXPERTS
        refreshed = lambda n: (n // PER + 1) * HB + n % HB + 1

        block = ctx.enter_context(nc.Block())

        @block.sync
        def _(sp):
            sp.dma_start(b1_in[:], dram["b1"].rearrange("e (h p) -> (e h) p", p=P)).then_inc(S["bias_in"], 16)
            sp.dma_start(b2_all[:], dram["b2"].partition_broadcast(P)).then_inc(S["bias_in"], 16)

            def weights(at, e_of, e):
                at_e = at.value(e_of)
                if e > 0:
                    at.wait_apart(sp, MET, (S["w1_lo_set"], lambda n: HB * e_of(n)))
                sp.dma_start(w1_in[:], w1_v[at_e]).then_inc(S["w1_arrived"], 16)
                if e > 0:
                    at.wait_apart(sp, MET, (S["w2_lo_set"], lambda n: HB * e_of(n)))
                sp.dma_start(w2_in[:], w2_v[at_e]).then_inc(S["w2_arrived"], 16)

            def step(at):
                n = at.t
                g, hb = n // HB, n % HB
                if n == -HB:
                    weights(at, lambda n: 0, 0)
                if unit_ok(n) and n % PER == 3 and n // PER + 1 < EXPERTS:
                    weights(at, lambda n: n // PER + 1, n // PER + 1)
                if hb == 2 and group_ok(g + 1):
                    if g - 1 >= 0:
                        at.wait_apart(sp, MET, (S["result_set"], lambda n: ST * (n // HB)))
                    sp.dma_start(rows[(g + 1) % 2][:], slots_v[at.value(lambda n: n // HB + 1)]) \
                        .then_inc(rows_in[(g + 1) % 2], 16)

            EXPERT_PIPE.run(sp, step)
            for n in range(2):
                sp.wait_ge(out_done[n], 16 * ST * EXPERTS * GROUPS // 2)

        @block.gpsimd
        def _(pool):
            g_ = nc.gpsimd

            def step(at):
                n = at.t
                if refresh_ok(n):
                    hb = n % HB
                    blk = slice(hb * P, hb * P + P)
                    at.wait(pool, S["w1_hi_set"], refreshed)
                    g_.tensor_tensor(out=w1_lo[:, :, blk], in0=w1_in[:, :, blk], in1=w1_hi[:, :, blk].bitcast(F32),
                                     op=ALU.subtract).then_inc(S["w1_lo_set"], 1)
                if refresh_ok(n - LAG):
                    hb = (n - LAG) % HB
                    at.wait(pool, S["w2_hi_set"], lambda n: refreshed(n - LAG))
                    g_.tensor_tensor(out=w2_lo[:, hb, :], in0=w2_in[:, hb, :], in1=w2_hi[:, hb, :].bitcast(F32),
                                     op=ALU.subtract).then_inc(S["w2_lo_set"], 1)
                last = n - LAG
                if unit_ok(last) and last % HB == HB - 1:
                    grp = last // HB
                    for s in range(ST):
                        at.wait_apart(pool, MET, (S["result_set"], lambda n: ST * ((n - LAG) // HB) + s + 1))
                        g_.indirect_dma_start(
                            out=out_rows, out_offset=bass.IndirectOffsetOnAxis(ap=token_of[grp % 2][:, s:s + 1], axis=0),
                            in_=result[grp % 2][:, s, :], in_offset=None, bounds_check=TOKENS - 1, oob_is_err=False) \
                            .then_inc(out_done[grp % 2], 16)

            EXPERT_PIPE.run(pool, step)

        @block.scalar
        def _(act):
            a = nc.scalar

            def step(at):
                n = at.t
                grp, hb = n // HB, n % HB
                if group_ok(grp + 1) and hb >= HB - KT:
                    k = hb - (HB - KT)
                    at.wait(act, S["x_turned"], lambda n: KT * (n // HB + 1) + k + 1)
                    a.activation(xT_hi[(grp + 1) % 2][:, k, :], xps[k][:], ACT.Copy).then_inc(S["x_hi"], 1)
                if unit_ok(n):
                    at.wait(act, S["hid_set"], lambda n: n + 1)
                    a.activation(hid_hi[n % 4][:], hid[n % 4][:], ACT.Copy).then_inc(S["hid_hi_set"], 1)
                if refresh_ok(n):
                    blk = slice(hb * P, hb * P + P)
                    at.wait(act, S["w1_arrived"], lambda n: 16 * (n // PER + 2))
                    if n >= 0:
                        at.wait(act, S["hid_full"], lambda n: n + 1)
                    a.activation(w1_hi[:, :, blk], w1_in[:, :, blk], ACT.Copy).then_inc(S["w1_hi_set"], 1)
                if refresh_ok(n - LAG):
                    b2 = (n - LAG) % HB
                    at.wait(act, S["w2_arrived"], lambda n: 16 * ((n - LAG) // PER + 2))
                    if n - LAG >= 0:
                        at.wait(act, S["hid_used"], lambda n: n - LAG + 1)
                    a.activation(w2_hi[:, b2, :], w2_in[:, b2, :], ACT.Copy).then_inc(S["w2_hi_set"], 1)

            EXPERT_PIPE.run(act, step)

        @block.vector
        def _(dve):
            v = nc.vector
            TT, TS, STT = v.tensor_tensor, v.tensor_scalar, v.scalar_tensor_tensor
            dve.wait_ge(S["b1_full"], 1)
            v.tensor_copy(b1_t[:], xps[0][:, 0:EXPERTS * HB]).then_inc(S["b1_set"], 1)
            dve.wait_ge(S["bias_in"], 32)
            dve.wait_ge(S["b1_set"], 1)

            def step(at):
                n = at.t
                grp, hb = n // HB, n % HB
                if unit_ok(n):
                    at.wait(dve, S["hid_full"], lambda n: n + 1)
                    col = at.value(lambda n: n // PER * HB + n % HB)
                    if n >= 4:
                        at.wait(dve, S["hid_used"], lambda n: n - 3)
                    TS(hid[n % 4][:], hps[n % 2][:], b1_t[:, bass.ds(col, 1)], 0.0, ALU.add, ALU.max) \
                        .then_inc(S["hid_set"], 1)
                if group_ok(grp + 1) and hb == HB - KT - 1:
                    k = (grp + 1) % 2
                    at.wait(dve, rows_in[k], lambda n: 16 * ((n // HB + 1) // 2 + 1))
                    if grp + 1 >= 2:
                        at.wait(dve, out_done[k], lambda n: 16 * ST * ((n // HB + 1) // 2))
                    v.tensor_copy(token_of[k][:], rows[k][:, :, D + 3]).then_inc(S["token_of_set"], 1)
                    for i in range(ST):
                        last = TS(xn[:, i, :], rows[k][:, i, 0:D], rows[k][:, i, D:D + 1],
                                  rows[k][:, i, D + 1:D + 2], ALU.subtract, ALU.mult)
                    last.then_inc(S["xn_set"], 1)
                if group_ok(grp + 1) and hb >= HB - KT:
                    k = hb - (HB - KT)
                    at.wait(dve, S["x_hi"], lambda n: KT * (n // HB + 1) + k + 1)
                    TT(out=xT_lo[(grp + 1) % 2][:, k, :], in0=xps[k][:], in1=xT_hi[(grp + 1) % 2][:, k, :].bitcast(F32),
                       op=ALU.subtract).then_inc(S["x_lo"], 1)
                if unit_ok(n):
                    at.wait(dve, S["hid_hi_set"], lambda n: n + 1)
                    TT(out=hid_lo[n % 4][:], in0=hid[n % 4][:], in1=hid_hi[n % 4][:].bitcast(F32),
                       op=ALU.subtract).then_inc(S["hid_lo_set"], 1)
                last = n - LAG
                if unit_ok(last) and last % HB == HB - 1:
                    g = last // HB
                    e = at.value(lambda n: (n - LAG) // PER)
                    for s in range(ST):
                        at.wait(dve, acc_full[s], lambda n: (n - LAG) // HB + 1)
                        TT(out=biased[s][:], in0=acc[s][:, 0:D],
                           in1=b2_all[:, bass.ds(e, 1), :].rearrange("p o d -> p (o d)"), op=ALU.add) \
                            .then_inc(S["biased_set"], 1)
                    for s in range(ST):
                        at.wait(dve, S["biased_set"], lambda n: ST * ((n - LAG) // HB) + s + 1)
                        STT(out=result[g % 2][:, s, :], in0=biased[s][:], scalar=rows[g % 2][:, s, D + 2:D + 3],
                            in1=rows[g % 2][:, s, 0:D], op0=ALU.mult, op1=ALU.add).then_inc(S["result_set"], 1)

            EXPERT_PIPE.run(dve, step)

        @block.tensor
        def _(pe):
            mm = nc.tensor.matmul

            def three(out, w_hi, w_lo, m_hi, m_lo, first, last):
                mm(out, w_hi, m_hi, start=first, stop=False)
                mm(out, w_hi, m_lo, start=False, stop=False)
                return mm(out, w_lo, m_hi, start=False, stop=last)

            pe.wait_ge(S["bias_in"], 32)
            nc.tensor.transpose(xps[0][:, 0:EXPERTS * HB], b1_in[:], ident[0:EXPERTS * HB, 0:EXPERTS * HB]) \
                .then_inc(S["b1_full"], 1)
            pe.wait_ge(S["b1_set"], 1)

            def step(at):
                n = at.t
                grp, hb = n // HB, n % HB
                if group_ok(grp + 1) and hb >= HB - KT:
                    k = hb - (HB - KT)
                    if k == 0:
                        at.wait(pe, S["xn_set"], lambda n: n // HB + 2)
                        if grp >= 0:
                            at.wait(pe, S["x_lo"], lambda n: KT * (n // HB + 1))
                    for i in range(ST):
                        last = nc.tensor.transpose(xps[k][:, i * P:i * P + P], xn[:, i, k * P:k * P + P], ident[:])
                    last.then_inc(S["x_turned"], 1)
                if unit_ok(n):
                    if hb == 0:
                        at.wait(pe, S["x_lo"], lambda n: KT * (n // HB + 1))
                    if grp % 2 == 0:
                        at.wait(pe, S["w1_lo_set"], lambda n: n // PER * HB + n % HB + 1)
                    if n >= 2:
                        at.wait(pe, S["hid_set"], lambda n: n - 1)
                    blk = slice(hb * P, hb * P + P)
                    for k in range(KT):
                        last = three(hps[n % 2][:], w1_hi[:, k, blk], w1_lo[:, k, blk],
                                     xT_hi[grp % 2][:, k, :], xT_lo[grp % 2][:, k, :], k == 0, k == KT - 1)
                    last.then_inc(S["hid_full"], 1)
                u = n - LAG
                if unit_ok(u):
                    ub = u % HB
                    if u // HB % 2 == 0:
                        at.wait(pe, S["w2_lo_set"], lambda n: (n - LAG) // PER * HB + (n - LAG) % HB + 1)
                    at.wait(pe, S["hid_lo_set"], lambda n: n - LAG + 1)
                    for s in range(ST):
                        if ub == 0 and u >= HB:
                            at.wait(pe, S["biased_set"], lambda n: ST * ((n - LAG) // HB - 1) + s + 1)
                        q = slice(s * P, s * P + P)
                        last = three(acc[s][:, 0:D], hid_hi[u % 4][:, q], hid_lo[u % 4][:, q],
                                     w2_hi[:, ub, :], w2_lo[:, ub, :], ub == 0, ub == HB - 1)
                        if ub == HB - 1:
                            last.then_inc(acc_full[s], 1)
                    if ub == HB - 1:
                        pe.wait_ge(acc_full[ST - 1], at.value(lambda n: (n - LAG) // HB + 1))
                        pe.sem_inc(S["hid_used"], 1)
                    else:
                        last.then_inc(S["hid_used"], 1)

            EXPERT_PIPE.run(pe, step)


def build(nc, x, ctx_in, mask, wq, bq, wk, bk, wv, bv, gamma, beta, wg, w1, b1, w2, b2, out):
    dram = dict(x=x, ctx=ctx_in, mask=mask, wq=wq, bq=bq, wk=wk, bk=bk, wv=wv, bv=bv, gamma=gamma, beta=beta,
                wg=wg, w1=w1, b1=b1, w2=w2, b2=b2, out=out,
                slots=nc.dram_tensor("slots", [TOKENS, ROW], F32, kind="Internal").ap())
    with nc.sbuf_tensor("ident", [P, P], F32) as ident:
        keep = {"ident": ident}
        attention(nc, dram, keep)
        experts(nc, dram, keep)


_INS = ["x", "ctx_1024", "mask_BxSxS2_ik1", "L0_xattn_Wq", "L0_xattn_bq", "L0_xattn_Wk", "L0_xattn_bk",
        "L0_xattn_Wv", "L0_xattn_bv", "L0_xattn_ln_gamma", "L0_xattn_ln_beta", "L0_ffn_wg", "L0_ffn_w1",
        "L0_ffn_b1", "L0_ffn_w2", "L0_ffn_b2"]


def kernel(**inputs):
    import numpy as _np
    import concourse.bacc as _bacc
    from concourse.bass_utils import run_bass_kernel_spmd as _run

    nc = _bacc.Bacc("TRN2", target_bir_lowering=False, num_devices=1)
    arrays, args = {}, []
    for name in _INS:
        a = _np.ascontiguousarray(inputs[name])
        arrays[f"in_{name}"] = a
        args.append(nc.dram_tensor(f"in_{name}", a.shape, mybir.dt.from_np(a.dtype), kind="ExternalInput").ap())
    out = nc.dram_tensor("out", (NB, SQ, D), F32, kind="ExternalOutput").ap()
    build(nc, *args, out)
    r = _run(nc, [arrays], core_ids=[0])
    return r.results[0]["out"]
```

```python
from contextlib import ExitStack

import concourse.bass as bass
from concourse import mybir

ALU = mybir.AluOpType
ACT = mybir.ActivationFunctionType
AX = mybir.AxisListType
F32 = mybir.dt.float32
F32R = mybir.dt.float32r
BF16 = mybir.dt.bfloat16
I32 = mybir.dt.int32
U32 = mybir.dt.uint32

P = 128
NB, SQ, D = 16, 512, 256
SK = 1601
KT = D // P
QT = SQ // P
NT = NB * QT
JF = SK // P
JR = SK - JF * P
JT = JF + 1
PIECES = [(0, 4), (4, 7), (7, 10), (10, JT)]
CH = 512
NC = (SK + CH - 1) // CH
CW = 2 * ((SK + 2 * NC - 1) // (2 * NC))
SKP = NC * CW
EXPERTS, HID = 8, 1024
TOKENS = NB * SQ
CAP = TOKENS // EXPERTS
ROW = D + 4
SCALE = 1.0 / float(D) ** 0.5
EPS = 1e-5
MASKED = -1e30
NOWHERE = 65536.0
SCATTERED = [(0, 1), (2,), (3,), ()]
FIRST_STEP, LAST_STEP = -QT, NT + QT


class Pipeline:

    def __init__(self, name, first, loop_from, period, loops, last):
        self.name = name
        self.first, self.loop_from, self.period, self.loops, self.last = first, loop_from, period, loops, last

    def run(self, eng, step):
        counts = [eng.alloc_register(f"{self.name}{n}") for n in range(3)]
        for t in range(self.first, self.loop_from):
            step(At(self, t))
        with eng.Fori(0, self.loops) as it:
            for u in range(self.period):
                step(At(self, self.loop_from + u, it, counts))
        for t in range(self.loop_from + self.loops * self.period, self.last + 1):
            step(At(self, t))


class At:

    def __init__(self, pipe, t, it=None, counts=()):
        self.pipe, self.t, self.it, self.counts = pipe, t, it, counts
        self.batch, self.quarter = t // QT, t % QT

    def value(self, f):
        v = f(self.t)
        if self.it is None:
            return v
        by = f(self.t + self.pipe.period) - v
        assert all(f(self.t + n * self.pipe.period) == v + n * by for n in range(self.pipe.loops))
        return v + self.it * by

    def count(self, f):
        v = self.value(f)
        assert not isinstance(v, int) or v > 0, "a wait for nothing"
        return v

    def ahead(self, eng, *fs):
        counts = [self.count(f) for f in fs]
        for n, v in enumerate(counts):
            if not isinstance(v, int):
                eng.reg_mov(self.counts[n], v)
                counts[n] = self.counts[n]
        return counts


ATTENTION = Pipeline("attention", FIRST_STEP, 2 * QT, 2 * QT, NB // 2 - 2, LAST_STEP)


def tile_ok(t):
    return 0 <= t < NT


def batch_ok(b):
    return 0 <= b < NB


def turn_groups(t):
    out = []
    if tile_ok(t - 1):
        out += [("probs", t - 1, c) for c in range(NC)]
    b, r = t // QT + 1, t % QT
    if batch_ok(b):
        out.append(("ctx", b, 2 * r))
    if tile_ok(t - 2):
        out.append(("attn", t - 2, 0))
    if tile_ok(t - 3):
        out.append(("xn2", t - 3, 0))
    if batch_ok(b):
        out.append(("ctx", b, 2 * r + 1))
        if r == 1:
            out += [("xn", b, 0), ("xn", b, 1)]
        if r == 2:
            out += [("qk", b, 0), ("qk", b, 1)]
    return out


def small_groups(t):
    out = []
    b, r = t // QT + 1, t % QT
    if batch_ok(b - 2) and r == 3:
        out.append(("places", b - 2))
    if tile_ok(t - 2):
        out.append(("value", t - 2))
    if tile_ok(t - 3):
        out.append(("logits", t - 3))
    if batch_ok(b) and r == 2:
        out.append(("keybias", b))
    return out


SETUP_TURNS = [("setup", 0, n) for n in range(3)]
SPLIT_KINDS = ("probs", "ctx", "qk")
TURNS = SETUP_TURNS + [g for t in range(FIRST_STEP, LAST_STEP + 1) for g in turn_groups(t)]
TURN_NO = {g: n for n, g in enumerate(TURNS)}
SPLITS = {g: n for n, g in enumerate(g for g in TURNS if g[0] in SPLIT_KINDS)}
SETUP_SMALL = [("setup", 0)]
READ_BY_ACT = ("logits",)
SMALLS = SETUP_SMALL + [g for t in range(FIRST_STEP, LAST_STEP + 1) for g in small_groups(t)]
SMALL_NO = {g: n for n, g in enumerate(SMALLS)}
SMALL_READ = {g: n for n, g in enumerate(g for g in SMALLS if g[0] not in READ_BY_ACT)}


def nth(table, group, t0, per=1):
    kind, of, *rest = group

    def f(t):
        shift = (t - t0) // per
        return table[(kind, of + shift, *rest)] + 1
    return f


def attention(nc, dram, keep):
    with ExitStack() as ctx:
        def sb(name, shape, dt=F32):
            return ctx.enter_context(nc.sbuf_tensor(name, shape, dt))

        def sem(name):
            return ctx.enter_context(nc.semaphore(name))

        ident = keep["ident"]
        tri = sb("tri", [P, P], BF16)
        ones = sb("ones", [P, P], BF16)
        halves = sb("halves", [P, QT])
        rank = sb("rank", [P, QT, EXPERTS])
        token = sb("token", [P, QT])
        wv = sb("wv", [P, KT, D])
        wg = sb("wg", [P, KT, EXPERTS])
        bq = sb("bq", [P, KT])
        bk = sb("bk", [P, KT])
        mqk = sb("mqk", [P, KT, D])
        qbias = sb("qbias", [P, KT])
        kbias = sb("kbias", [P, KT])
        bqk = sb("bqk", [P, 1])
        bqw = sb("bqw", [P, KT, P])
        bv_all = sb("bv_all", [P, D])
        gamma_all = sb("gamma_all", [P, D])
        beta_all = sb("beta_all", [P, D])

        ctx_in = sb("ctx_in", [P, JT, D])
        ctx_hi = [sb(f"ctx_hi{n}", [P, JT, D], F32R) for n in range(2)]
        ctx_lo = [sb(f"ctx_lo{n}", [P, JT, D], F32R) for n in range(2)]
        ctxT_hi = [sb(f"ctxT_hi{n}", [P, KT, SKP], F32R) for n in range(2)]
        ctxT_lo = [sb(f"ctxT_lo{n}", [P, KT, SKP], F32R) for n in range(2)]
        xb = sb("xb", [P, QT, D])
        xnT = sb("xnT", [P, KT, SQ])
        qkT_hi = [sb(f"qkT_hi{n}", [P, KT, SQ], F32R) for n in range(2)]
        qkT_lo = [sb(f"qkT_lo{n}", [P, KT, SQ], F32R) for n in range(2)]
        kb16 = [sb(f"kb16_{n}", [P, QT]) for n in range(2)]
        mask_in = sb("mask_in", [P, SK], I32)
        mask_add = [sb(f"mask_add{n}", [P, SKP], BF16) for n in range(2)]
        probs = sb("probs", [P, SKP])
        probsT_hi = sb("probsT_hi", [P, JT, P], F32R)
        probsT_lo = sb("probsT_lo", [P, JT, P], F32R)
        wq, wk = (probs[:, n * KT * D:(n + 1) * KT * D].rearrange("p (k n) -> p k n", k=KT) for n in range(2))
        wq_t, wk_t = (xnT[:, n, :].rearrange("p (k n) -> p k n", k=KT) for n in range(2))
        rowmax = sb("rowmax", [P, 2])
        fullmax = sb("fullmax", [P, 2])
        negmax = sb("negmax", [P, 2])
        rowsum = sb("rowsum", [P, 2])
        rsum = sb("rsum", [P, 2])
        attn = sb("attn", [P, D])
        attnT = sb("attnT", [P, KT, P])
        xres = [sb(f"xres{n}", [P, D]) for n in range(4)]
        value = sb("value", [P, D])
        scaled = sb("scaled", [P, D])
        bn1 = sb("bn1", [P, 6])
        mv1 = sb("mv1", [P, 2])
        ve1 = sb("ve1", [P, 1])
        rstd1 = sb("rstd1", [P, 1])
        bn2 = sb("bn2", [P, 6])
        mv2 = sb("mv2", [P, 2])
        ve2 = sb("ve2", [P, 1])
        bnx = sb("bnx", [P, QT, 6])
        mvx = sb("mvx", [P, QT, 2])
        vex = sb("vex", [P, QT])
        rstdx = sb("rstdx", [P, QT])
        row = [sb(f"row{n}", [P, QT, ROW]) for n in range(2)]
        xn2 = sb("xn2", [P, D])
        xn2T = sb("xn2T", [P, KT, P])
        logits = sb("logits", [P, QT, EXPERTS])
        best = sb("best", [P, QT])
        below = sb("below", [P, QT, EXPERTS])
        gates = sb("gates", [P, QT, EXPERTS])
        gsum = sb("gsum", [P, QT])
        tied = sb("tied", [P, QT, EXPERTS])
        pick = sb("pick", [P, QT])
        onehot = sb("onehot", [P, QT, EXPERTS], BF16)
        added = sb("added", [P, EXPERTS])
        count = sb("count", [P, EXPERTS])
        countb = sb("countb", [P, EXPERTS], BF16)
        placed = sb("placed", [P, QT, EXPERTS])
        place = sb("place", [P, QT])
        base = sb("base", [P, QT])
        over = sb("over", [P, QT])
        slotf = sb("slotf", [P, QT])
        slot = [sb(f"slot{n}", [P, QT], U32) for n in range(2)]
        blank = sb("blank", [P, ROW])

        scores = ctx.enter_context(nc.psum_tensor("scores", [P, NC, CH], F32))
        turn = [ctx.enter_context(nc.psum_tensor(f"turn{n}", [P, CH], F32)) for n in range(2)]
        outp = ctx.enter_context(nc.psum_tensor("outp", [P, CH], F32))
        small = ctx.enter_context(nc.psum_tensor("small", [P, CH], F32))

        S = {}
        for name in ("consts wqk_in weights_in bcast_in blank_set blanks_out "
                     "turn_full turn_evac turn_low small_full small_read logits_read setup_done "
                     "x_in ctx_in0 ctx_in1 ctx_in2 ctx_in3 mask_in xres_in0 xres_in1 xres_in2 xres_in3 "
                     "scores_full mask_ready max_raw max_full max_neg exp_done sum_inv "
                     "out_full attn_ready ctx_hi_done ctx_lo_done xres_beta "
                     "value_set bn1_set mv1_set var1 rstd1 scaled_set x1_done bn2_set mv2_set var2 rstd2 xn2_done "
                     "bnx_set mvx_set varx rstdx xnorm_done "
                     "best_set below_set gates_done tied_set pick_set onehot_done added_set count_set countb_set "
                     "placed_set place_set base_set over_set part_set slot_ready gsum_set gate_done token_set token_next "
                     "store0 store1 scatter0 scatter1").split():
            S[name] = sem(name)
        MET = (S["consts"], 14)
        store_done = [S["store0"], S["store1"]]
        scatter_done = [S["scatter0"], S["scatter1"]]
        ctx_in_done = [S[f"ctx_in{n}"] for n in range(QT)]
        xres_in = [S[f"xres_in{n}"] for n in range(4)]

        x_v = dram["x"].rearrange("b (i p) d -> b p i d", p=P)
        ctx_v = dram["ctx"]
        mask_v = dram["mask"].rearrange("b (i p) k -> (b i) p k", p=P)
        x_t = dram["x"].rearrange("b (i p) d -> (b i) p d", p=P)
        out_t = dram["out"].rearrange("b (i p) d -> (b i) p d", p=P)
        slots = dram["slots"]

        def piece_keys(q):
            j0, j1 = PIECES[q]
            return slice(j0 * P, min(j1 * P, SK))

        def piece_in(at, eng):
            loads = 2 if at.quarter == QT - 1 else 1
            eng.wait_ge(ctx_in_done[at.quarter], at.count(lambda t: 16 * loads * (t // QT + 2)))

        block = ctx.enter_context(nc.Block())

        @block.sync
        def _(sp):
            def load_piece(nb, q):
                j0, j1 = PIECES[q]
                full = min(j1, JF)
                sp.dma_start(ctx_in[:, j0:full, :], ctx_v[nb, j0 * P:full * P, :].rearrange("(j p) d -> p j d", p=P)) \
                    .then_inc(ctx_in_done[q], 16)
                if j1 == JT:
                    sp.dma_start(ctx_in[0:JR, JF, :], ctx_v[nb, JF * P:SK, :]).then_inc(ctx_in_done[q], 16)

            for dst, src in ((wq, "wq"), (wk, "wk")):
                sp.dma_start(dst[:], dram[src].rearrange("(k p) n -> p k n", p=P)).then_inc(S["wqk_in"], 16)
            for dst, src in ((bq, "bq"), (bk, "bk")):
                sp.dma_start(dst[:], dram[src].rearrange("(k p) -> p k", p=P), allow_slow_non_contiguous=True) \
                    .then_inc(S["wqk_in"], 16)
            load_piece(0, 0)
            sp.dma_start(xb[:], x_v[0]).then_inc(S["x_in"], 16)
            for dst, src in ((wv, "wv"), (wg, "wg")):
                sp.dma_start(dst[:], dram[src].rearrange("(k p) n -> p k n", p=P)).then_inc(S["weights_in"], 16)
            for dst, src in ((bv_all, "bv"), (gamma_all, "gamma"), (beta_all, "beta")):
                sp.dma_start(dst[:], dram[src].partition_broadcast(P)).then_inc(S["bcast_in"], 16)
            for q in range(1, QT):
                load_piece(0, q)

            def step(at):
                t, b, r = at.t, at.batch, at.quarter
                if tile_ok(t - 3):
                    count, = at.ahead(sp, lambda t: t - 2)
                    sp.wait_ge(*MET)
                    sp.wait_ge(S["x1_done"], count)
                    sp.dma_start(out_t[at.value(lambda t: t - 3)],
                                 row[(t - 3) // QT % 2][:, (t - 3) % QT, 0:D]).then_inc(store_done[(t - 3) // QT % 2], 16)
                if tile_ok(t + 1):
                    if tile_ok(t):
                        count, = at.ahead(sp, lambda t: t + 1)
                        sp.wait_ge(*MET)
                        sp.wait_ge(S["mask_ready"], count)
                    sp.dma_start(mask_in[:], mask_v[at.value(lambda t: t + 1)]).then_inc(S["mask_in"], 16)
                if tile_ok(t):
                    if tile_ok(t - 4):
                        count, = at.ahead(sp, lambda t: t - 3)
                        sp.wait_ge(*MET)
                        sp.wait_ge(S["x1_done"], count)
                    sp.dma_start(xres[t % 4][:], x_t[at.value(lambda t: t)]).then_inc(xres_in[t % 4], 16)
                nb, q = (t - 2) // QT + 2, (t - 2) % QT
                if 0 < nb < NB:
                    turn_full, ctx_hi_done, ctx_lo_done = at.ahead(sp, nth(TURN_NO, ("ctx", nb - 1, 2 * q + 1), t, QT),
                        lambda t: t + QT - 1,
                        lambda t: t + QT - 1)
                    sp.wait_ge(*MET)
                    sp.wait_ge(S["turn_full"], turn_full)
                    sp.wait_ge(S["ctx_hi_done"], ctx_hi_done)
                    sp.wait_ge(S["ctx_lo_done"], ctx_lo_done)
                    load_piece(at.value(lambda t: (t - 2) // QT + 2), q)
                if 0 < b + 2 < NB and r == 3:
                    count, = at.ahead(sp, nth(TURN_NO, ("xn", b + 1, 1), t, QT))
                    sp.wait_ge(*MET)
                    sp.wait_ge(S["turn_full"], count)
                    sp.dma_start(xb[:], x_v[at.value(lambda t: t // QT + 2)]).then_inc(S["x_in"], 16)
                if 0 <= t < 2 * QT:
                    if t == 0:
                        sp.wait_ge(S["blank_set"], 3)
                    sp.dma_start(slots.rearrange("(c p n) w -> c p n w", c=2 * QT, p=P)[t],
                                 blank[:].unsqueeze(1).broadcast_to([P, TOKENS // P // (2 * QT), ROW])) \
                        .then_inc(S["blanks_out"], 16)

            ATTENTION.run(sp, step)
            for n in range(2):
                sp.wait_ge(store_done[n], 16 * NT // 2)
                sp.wait_ge(scatter_done[n], 16 * NT // 2)

        @block.gpsimd
        def _(pool):
            g = nc.gpsimd
            g.memset(ident[:], 0.0).then_inc(S["consts"], 1)
            g.memset(tri[:], 0.0).then_inc(S["consts"], 1)
            g.memset(ones[:], 1.0).then_inc(S["consts"], 1)
            g.memset(halves[:], -0.5).then_inc(S["consts"], 1)
            for n in range(2):
                g.memset(mask_add[n][:, SK:SKP], MASKED).then_inc(S["consts"], 1)
                for part in (ctxT_hi[n], ctxT_lo[n]):
                    g.memset(part[:, :, SK:SKP].bitcast(F32), 0.0).then_inc(S["consts"], 1)
            g.iota(rank[:], pattern=[[0, QT], [-1, EXPERTS]], base=EXPERTS, channel_multiplier=0,
                   allow_small_or_imprecise_dtypes=True).then_inc(S["consts"], 1)
            g.iota(token[:], pattern=[[P, QT]], base=0, channel_multiplier=1,
                   allow_small_or_imprecise_dtypes=True).then_inc(S["consts"], 1)
            pool.wait_ge(S["consts"], 12)
            g.affine_select(out=ident[:], in_=ident[:], compare_op=ALU.not_equal, fill=1.0, base=0,
                            pattern=[[-1, P]], channel_multiplier=1).then_inc(S["consts"], 1)
            g.affine_select(out=tri[:], in_=tri[:], compare_op=ALU.is_ge, fill=1.0, base=0,
                            pattern=[[-1, P]], channel_multiplier=1).then_inc(S["consts"], 1)
            g.memset(blank[:, 0:D + 3], 0.0).then_inc(S["blank_set"], 1)
            g.memset(blank[:, D + 3:ROW], NOWHERE).then_inc(S["blank_set"], 1)
            g.memset(countb[:], 0.0).then_inc(S["blank_set"], 1)
            pool.wait_ge(S["bcast_in"], 48)

            def low_part(at, b, r):
                j0, j1 = PIECES[r]
                full = min(j1, JF)
                par = b % 2
                pool.wait_ge(S["ctx_hi_done"], at.count(lambda t: t + QT + 1))
                last = g.tensor_tensor(out=ctx_lo[par][:, j0:full, :], in0=ctx_in[:, j0:full, :],
                                       in1=ctx_hi[par][:, j0:full, :].bitcast(F32), op=ALU.subtract)
                if j1 == JT:
                    last = g.tensor_tensor(out=ctx_lo[par][0:JR, JF, :], in0=ctx_in[0:JR, JF, :],
                                           in1=ctx_hi[par][0:JR, JF, :].bitcast(F32), op=ALU.subtract)
                last.then_inc(S["ctx_lo_done"], 1)

            def step(at):
                t, b, r = at.t, at.batch, at.quarter
                if tile_ok(t - 3):
                    pool.wait_ge(S["var2"], at.count(lambda t: t - 2))
                    k = (t - 3) // QT % 2
                    g.tensor_tensor(out=row[k][:, (t - 3) % QT, D + 1:D + 2], in0=ve2[:], in1=halves[:, 0:1],
                                    op=ALU.pow).then_inc(S["rstd2"], 1)
                if batch_ok(b + 1) and r == 0:
                    pool.wait_ge(S["varx"], at.count(lambda t: t // QT + 2))
                    g.tensor_tensor(out=rstdx[:], in0=vex[:], in1=halves[:], op=ALU.pow).then_inc(S["rstdx"], 1)
                if tile_ok(t - 2):
                    pool.wait_ge(S["var1"], at.count(lambda t: t - 1))
                    g.tensor_tensor(out=rstd1[:], in0=ve1[:], in1=halves[:, 0:1], op=ALU.pow).then_inc(S["rstd1"], 1)
                if batch_ok(b - 2):
                    k = b % 2
                    if r == 0:
                        slot_ready, gate_done, token_set = at.ahead(
                            pool, lambda t: t // QT - 1, lambda t: t // QT - 1, lambda t: t // QT - 1)
                        pool.wait_ge(*MET)
                        pool.wait_ge(S["slot_ready"], slot_ready)
                        pool.wait_ge(S["gate_done"], gate_done)
                        pool.wait_ge(S["token_set"], token_set)
                    if t == 2 * QT:
                        pool.wait_ge(S["blanks_out"], 2 * QT * 16)
                    for i in range(QT) if b - 2 == NB - 1 else SCATTERED[r]:
                        g.indirect_dma_start(
                            out=slots, out_offset=bass.IndirectOffsetOnAxis(ap=slot[k][:, i:i + 1], axis=0),
                            in_=row[k][:, i, :], in_offset=None, bounds_check=TOKENS - 1, oob_is_err=False) \
                            .then_inc(scatter_done[k], 16)
                if batch_ok(b + 1):
                    low_part(at, b + 1, r)
                if tile_ok(t - 1):
                    pool.wait_ge(xres_in[(t - 1) % 4], at.count(lambda t: 16 * ((t - 1) // 4 + 1)))
                    g.tensor_tensor(out=xres[(t - 1) % 4][:], in0=xres[(t - 1) % 4][:], in1=beta_all[:],
                                    op=ALU.add).then_inc(S["xres_beta"], 1)

            ATTENTION.run(pool, step)

        @block.scalar
        def _(act):
            a = nc.scalar

            def evac(at, group, t0, per, out, in_, **kw):
                act.wait_ge(S["turn_full"], at.count(nth(TURN_NO, group, t0, per)))
                a.activation(out, in_, kw.pop("func", ACT.Copy), **kw).then_inc(S["turn_evac"], 1)

            def ctx_high(at, i):
                par = (at.batch + 1) % 2
                g = ("ctx", at.batch + 1, i)
                keys = piece_keys(i // 2)
                evac(at, g, at.t, QT, ctxT_hi[par][:, i % 2, keys], turn[TURN_NO[g] % 2][:, 0:keys.stop - keys.start])

            for n, dst in enumerate((wq_t, wk_t, mqk)):
                act.wait_ge(S["turn_full"], n + 1)
                a.activation(dst[:].rearrange("p k n -> p (k n)"), turn[n % 2][:], ACT.Copy).then_inc(S["turn_evac"], 1)

            def step(at):
                t, b, r = at.t, at.batch, at.quarter
                if tile_ok(t - 1):
                    for c in range(NC):
                        g = ("probs", t - 1, c)
                        bank = turn[TURN_NO[g] % 2]
                        if c < NC - 1:
                            dst, src = probsT_hi[:, 4 * c:4 * c + 4, :].rearrange("p j q -> p (j q)"), bank[:]
                        else:
                            dst, src = probsT_hi[0:JR, JF, :], bank[0:JR, 0:P]
                        evac(at, g, t, 1, dst, src)
                if batch_ok(b + 1):
                    ctx_high(at, 2 * r)
                if tile_ok(t - 2):
                    g = ("attn", t - 2, 0)
                    evac(at, g, t, 1, attnT[:].rearrange("p k q -> p (k q)"), turn[TURN_NO[g] % 2][:, 0:KT * P])
                if tile_ok(t):
                    act.wait_ge(S["max_neg"], at.count(lambda t: t + 1))
                    a.activation(probs[:], probs[:], ACT.Exp, bias=negmax[:, t % 2:t % 2 + 1], scale=SCALE,
                                 accum_out=rowsum[:, t % 2:t % 2 + 1]).then_inc(S["exp_done"], 1)
                if batch_ok(b + 1):
                    par = (b + 1) % 2
                    piece_in(at, act)
                    j0, j1 = PIECES[r]
                    full = min(j1, JF)
                    last = a.activation(ctx_hi[par][:, j0:full, :], ctx_in[:, j0:full, :], ACT.Copy)
                    if j1 == JT:
                        last = a.activation(ctx_hi[par][0:JR, JF, :], ctx_in[0:JR, JF, :], ACT.Copy)
                    last.then_inc(S["ctx_hi_done"], 1)
                if tile_ok(t - 3):
                    g = ("xn2", t - 3, 0)
                    evac(at, g, t, 1, xn2T[:].rearrange("p k q -> p (k q)"), turn[TURN_NO[g] % 2][:, 0:KT * P])
                if batch_ok(b + 1):
                    ctx_high(at, 2 * r + 1)
                if tile_ok(t - 1):
                    act.wait_ge(S["sum_inv"], at.count(lambda t: t))
                    act.wait_ge(S["out_full"], at.count(lambda t: t))
                    a.activation(attn[:], outp[:, 0:D], ACT.Copy, scale=rsum[:, (t - 1) % 2:(t - 1) % 2 + 1]) \
                        .then_inc(S["attn_ready"], 1)
                if tile_ok(t - 3):
                    act.wait_ge(S["small_full"], at.count(nth(SMALL_NO, ("logits", t - 3), t)))
                    if (t - 3) % QT == 0 and t - 3 > 0:
                        act.wait_ge(S["below_set"], at.count(lambda t: (t - 3) // QT))
                    a.activation(logits[:, (t - 3) % QT, :], small[:, 0:EXPERTS], ACT.Copy) \
                        .then_inc(S["logits_read"], 1)
                if batch_ok(b + 1):
                    if r == 1:
                        for k in range(KT):
                            g = ("xn", b + 1, k)
                            evac(at, g, t, QT, xnT[:, k, :], turn[TURN_NO[g] % 2][:])
                    if r == 2:
                        for m in range(KT):
                            g = ("qk", b + 1, m)
                            evac(at, g, t, QT, qkT_hi[par][:, m, :], turn[TURN_NO[g] % 2][:],
                                 func=ACT.Identity, bias=qbias[:, m:m + 1])
                if batch_ok(b - 1) and r == 2:
                    act.wait_ge(S["below_set"], at.count(lambda t: t // QT))
                    a.activation(gates[:].rearrange("p i e -> p (i e)"), below[:].rearrange("p i e -> p (i e)"),
                                 ACT.Exp).then_inc(S["gates_done"], 1)

            ATTENTION.run(act, step)

        @block.vector
        def _(dve):
            v = nc.vector
            TT, TS, STT = v.tensor_tensor, v.tensor_scalar, v.scalar_tensor_tensor

            dve.wait_ge(S["consts"], 14)
            dve.wait_ge(S["blank_set"], 3)
            v.memset(count[:], 0.0).then_inc(S["count_set"], 1)
            dve.wait_ge(S["wqk_in"], 64)
            for k in range(KT):
                last = v.tensor_copy(bqw[:, k, :], bq[:, k:k + 1].broadcast_to([P, P]))
            last.then_inc(S["setup_done"], 1)
            dve.wait_ge(S["small_full"], 1)
            v.tensor_copy(qbias[:], small[:, 0:KT])
            v.tensor_copy(kbias[:], small[:, KT:2 * KT])
            v.tensor_copy(bqk[:], small[:, 2 * KT:2 * KT + 1]).then_inc(S["small_read"], 1)
            dve.wait_ge(S["small_read"], 1)
            dve.wait_ge(S["bcast_in"], 48)

            def low(at, group, t0, per, out, psum, hi, bias=None):
                dve.wait_ge(S["turn_evac"], at.count(nth(TURN_NO, group, t0, per)))
                if bias is None:
                    ins = TT(out=out, in0=psum, in1=hi.bitcast(F32), op=ALU.subtract)
                else:
                    ins = STT(out=out, in0=psum, scalar=bias, in1=hi.bitcast(F32), op0=ALU.add, op1=ALU.subtract)
                ins.then_inc(S["turn_low"], 1)

            def probs_low(at, c):
                t = at.t
                g = ("probs", t - 1, c)
                bank = turn[TURN_NO[g] % 2]
                if c < NC - 1:
                    sl = lambda a: a[:, 4 * c:4 * c + 4, :].rearrange("p j q -> p (j q)")
                    low(at, g, t, 1, sl(probsT_lo), bank[:], sl(probsT_hi))
                else:
                    low(at, g, t, 1, probsT_lo[0:JR, JF, :], bank[0:JR, 0:P], probsT_hi[0:JR, JF, :])

            def mask_prep(at):
                dve.wait_ge(S["mask_in"], at.count(lambda t: 16 * (t + 2)))
                TS(mask_add[(at.t + 1) % 2][:, 0:SK], mask_in[:], 0.0, MASKED, ALU.is_equal, ALU.mult) \
                    .then_inc(S["mask_ready"], 1)

            def ctx_low(at, i):
                par = (at.batch + 1) % 2
                g = ("ctx", at.batch + 1, i)
                keys = piece_keys(i // 2)
                low(at, g, at.t, QT, ctxT_lo[par][:, i % 2, keys], turn[TURN_NO[g] % 2][:, 0:keys.stop - keys.start],
                    ctxT_hi[par][:, i % 2, keys])

            def step(at):
                t, b, r = at.t, at.batch, at.quarter
                if tile_ok(t - 1):
                    dve.wait_ge(S["exp_done"], at.count(lambda t: t))
                    v.reciprocal(rsum[:, (t - 1) % 2:(t - 1) % 2 + 1], rowsum[:, (t - 1) % 2:(t - 1) % 2 + 1]) \
                        .then_inc(S["sum_inv"], 1)
                    probs_low(at, 0)
                if tile_ok(t - 3):
                    k, i = (t - 3) // QT % 2, (t - 3) % QT
                    x1 = row[k][:, i, 0:D]
                    dve.wait_ge(S["rstd1"], at.count(lambda t: t - 2))
                    dve.wait_ge(S["xres_beta"], at.count(lambda t: t - 2))
                    dve.wait_ge(S["scaled_set"], at.count(lambda t: t - 2))
                    if i == 0 and (t - 3) // QT >= 2:
                        dve.wait_ge(store_done[k], at.count(lambda t: 16 * QT * ((t - 3) // QT // 2)))
                        dve.wait_ge(scatter_done[k], at.count(lambda t: 16 * QT * ((t - 3) // QT // 2)))
                    STT(out=x1, in0=scaled[:], scalar=rstd1[:], in1=xres[(t - 3) % 4][:],
                        op0=ALU.mult, op1=ALU.add).then_inc(S["x1_done"], 1)
                if tile_ok(t - 1):
                    probs_low(at, 1)
                if tile_ok(t - 3):
                    dve.wait_ge(S["x1_done"], at.count(lambda t: t - 2))
                    v.bn_stats(bn2[:], x1).then_inc(S["bn2_set"], 1)
                if tile_ok(t - 1):
                    probs_low(at, 2)
                if tile_ok(t - 3):
                    bn2_set, = at.ahead(dve, lambda t: t - 2)
                    dve.wait_ge(*MET)
                    dve.wait_ge(S["bn2_set"], bn2_set)
                    v.bn_aggr(mv2[:], bn2[:]).then_inc(S["mv2_set"], 1)
                if tile_ok(t - 1):
                    probs_low(at, 3)
                if tile_ok(t - 3):
                    dve.wait_ge(S["mv2_set"], at.count(lambda t: t - 2))
                    v.tensor_scalar_add(ve2[:], mv2[:, 1:2], EPS).then_inc(S["var2"], 1)
                    v.tensor_copy(row[k][:, i, D:D + 1], mv2[:, 0:1])
                if tile_ok(t):
                    o = t % 2
                    scores_full, mask_ready = at.ahead(dve, lambda t: t + 1,
                        lambda t: t + 1)
                    dve.wait_ge(*MET)
                    dve.wait_ge(S["scores_full"], scores_full)
                    dve.wait_ge(S["mask_ready"], mask_ready)
                    v.tensor_tensor_reduce(out=probs[:].rearrange("p (c w) -> p c w", c=NC), in0=scores[:, :, 0:CW],
                                           in1=mask_add[o][:].rearrange("p (c w) -> p c w", c=NC), scale=1.0,
                                           scalar=-3e38, op0=ALU.add, op1=ALU.max,
                                           accum_out=rowmax[:, o:o + 1]).then_inc(S["max_raw"], 1)
                    kb = kb16[b % 2][:, r:r + 1]
                    dve.wait_ge(S["max_raw"], at.count(lambda t: t + 1))
                    STT(out=fullmax[:, o:o + 1], in0=rowmax[:, o:o + 1], scalar=SCALE, in1=kb,
                        op0=ALU.mult, op1=ALU.add).then_inc(S["max_full"], 1)
                    dve.wait_ge(S["max_full"], at.count(lambda t: t + 1))
                    TT(out=negmax[:, o:o + 1], in0=kb, in1=fullmax[:, o:o + 1], op=ALU.subtract) \
                        .then_inc(S["max_neg"], 1)
                if batch_ok(b + 1):
                    ctx_low(at, 2 * r)
                if tile_ok(t - 3):
                    k, i = (t - 3) // QT % 2, (t - 3) % QT
                    if tile_ok(t - 4):
                        dve.wait_ge(S["turn_full"], at.count(nth(TURN_NO, ("xn2", t - 4, 0), t)))
                    dve.wait_ge(S["rstd2"], at.count(lambda t: t - 2))
                    TS(xn2[:], row[k][:, i, 0:D], mv2[:, 0:1], row[k][:, i, D + 1:D + 2], ALU.subtract, ALU.mult) \
                        .then_inc(S["xn2_done"], 1)
                if batch_ok(b - 1) and r == 3:
                    places(at)
                if tile_ok(t + 1):
                    mask_prep(at)
                if batch_ok(b + 1):
                    if r == 0:
                        dve.wait_ge(S["x_in"], at.count(lambda t: 16 * (t // QT + 2)))
                        for i in range(QT):
                            last = v.bn_stats(bnx[:, i, :], xb[:, i, :])
                        last.then_inc(S["bnx_set"], 1)
                        count, = at.ahead(dve, lambda t: t // QT + 2)
                        dve.wait_ge(*MET)
                        dve.wait_ge(S["bnx_set"], count)
                        for i in range(QT):
                            last = v.bn_aggr(mvx[:, i, :], bnx[:, i, :])
                        last.then_inc(S["mvx_set"], 1)
                        dve.wait_ge(S["mvx_set"], at.count(lambda t: t // QT + 2))
                        v.tensor_scalar_add(vex[:], mvx[:, :, 1], EPS).then_inc(S["varx"], 1)
                    if r == 1:
                        dve.wait_ge(S["rstdx"], at.count(lambda t: t // QT + 2))
                        for i in range(QT):
                            last = TS(xb[:, i, :], xb[:, i, :], mvx[:, i, 0:1], rstdx[:, i:i + 1],
                                      ALU.subtract, ALU.mult)
                        last.then_inc(S["xnorm_done"], 1)
                if tile_ok(t - 2):
                    dve.wait_ge(S["small_full"], at.count(nth(SMALL_NO, ("value", t - 2), t)))
                    TT(out=value[:], in0=small[:, D:2 * D], in1=bv_all[:], op=ALU.add).then_inc(S["small_read"], 1)
                    dve.wait_ge(S["small_read"], at.count(nth(SMALL_READ, ("value", t - 2), t)))
                    v.bn_stats(bn1[:], value[:]).then_inc(S["bn1_set"], 1)
                if batch_ok(b + 1):
                    ctx_low(at, 2 * r + 1)
                if tile_ok(t - 2):
                    bn1_set, = at.ahead(dve, lambda t: t - 1)
                    dve.wait_ge(*MET)
                    dve.wait_ge(S["bn1_set"], bn1_set)
                    v.bn_aggr(mv1[:], bn1[:]).then_inc(S["mv1_set"], 1)
                    dve.wait_ge(S["mv1_set"], at.count(lambda t: t - 1))
                    v.tensor_scalar_add(ve1[:], mv1[:, 1:2], EPS).then_inc(S["var1"], 1)
                    STT(out=scaled[:], in0=value[:], scalar=mv1[:, 0:1], in1=gamma_all[:],
                        op0=ALU.subtract, op1=ALU.mult).then_inc(S["scaled_set"], 1)
                if batch_ok(b + 1):
                    par = (b + 1) % 2
                    if r == 2:
                        for m in range(KT):
                            g = ("qk", b + 1, m)
                            low(at, g, t, QT, qkT_lo[par][:, m, :], turn[TURN_NO[g] % 2][:], qkT_hi[par][:, m, :],
                                bias=qbias[:, m:m + 1])
                        dve.wait_ge(S["small_full"], at.count(nth(SMALL_NO, ("keybias", b + 1), t, QT)))
                        TS(kb16[par][:], small[:, 16:16 + QT], bqk[:], SCALE, ALU.add, ALU.mult) \
                            .then_inc(S["small_read"], 1)
                if batch_ok(b - 1) and r == 2:
                    router(at)

            nbatch = lambda t: t // QT

            def router(at):
                k = (at.batch - 1) % 2
                wide = lambda a: a.unsqueeze(2).broadcast_to([P, QT, EXPERTS])
                dve.wait_ge(S["logits_read"], at.count(lambda t: t - 2))
                v.tensor_reduce(best[:], logits[:], AX.X, ALU.max).then_inc(S["best_set"], 1)
                dve.wait_ge(S["best_set"], at.count(nbatch))
                TT(out=below[:], in0=logits[:], in1=wide(best[:]), op=ALU.subtract).then_inc(S["below_set"], 1)
                dve.wait_ge(S["below_set"], at.count(nbatch))
                STT(out=tied[:], in0=below[:], scalar=0.0, in1=rank[:], op0=ALU.is_equal, op1=ALU.mult) \
                    .then_inc(S["tied_set"], 1)
                dve.wait_ge(S["tied_set"], at.count(nbatch))
                v.tensor_reduce(pick[:], tied[:], AX.X, ALU.max).then_inc(S["pick_set"], 1)
                dve.wait_ge(S["pick_set"], at.count(nbatch))
                TT(out=onehot[:], in0=tied[:], in1=wide(pick[:]), op=ALU.is_equal).then_inc(S["onehot_done"], 1)
                if at.batch - 1 > 0:
                    dve.wait_ge(S["token_next"], at.count(lambda t: t // QT - 1))
                v.tensor_copy(row[k][:, :, D + 3], token[:]).then_inc(S["token_set"], 1)
                dve.wait_ge(S["token_set"], at.count(nbatch))
                v.tensor_scalar_add(token[:], token[:], float(SQ)).then_inc(S["token_next"], 1)

            def places(at):
                k = (at.batch - 1) % 2
                dve.wait_ge(S["small_full"], at.count(nth(SMALL_NO, ("places", at.batch - 1), at.t, QT)))
                TT(out=placed[:], in0=small[:, 32:32 + QT * EXPERTS].rearrange("p (i e) -> p i e", e=EXPERTS),
                   in1=onehot[:], op=ALU.mult).then_inc(S["small_read"], 1)
                v.tensor_reduce(added[:], onehot[:].rearrange("p i e -> p e i"), AX.X, ALU.add) \
                    .then_inc(S["added_set"], 1)
                dve.wait_ge(S["small_read"], at.count(nth(SMALL_READ, ("places", at.batch - 1), at.t, QT)))
                v.tensor_reduce(place[:], placed[:], AX.X, ALU.add).then_inc(S["place_set"], 1)
                dve.wait_ge(S["added_set"], at.count(nbatch))
                TT(out=count[:], in0=count[:], in1=added[:], op=ALU.add).then_inc(S["count_set"], 1)
                dve.wait_ge(S["place_set"], at.count(nbatch))
                TS(base[:], pick[:], -float(CAP), float(EXPERTS * CAP), ALU.mult, ALU.add).then_inc(S["base_set"], 1)
                TS(over[:], place[:], float(CAP), NOWHERE, ALU.is_ge, ALU.mult).then_inc(S["over_set"], 1)
                dve.wait_ge(S["count_set"], at.count(lambda t: t // QT + 1))
                v.tensor_copy(countb[:], count[:]).then_inc(S["countb_set"], 1)
                dve.wait_ge(S["base_set"], at.count(nbatch))
                TT(out=slotf[:], in0=base[:], in1=place[:], op=ALU.add).then_inc(S["part_set"], 1)
                dve.wait_ge(S["over_set"], at.count(nbatch))
                dve.wait_ge(S["part_set"], at.count(nbatch))
                TT(out=slot[k][:], in0=slotf[:], in1=over[:], op=ALU.add).then_inc(S["slot_ready"], 1)
                dve.wait_ge(S["gates_done"], at.count(nbatch))
                v.tensor_reduce(gsum[:], gates[:], AX.X, ALU.add).then_inc(S["gsum_set"], 1)
                dve.wait_ge(S["gsum_set"], at.count(nbatch))
                v.reciprocal(row[k][:, :, D + 2], gsum[:]).then_inc(S["gate_done"], 1)

            ATTENTION.run(dve, step)

        @block.tensor
        def _(pe):
            mm = nc.tensor.matmul

            def turn_bank(at, group, t0, per):
                n = TURN_NO[group]
                before = TURNS[n - 2]

                def shifted(table):
                    def f(t):
                        kind, of, *rest = group
                        return table(TURNS[TURN_NO[(kind, of + (t - t0) // per, *rest)] - 2])
                    return f
                if before[0] in SPLIT_KINDS:
                    pe.wait_ge(S["turn_low"], at.count(shifted(lambda g: SPLITS[g] + 1)))
                else:
                    pe.wait_ge(S["turn_evac"], at.count(shifted(lambda g: TURN_NO[g] + 1)))
                return turn[n % 2]

            def small_free(at, group, t0, per=1):
                before = SMALLS[SMALL_NO[group] - 1]

                def prior(t):
                    g = SMALLS[nth(SMALL_NO, group, t0, per)(t) - 2]
                    assert g[0] == before[0]
                    return g[1] + 1 if g[0] in READ_BY_ACT else SMALL_READ[g] + 1
                pe.wait_ge(S["logits_read" if before[0] in READ_BY_ACT else "small_read"], at.count(prior))

            def three(out, w_hi, w_lo, m_hi, m_lo, first, last):
                mm(out, w_hi, m_hi, start=first, stop=False)
                mm(out, w_hi, m_lo, start=False, stop=False)
                return mm(out, w_lo, m_hi, start=False, stop=last)

            pe.wait_ge(S["consts"], 14)
            pe.wait_ge(S["wqk_in"], 64)
            for n, w in enumerate((wq, wk)):
                for k in range(KT):
                    for m in range(KT):
                        last = nc.tensor.transpose(turn[n][:, k * D + m * P:k * D + m * P + P],
                                                   w[:, m, k * P:k * P + P], ident[:])
                last.then_inc(S["turn_full"], 1)
            pe.wait_ge(S["turn_evac"], 2)
            for m in range(KT):
                for k in range(KT):
                    last = mm(turn[0][:, m * D:m * D + D], wq_t[:, k, m * P:m * P + P], wk_t[:, k, :],
                              start=(k == 0), stop=(k == KT - 1))
            last.then_inc(S["turn_full"], 1)
            pe.wait_ge(S["setup_done"], 1)
            for w, vec, at0 in ((wk_t, bq, 0), (wq_t, bk, KT)):
                for m in range(KT):
                    for k in range(KT):
                        mm(small[:, at0 + m:at0 + m + 1], w[:, k, m * P:m * P + P], vec[:, k:k + 1],
                           start=(k == 0), stop=(k == KT - 1))
            for k in range(KT):
                last = mm(small[:, 2 * KT:2 * KT + 1], bqw[:, k, :], bk[:, k:k + 1],
                          start=(k == 0), stop=(k == KT - 1))
            last.then_inc(S["small_full"], 1)

            def score_chunk(at, c):
                t, b, r = at.t, at.batch, at.quarter
                par = b % 2
                if c == 0:
                    if tile_ok(t - 1):
                        pe.wait_ge(S["max_raw"], at.count(lambda t: t))
                    if r == 0:
                        pe.wait_ge(S["turn_low"], at.count(nth(SPLITS, ("qk", b, 1), t, QT)))
                if r == 0 and c == NC - 1:
                    pe.wait_ge(S["turn_low"], at.count(nth(SPLITS, ("ctx", b, 2 * c + 1), t, QT)))
                sl = slice(c * CW, c * CW + CW)
                q = slice(r * P, r * P + P)
                for k in range(KT):
                    last = three(scores[:, c, 0:CW], qkT_hi[par][:, k, q], qkT_lo[par][:, k, q],
                                 ctxT_hi[par][:, k, sl], ctxT_lo[par][:, k, sl], k == 0, k == KT - 1)
                if c == NC - 1:
                    last.then_inc(S["scores_full"], 1)

            def probs_turn(at, c):
                t = at.t
                if c == 0:
                    pe.wait_ge(S["exp_done"], at.count(lambda t: t))
                bank = turn_bank(at, ("probs", t - 1, c), t, 1)
                for j in range(4 * c, min(4 * c + 4, JT)):
                    n = P if j < JF else JR
                    o = (j - 4 * c) * P
                    last = nc.tensor.transpose(bank[0:n, o:o + P], probs[:, j * P:j * P + n], ident[:])
                last.then_inc(S["turn_full"], 1)

            def attend(at, j0, j1):
                t = at.t
                par = (t - 1) // QT % 2
                if j0 == 0:
                    if tile_ok(t - 2):
                        pe.wait_ge(S["attn_ready"], at.count(lambda t: t - 1))
                    if (t - 1) % QT == 0:
                        pe.wait_ge(S["ctx_lo_done"], at.count(lambda t: (t - 1) + QT))
                for j in range(j0, j1):
                    n = P if j < JF else JR
                    if j % 4 == 0:
                        pe.wait_ge(S["turn_low"], at.count(nth(SPLITS, ("probs", t - 1, j // 4), t)))
                    last = three(outp[:, 0:D], probsT_hi[0:n, j, :], probsT_lo[0:n, j, :],
                                 ctx_hi[par][0:n, j, :], ctx_lo[par][0:n, j, :], j == 0, j == JT - 1)
                if j1 == JT:
                    last.then_inc(S["out_full"], 1)

            def ctx_turn(at, i):
                bank = turn_bank(at, ("ctx", at.batch + 1, i), at.t, QT)
                k, (j0, j1) = i % 2, PIECES[i // 2]
                for j in range(j0, j1):
                    n = P if j < JF else JR
                    o = (j - j0) * P
                    last = nc.tensor.transpose(bank[:, o:o + n], ctx_in[0:n, j, k * P:k * P + P], ident[0:n, 0:n])
                last.then_inc(S["turn_full"], 1)

            def step(at):
                t, b, r = at.t, at.batch, at.quarter
                for c in range(NC):
                    if tile_ok(t):
                        score_chunk(at, c)
                    if tile_ok(t - 1):
                        probs_turn(at, c)
                if tile_ok(t - 1):
                    attend(at, 0, 2)
                if batch_ok(b + 1):
                    piece_in(at, pe)
                    ctx_turn(at, 2 * r)
                if tile_ok(t - 1):
                    attend(at, 2, 4)
                if batch_ok(b - 1) and r == 3:
                    pe.wait_ge(S["onehot_done"], at.count(lambda t: t // QT))
                    if b - 1 > 0:
                        pe.wait_ge(S["countb_set"], at.count(lambda t: t // QT - 1))
                    small_free(at, ("places", b - 1), t, QT)
                    flat = lambda a: a.rearrange("p i e -> p (i e)")
                    region = small[:, 32:32 + QT * EXPERTS]
                    mm(region, tri[:], flat(onehot[:]), start=True, stop=False)
                    for back in range(1, QT):
                        mm(region[:, back * EXPERTS:], ones[:], flat(onehot[:, 0:QT - back, :]),
                           start=False, stop=False)
                    mm(region, ones[:], countb[:].unsqueeze(1).broadcast_to([P, QT, EXPERTS]), start=False, stop=True) \
                        .then_inc(S["small_full"], 1)
                if tile_ok(t - 2):
                    pe.wait_ge(S["attn_ready"], at.count(lambda t: t - 1))
                    bank = turn_bank(at, ("attn", t - 2, 0), t, 1)
                    for k in range(KT):
                        last = nc.tensor.transpose(bank[:, k * P:k * P + P], attn[:, k * P:k * P + P], ident[:])
                    last.then_inc(S["turn_full"], 1)
                if tile_ok(t - 1):
                    attend(at, 4, 6)
                if tile_ok(t - 1):
                    attend(at, 6, 8)
                if tile_ok(t - 2):
                    pe.wait_ge(S["turn_evac"], at.count(nth(TURN_NO, ("attn", t - 2, 0), t)))
                    small_free(at, ("value", t - 2), t)
                    for k in range(KT):
                        last = mm(small[:, D:2 * D], attnT[:, k, :], wv[:, k, :], start=(k == 0), stop=(k == KT - 1))
                    last.then_inc(S["small_full"], 1)
                if tile_ok(t - 3):
                    pe.wait_ge(S["xn2_done"], at.count(lambda t: t - 2))
                    bank = turn_bank(at, ("xn2", t - 3, 0), t, 1)
                    for k in range(KT):
                        last = nc.tensor.transpose(bank[:, k * P:k * P + P], xn2[:, k * P:k * P + P], ident[:])
                    last.then_inc(S["turn_full"], 1)
                if tile_ok(t - 1):
                    attend(at, 8, 10)
                if batch_ok(b + 1):
                    ctx_turn(at, 2 * r + 1)
                if tile_ok(t - 1):
                    attend(at, 10, JT)
                if tile_ok(t - 3):
                    pe.wait_ge(S["turn_evac"], at.count(nth(TURN_NO, ("xn2", t - 3, 0), t)))
                    small_free(at, ("logits", t - 3), t)
                    for k in range(KT):
                        last = mm(small[:, 0:EXPERTS], xn2T[:, k, :], wg[:, k, :], start=(k == 0), stop=(k == KT - 1))
                    last.then_inc(S["small_full"], 1)
                if batch_ok(b + 1):
                    if r == 1:
                        pe.wait_ge(S["xnorm_done"], at.count(lambda t: t // QT + 2))
                        for k in range(KT):
                            bank = turn_bank(at, ("xn", b + 1, k), t, QT)
                            for i in range(QT):
                                last = nc.tensor.transpose(bank[:, i * P:i * P + P], xb[:, i, k * P:k * P + P],
                                                           ident[:])
                            last.then_inc(S["turn_full"], 1)
                    if r == 2:
                        pe.wait_ge(S["turn_evac"], at.count(nth(TURN_NO, ("xn", b + 1, 1), t, QT)))
                        for m in range(KT):
                            bank = turn_bank(at, ("qk", b + 1, m), t, QT)
                            for k in range(KT):
                                last = mm(bank[:], mqk[:, k, m * P:m * P + P], xnT[:, k, :],
                                          start=(k == 0), stop=(k == KT - 1))
                            last.then_inc(S["turn_full"], 1)
                        small_free(at, ("keybias", b + 1), t, QT)
                        for i in range(QT):
                            for k in range(KT):
                                last = mm(small[:, 16 + i:17 + i], xnT[:, k, i * P:i * P + P], kbias[:, k:k + 1],
                                          start=(k == 0), stop=(k == KT - 1))
                        last.then_inc(S["small_full"], 1)
            pe.wait_ge(S["weights_in"], 32)
            ATTENTION.run(pe, step)


LAG = 2
HB = HID // P
SG = 512
GROUPS = CAP // SG
ST = SG // P
UNITS = EXPERTS * GROUPS * HB
PER = GROUPS * HB
EXPERT_PIPE = Pipeline("experts", -HB, PER, PER, EXPERTS - 2, UNITS + LAG + 1)


def experts(nc, dram, keep):
    with ExitStack() as ctx:
        def sb(name, shape, dt=F32):
            return ctx.enter_context(nc.sbuf_tensor(name, shape, dt))

        def sem(name):
            return ctx.enter_context(nc.semaphore(name))

        ident = keep["ident"]
        w1_in = sb("w1_in", [P, KT, HID])
        w2_in = sb("w2_in", [P, HB, D])
        w1_hi = sb("w1_hi", [P, KT, HID], F32R)
        w1_lo = sb("w1_lo", [P, KT, HID], F32R)
        w2_hi = sb("w2_hi", [P, HB, D], F32R)
        w2_lo = sb("w2_lo", [P, HB, D], F32R)
        b1_in = sb("b1_in", [EXPERTS * HB, P])
        b1_t = sb("b1_t", [P, EXPERTS * HB])
        b2_all = sb("b2_all", [P, EXPERTS, D])
        rows = [sb(f"rows{n}", [P, ST, ROW]) for n in range(2)]
        token_of = [sb(f"token_of{n}", [P, ST], U32) for n in range(2)]
        xn = sb("xn", [P, ST, D])
        xT_hi = [sb(f"xT_hi{n}", [P, KT, SG], F32R) for n in range(2)]
        xT_lo = [sb(f"xT_lo{n}", [P, KT, SG], F32R) for n in range(2)]
        hid = [sb(f"hid{n}", [P, SG]) for n in range(4)]
        hid_hi = [sb(f"hid_hi{n}", [P, SG], F32R) for n in range(4)]
        hid_lo = [sb(f"hid_lo{n}", [P, SG], F32R) for n in range(4)]
        base = [sb(f"base{n}", [P, ST, D]) for n in range(2)]
        gate_of = [sb(f"gate_of{n}", [P, ST]) for n in range(2)]
        result = [sb(f"result{n}", [P, ST, D]) for n in range(2)]

        hps = [ctx.enter_context(nc.psum_tensor(f"hps{n}", [P, SG], F32)) for n in range(2)]
        xps = [ctx.enter_context(nc.psum_tensor(f"xps{n}", [P, SG], F32)) for n in range(KT)]
        acc = [ctx.enter_context(nc.psum_tensor(f"acc{n}", [P, SG], F32)) for n in range(ST)]

        S = {}
        for name in ("w1_arrived w2_arrived b1_in b2_in b1_full b1_set rows_in0 rows_in1 xn_set token_of_set "
                     "w1_hi_set w1_lo_set w2_hi_set w2_lo_set x_turned x_hi x_lo hid_full hid_set hid_hi_set hid_lo_set "
                     "hid_used base_set result_set out0 out1").split():
            S[name] = sem("e_" + name)
        MET = (S["b1_in"], 16)
        rows_in = [S["rows_in0"], S["rows_in1"]]
        out_done = [S["out0"], S["out1"]]
        slots_v = dram["slots"].rearrange("(g p n) w -> g p n w", g=EXPERTS * GROUPS, p=P)
        w1_v = dram["w1"].rearrange("e (k p) h -> e p k h", p=P)
        w2_v = dram["w2"].rearrange("e (h p) n -> e p h n", p=P)
        out_rows = dram["out"].rearrange("b q d -> (b q) d")

        unit_ok = lambda n: 0 <= n < UNITS
        group_ok = lambda g: 0 <= g < EXPERTS * GROUPS
        refresh_ok = lambda n: n >= -HB and n // HB % 2 == 1 and 0 <= n // PER + 1 < EXPERTS
        refreshed = lambda n: (n // PER + 1) * HB + n % HB + 1

        block = ctx.enter_context(nc.Block())

        @block.sync
        def _(sp):
            def load(at, dst, src, arrived, used, e_of):
                if e_of(at.t) > 0:
                    count, = at.ahead(sp, lambda n: HB * e_of(n))
                    sp.wait_ge(*MET)
                    sp.wait_ge(used, count)
                sp.dma_start(dst[:], src[at.value(e_of)]).then_inc(arrived, 16)

            def load_rows(at, g_of):
                g = g_of(at.t)
                if g >= 2:
                    count, = at.ahead(sp, lambda n: ST * (g_of(n) - 1))
                    sp.wait_ge(*MET)
                    sp.wait_ge(S["base_set"], count)
                sp.dma_start(rows[g % 2][:], slots_v[at.value(g_of)]).then_inc(rows_in[g % 2], 16)

            def step(at):
                n = at.t
                g, hb = n // HB, n % HB
                if n == -HB:
                    load_rows(at, lambda n: 0)
                    sp.dma_start(b1_in[:], dram["b1"].rearrange("e (h p) -> (e h) p", p=P)).then_inc(S["b1_in"], 16)
                    load(at, w1_in, w1_v, S["w1_arrived"], S["w1_lo_set"], lambda n: 0)
                    load(at, w2_in, w2_v, S["w2_arrived"], S["w2_lo_set"], lambda n: 0)
                    sp.dma_start(b2_all[:], dram["b2"].partition_broadcast(P)).then_inc(S["b2_in"], 16)
                new_expert = n >= 0 and n // PER + 1 < EXPERTS
                if new_expert and n % PER == 0:
                    load(at, w1_in, w1_v, S["w1_arrived"], S["w1_lo_set"], lambda n: n // PER + 1)
                if hb == 2 and group_ok(g + 2):
                    load_rows(at, lambda n: n // HB + 2)
                if new_expert and n % PER == LAG:
                    load(at, w2_in, w2_v, S["w2_arrived"], S["w2_lo_set"], lambda n: n // PER + 1)

            EXPERT_PIPE.run(sp, step)
            for n in range(2):
                sp.wait_ge(out_done[n], 16 * ST * EXPERTS * GROUPS // 2)

        @block.gpsimd
        def _(pool):
            g_ = nc.gpsimd

            def step(at):
                n = at.t
                grp, hb = n // HB, n % HB
                if refresh_ok(n):
                    blk = slice(hb * P, hb * P + P)
                    pool.wait_ge(S["w1_hi_set"], at.count(refreshed))
                    g_.tensor_tensor(out=w1_lo[:, :, blk], in0=w1_in[:, :, blk], in1=w1_hi[:, :, blk].bitcast(F32),
                                     op=ALU.subtract).then_inc(S["w1_lo_set"], 1)
                if refresh_ok(n - LAG):
                    b2 = (n - LAG) % HB
                    pool.wait_ge(S["w2_hi_set"], at.count(lambda n: refreshed(n - LAG)))
                    g_.tensor_tensor(out=w2_lo[:, b2, :], in0=w2_in[:, b2, :], in1=w2_hi[:, b2, :].bitcast(F32),
                                     op=ALU.subtract).then_inc(S["w2_lo_set"], 1)
                if group_ok(grp - 1) and hb in (LAG, LAG + 1):
                    k = (grp - 1) % 2
                    for s in ((0, 1), (2, 3))[hb - LAG]:
                        count, = at.ahead(pool, lambda n: ST * (n // HB - 1) + s + 1)
                        pool.wait_ge(*MET)
                        pool.wait_ge(S["result_set"], count)
                        g_.indirect_dma_start(
                            out=out_rows, out_offset=bass.IndirectOffsetOnAxis(ap=token_of[k][:, s:s + 1], axis=0),
                            in_=result[k][:, s, :], in_offset=None, bounds_check=TOKENS - 1, oob_is_err=False) \
                            .then_inc(out_done[k], 16)

            EXPERT_PIPE.run(pool, step)

        @block.scalar
        def _(act):
            a = nc.scalar

            def step(at):
                n = at.t
                grp, hb = n // HB, n % HB
                if group_ok(grp + 1) and hb >= HB - KT:
                    k = hb - (HB - KT)
                    act.wait_ge(S["x_turned"], at.count(lambda n: KT * (n // HB + 1) + k + 1))
                    a.activation(xT_hi[(grp + 1) % 2][:, k, :], xps[k][:], ACT.Copy).then_inc(S["x_hi"], 1)
                if unit_ok(n):
                    act.wait_ge(S["hid_set"], at.count(lambda n: n + 1))
                    a.activation(hid_hi[n % 4][:], hid[n % 4][:], ACT.Copy).then_inc(S["hid_hi_set"], 1)
                if refresh_ok(n):
                    blk = slice(hb * P, hb * P + P)
                    act.wait_ge(S["w1_arrived"], at.count(lambda n: 16 * (n // PER + 2)))
                    if n >= 0:
                        act.wait_ge(S["hid_full"], at.count(lambda n: n + 1))
                    a.activation(w1_hi[:, :, blk], w1_in[:, :, blk], ACT.Copy).then_inc(S["w1_hi_set"], 1)
                if refresh_ok(n - LAG):
                    b2 = (n - LAG) % HB
                    act.wait_ge(S["w2_arrived"], at.count(lambda n: 16 * ((n - LAG) // PER + 2)))
                    if n - LAG >= 0:
                        act.wait_ge(S["hid_used"], at.count(lambda n: n - LAG + 1))
                    a.activation(w2_hi[:, b2, :], w2_in[:, b2, :], ACT.Copy).then_inc(S["w2_hi_set"], 1)

            EXPERT_PIPE.run(act, step)

        @block.vector
        def _(dve):
            v = nc.vector
            TT, TS, STT = v.tensor_tensor, v.tensor_scalar, v.scalar_tensor_tensor
            dve.wait_ge(S["b1_full"], 1)
            v.tensor_copy(b1_t[:], xps[0][:, 0:EXPERTS * HB]).then_inc(S["b1_set"], 1)
            dve.wait_ge(S["b1_set"], 1)

            def step(at):
                n = at.t
                grp, hb = n // HB, n % HB
                if group_ok(grp - 1) and hb == LAG:
                    k = (grp - 1) % 2
                    dve.wait_ge(S["token_of_set"], at.count(lambda n: 2 * (n // HB)))
                    dve.wait_ge(S["base_set"], at.count(lambda n: ST * (n // HB)))
                    dve.wait_ge(S["hid_used"], at.count(lambda n: n // HB * HB))
                    for s in range(ST):
                        STT(out=result[k][:, s, :], in0=acc[s][:, 0:D], scalar=gate_of[k][:, s:s + 1],
                            in1=base[k][:, s, :], op0=ALU.mult, op1=ALU.add).then_inc(S["result_set"], 1)
                if group_ok(grp + 1) and hb >= HB - KT:
                    k = hb - (HB - KT)
                    dve.wait_ge(S["x_hi"], at.count(lambda n: KT * (n // HB + 1) + k + 1))
                    TT(out=xT_lo[(grp + 1) % 2][:, k, :], in0=xps[k][:], in1=xT_hi[(grp + 1) % 2][:, k, :].bitcast(F32),
                       op=ALU.subtract).then_inc(S["x_lo"], 1)
                if unit_ok(n):
                    dve.wait_ge(S["hid_full"], at.count(lambda n: n + 1))
                    col = at.value(lambda n: n // PER * HB + n % HB)
                    if n >= 4:
                        dve.wait_ge(S["hid_used"], at.count(lambda n: n - 3))
                    TS(hid[n % 4][:], hps[n % 2][:], b1_t[:, bass.ds(col, 1)], 0.0, ALU.add, ALU.max) \
                        .then_inc(S["hid_set"], 1)
                if unit_ok(n - 1):
                    dve.wait_ge(S["hid_hi_set"], at.count(lambda n: n))
                    j = (n - 1) % 4
                    TT(out=hid_lo[j][:], in0=hid[j][:], in1=hid_hi[j][:].bitcast(F32), op=ALU.subtract) \
                        .then_inc(S["hid_lo_set"], 1)
                k = grp % 2
                if group_ok(grp) and hb < 2:
                    if n == 0:
                        dve.wait_ge(S["b2_in"], 16)
                    if hb == 0:
                        if grp >= 2:
                            dve.wait_ge(out_done[k], at.count(lambda n: 16 * ST * (n // HB // 2)))
                        v.tensor_copy(token_of[k][:], rows[k][:, :, D + 3]).then_inc(S["token_of_set"], 1)
                        v.tensor_copy(gate_of[k][:], rows[k][:, :, D + 2]).then_inc(S["token_of_set"], 1)
                    e = at.value(lambda n: n // PER)
                    for s in ((0, 1), (2, 3))[hb]:
                        STT(out=base[k][:, s, :], in0=b2_all[:, bass.ds(e, 1), :].rearrange("p o d -> p (o d)"),
                            scalar=rows[k][:, s, D + 2:D + 3], in1=rows[k][:, s, 0:D],
                            op0=ALU.mult, op1=ALU.add).then_inc(S["base_set"], 1)
                if group_ok(grp + 1) and hb == HB - KT - 3:
                    k = (grp + 1) % 2
                    dve.wait_ge(rows_in[k], at.count(lambda n: 16 * ((n // HB + 1) // 2 + 1)))
                    if grp >= 0:
                        dve.wait_ge(S["x_turned"], at.count(lambda n: KT * (n // HB + 1)))
                    for i in range(ST):
                        last = TS(xn[:, i, :], rows[k][:, i, 0:D], rows[k][:, i, D:D + 1],
                                  rows[k][:, i, D + 1:D + 2], ALU.subtract, ALU.mult)
                    last.then_inc(S["xn_set"], 1)

            EXPERT_PIPE.run(dve, step)

        @block.tensor
        def _(pe):
            mm = nc.tensor.matmul

            def three(out, w_hi, w_lo, m_hi, m_lo, first, last):
                mm(out, w_hi, m_hi, start=first, stop=False)
                mm(out, w_hi, m_lo, start=False, stop=False)
                return mm(out, w_lo, m_hi, start=False, stop=last)

            pe.wait_ge(S["b1_in"], 16)
            nc.tensor.transpose(xps[0][:, 0:EXPERTS * HB], b1_in[:], ident[0:EXPERTS * HB, 0:EXPERTS * HB]) \
                .then_inc(S["b1_full"], 1)
            pe.wait_ge(S["b1_set"], 1)

            def step(at):
                n = at.t
                grp, hb = n // HB, n % HB
                if unit_ok(n):
                    if hb == 0:
                        pe.wait_ge(S["x_lo"], at.count(lambda n: KT * (n // HB + 1)))
                    if grp % 2 == 0:
                        pe.wait_ge(S["w1_lo_set"], at.count(lambda n: n // PER * HB + n % HB + 1))
                    if n >= 2:
                        pe.wait_ge(S["hid_set"], at.count(lambda n: n - 1))
                    blk = slice(hb * P, hb * P + P)
                    for k in range(KT):
                        last = three(hps[n % 2][:], w1_hi[:, k, blk], w1_lo[:, k, blk],
                                     xT_hi[grp % 2][:, k, :], xT_lo[grp % 2][:, k, :], k == 0, k == KT - 1)
                    last.then_inc(S["hid_full"], 1)
                if group_ok(grp + 1) and HB - KT - 1 <= hb < HB - 1:
                    k = hb - (HB - KT - 1)
                    if k == 0:
                        pe.wait_ge(S["xn_set"], at.count(lambda n: n // HB + 2))
                        if grp >= 0:
                            pe.wait_ge(S["x_lo"], at.count(lambda n: KT * (n // HB + 1)))
                    for i in range(ST):
                        last = nc.tensor.transpose(xps[k][:, i * P:i * P + P], xn[:, i, k * P:k * P + P], ident[:])
                    last.then_inc(S["x_turned"], 1)
                u = n - LAG
                if unit_ok(u):
                    ub = u % HB
                    if u // HB % 2 == 0:
                        pe.wait_ge(S["w2_lo_set"], at.count(lambda n: (n - LAG) // PER * HB + (n - LAG) % HB + 1))
                    pe.wait_ge(S["hid_lo_set"], at.count(lambda n: n - LAG + 1))
                    for s in range(ST):
                        if ub == 0 and u >= HB:
                            pe.wait_ge(S["result_set"], at.count(lambda n: ST * ((n - LAG) // HB - 1) + s + 1))
                        q = slice(s * P, s * P + P)
                        last = three(acc[s][:, 0:D], hid_hi[u % 4][:, q], hid_lo[u % 4][:, q],
                                     w2_hi[:, ub, :], w2_lo[:, ub, :], ub == 0, ub == HB - 1)
                    last.then_inc(S["hid_used"], 1)

            EXPERT_PIPE.run(pe, step)


def build(nc, x, ctx_in, mask, wq, bq, wk, bk, wv, bv, gamma, beta, wg, w1, b1, w2, b2, out):
    dram = dict(x=x, ctx=ctx_in, mask=mask, wq=wq, bq=bq, wk=wk, bk=bk, wv=wv, bv=bv, gamma=gamma, beta=beta,
                wg=wg, w1=w1, b1=b1, w2=w2, b2=b2, out=out,
                slots=nc.dram_tensor("slots", [TOKENS, ROW], F32, kind="Internal").ap())
    with nc.sbuf_tensor("ident", [P, P], F32) as ident:
        keep = {"ident": ident}
        attention(nc, dram, keep)
        experts(nc, dram, keep)


_INS = ["x", "ctx_1024", "mask_BxSxS2_ik1", "L0_xattn_Wq", "L0_xattn_bq", "L0_xattn_Wk", "L0_xattn_bk",
        "L0_xattn_Wv", "L0_xattn_bv", "L0_xattn_ln_gamma", "L0_xattn_ln_beta", "L0_ffn_wg", "L0_ffn_w1",
        "L0_ffn_b1", "L0_ffn_w2", "L0_ffn_b2"]


def kernel(**inputs):
    import numpy as _np
    import concourse.bacc as _bacc
    from concourse.bass_utils import run_bass_kernel_spmd as _run

    nc = _bacc.Bacc("TRN2", target_bir_lowering=False, num_devices=1)
    arrays, args = {}, []
    for name in _INS:
        a = _np.ascontiguousarray(inputs[name])
        arrays[f"in_{name}"] = a
        args.append(nc.dram_tensor(f"in_{name}", a.shape, mybir.dt.from_np(a.dtype), kind="ExternalInput").ap())
    out = nc.dram_tensor("out", (NB, SQ, D), F32, kind="ExternalOutput").ap()
    build(nc, *args, out)
    r = _run(nc, [arrays], core_ids=[0])
    return r.results[0]["out"]
```

```python
from contextlib import ExitStack

import concourse.bass as bass
from concourse import mybir

ALU = mybir.AluOpType
ACT = mybir.ActivationFunctionType
AX = mybir.AxisListType
F32 = mybir.dt.float32
F32R = mybir.dt.float32r
BF16 = mybir.dt.bfloat16
I32 = mybir.dt.int32
U32 = mybir.dt.uint32

P = 128
NB, SQ, D = 16, 512, 256
SK = 1601
KT = D // P
QT = SQ // P
NT = NB * QT
JF = SK // P
JR = SK - JF * P
JT = JF + 1
PIECES = [(0, 4), (4, 7), (7, 10), (10, JT)]
CH = 512
NC = (SK + CH - 1) // CH
CW = 2 * ((SK + 2 * NC - 1) // (2 * NC))
SKP = NC * CW
EXPERTS, HID = 8, 1024
TOKENS = NB * SQ
CAP = TOKENS // EXPERTS
ROW = D + 4
SCALE = 1.0 / float(D) ** 0.5
EPS = 1e-5
MASKED = -1e30
NOWHERE = 65536.0
SCATTERED = [(0, 1), (2,), (3,), ()]
W1_STEP = NT - QT
FIRST_STEP, LAST_STEP = -QT, NT + QT


class Pipeline:

    def __init__(self, name, first, loop_from, period, loops, last):
        self.name = name
        self.first, self.loop_from, self.period, self.loops, self.last = first, loop_from, period, loops, last

    def run(self, eng, step):
        counts = [eng.alloc_register(f"{self.name}{n}") for n in range(3)]
        for t in range(self.first, self.loop_from):
            step(At(self, t))
        with eng.Fori(0, self.loops) as it:
            for u in range(self.period):
                step(At(self, self.loop_from + u, it, counts))
        for t in range(self.loop_from + self.loops * self.period, self.last + 1):
            step(At(self, t))


class At:

    def __init__(self, pipe, t, it=None, counts=()):
        self.pipe, self.t, self.it, self.counts = pipe, t, it, counts
        self.batch, self.quarter = t // QT, t % QT

    def value(self, f):
        v = f(self.t)
        if self.it is None:
            return v
        by = f(self.t + self.pipe.period) - v
        assert all(f(self.t + n * self.pipe.period) == v + n * by for n in range(self.pipe.loops))
        return v + self.it * by

    def count(self, f):
        v = self.value(f)
        assert not isinstance(v, int) or v > 0, "a wait for nothing"
        return v

    def ahead(self, eng, *fs):
        counts = [self.count(f) for f in fs]
        for n, v in enumerate(counts):
            if not isinstance(v, int):
                eng.reg_mov(self.counts[n], v)
                counts[n] = self.counts[n]
        return counts


ATTENTION = Pipeline("attention", FIRST_STEP, 2 * QT, 2 * QT, NB // 2 - 2, LAST_STEP)


def tile_ok(t):
    return 0 <= t < NT


def batch_ok(b):
    return 0 <= b < NB


def turn_groups(t):
    out = []
    b, r = t // QT + 1, t % QT
    if tile_ok(t - 2):
        out.append(("attn", t - 2, 0))
    if tile_ok(t - 1):
        out += [("probs", t - 1, c) for c in range(NC)]
    if batch_ok(b):
        out.append(("ctx", b, 2 * r))
    if tile_ok(t - 3):
        out.append(("xn2", t - 3, 0))
    if batch_ok(b):
        out.append(("ctx", b, 2 * r + 1))
        if r == 1:
            out += [("xn", b, 0), ("xn", b, 1)]
        if r == 2:
            out += [("qk", b, 0), ("qk", b, 1)]
    return out


def small_groups(t):
    out = []
    if tile_ok(t - 2):
        out.append(("value", t - 2))
    if batch_ok(t // QT - 1) and t % QT == QT - 1:
        out.append(("places", t // QT - 1))
    if tile_ok(t - 3):
        out.append(("logits", t - 3))
    return out


SETUP_TURNS = [("setup", 0, 0), ("setup", 0, 1), ("product", 0, 0)]
SPLIT_KINDS = ("product", "probs", "ctx", "attn", "xn", "qk")
TURNS = SETUP_TURNS + [g for t in range(FIRST_STEP, LAST_STEP + 1) for g in turn_groups(t)]
TURN_NO = {g: n for n, g in enumerate(TURNS)}
SPLITS = {g: n for n, g in enumerate(g for g in TURNS if g[0] in SPLIT_KINDS)}
SETUP_SMALL = [("setup", 0)]
READ_BY_ACT = ("logits",)
SMALLS = SETUP_SMALL + [g for t in range(FIRST_STEP, LAST_STEP + 1) for g in small_groups(t)]
SMALL_NO = {g: n for n, g in enumerate(SMALLS)}
SMALL_READ = {g: n for n, g in enumerate(g for g in SMALLS if g[0] not in READ_BY_ACT)}


def nth(table, group, t0, per=1):
    kind, of, *rest = group

    def f(t):
        shift = (t - t0) // per
        return table[(kind, of + shift, *rest)] + 1
    return f


def attention(nc, dram, keep):
    with ExitStack() as ctx:
        def sb(name, shape, dt=F32):
            return ctx.enter_context(nc.sbuf_tensor(name, shape, dt))

        def sem(name):
            return ctx.enter_context(nc.semaphore(name))

        ident = keep["ident"]
        tri = sb("tri", [P, P], BF16)
        ones = sb("ones", [P, P], BF16)
        halves = sb("halves", [P, QT])
        rank = sb("rank", [P, QT, EXPERTS])
        token = sb("token", [P, QT])
        wv_hi = sb("wv_hi", [P, KT, D], F32R)
        wv_lo = sb("wv_lo", [P, KT, D], F32R)
        wg = sb("wg", [P, KT, EXPERTS])
        bq = sb("bq", [P, KT])
        bk = sb("bk", [P, KT])
        mqk_hi = sb("mqk_hi", [P, KT, D], F32R)
        mqk_lo = sb("mqk_lo", [P, KT, D], F32R)
        qbias = sb("qbias", [P, KT])
        kbias = sb("kbias", [P, D])
        bqk = sb("bqk", [P, 1])
        kb_sum = sb("kb_sum", [P, QT])
        bv_all = sb("bv_all", [P, D])
        gamma_all = sb("gamma_all", [P, D])
        beta_all = sb("beta_all", [P, D])

        ctx_in, xb = keep["room"][:, 0:JT, :], keep["room"][:, JT:, :]
        ctx_hi = [keep["ctx_hi0"], sb("ctx_hi1", [P, JT, D], F32R)]
        ctx_lo = [keep["ctx_lo0"], sb("ctx_lo1", [P, JT, D], F32R)]
        ctxT_hi = [keep["ctxT_hi0"], sb("ctxT_hi1", [P, KT, SKP], F32R)]
        ctxT_lo = [keep["ctxT_lo0"], sb("ctxT_lo1", [P, KT, SKP], F32R)]
        xnT_hi = sb("xnT_hi", [P, KT, SQ], F32R)
        xnT_lo = sb("xnT_lo", [P, KT, SQ], F32R)
        qkT_hi = [sb(f"qkT_hi{n}", [P, KT, SQ], F32R) for n in range(2)]
        qkT_lo = [sb(f"qkT_lo{n}", [P, KT, SQ], F32R) for n in range(2)]
        w1_in, w2_in, w1_hi, w1_lo, w2_hi, w2_lo = weight_places(keep)
        kb16 = [sb(f"kb16_{n}", [P, QT]) for n in range(2)]
        mask_in = sb("mask_in", [P, SK], I32)
        mask_add = sb("mask_add", [P, SKP], BF16)
        probs = sb("probs", [P, SKP])
        probsT_hi = sb("probsT_hi", [P, JT, P], F32R)
        probsT_lo = sb("probsT_lo", [P, JT, P], F32R)
        wq, wk, wv = (probs[:, n * KT * D:(n + 1) * KT * D].rearrange("p (k n) -> p k n", k=KT) for n in range(3))
        wq_t, wk_t = (mask_in[:, n * KT * D:(n + 1) * KT * D].bitcast(F32).rearrange("p (k n) -> p k n", k=KT)
                      for n in range(2))
        rowmax = sb("rowmax", [P, 2])
        fullmax = sb("fullmax", [P, 2])
        negmax = sb("negmax", [P, 2])
        rowsum = sb("rowsum", [P, 2])
        rsum = sb("rsum", [P, 2])
        attn = sb("attn", [P, D])
        attnT_hi = sb("attnT_hi", [P, KT, P], F32R)
        attnT_lo = sb("attnT_lo", [P, KT, P], F32R)
        xres = [sb(f"xres{n}", [P, D]) for n in range(4)]
        value = sb("value", [P, D])
        bkw = value[:].rearrange("p (k q) -> p k q", k=KT)
        scaled = sb("scaled", [P, D])
        bn1 = sb("bn1", [P, 6])
        mv1 = sb("mv1", [P, 2])
        ve1 = sb("ve1", [P, 1])
        rstd1 = sb("rstd1", [P, 1])
        bn2 = sb("bn2", [P, 6])
        mv2 = sb("mv2", [P, 2])
        ve2 = sb("ve2", [P, 1])
        bnx = sb("bnx", [P, QT, 6])
        mvx = sb("mvx", [P, QT, 2])
        vex = sb("vex", [P, QT])
        rstdx = sb("rstdx", [P, QT])
        row = [sb(f"row{n}", [P, QT, ROW]) for n in range(2)]
        xn2 = sb("xn2", [P, D])
        xn2T = sb("xn2T", [P, KT, P])
        logits = sb("logits", [P, QT, EXPERTS])
        best = sb("best", [P, QT])
        below = sb("below", [P, QT, EXPERTS])
        gates = sb("gates", [P, QT, EXPERTS])
        gsum = sb("gsum", [P, QT])
        tied = sb("tied", [P, QT, EXPERTS])
        pick = sb("pick", [P, QT])
        onehot = sb("onehot", [P, QT, EXPERTS], BF16)
        added = sb("added", [P, EXPERTS])
        count = sb("count", [P, EXPERTS])
        countb = sb("countb", [P, EXPERTS], BF16)
        placed = sb("placed", [P, QT, EXPERTS])
        place = sb("place", [P, QT])
        base = sb("base", [P, QT])
        over = sb("over", [P, QT])
        slotf = sb("slotf", [P, QT])
        slot = [sb(f"slot{n}", [P, QT], U32) for n in range(2)]
        blank = sb("blank", [P, ROW])

        scores = ctx.enter_context(nc.psum_tensor("scores", [P, NC, CH], F32))
        turn = [ctx.enter_context(nc.psum_tensor(f"turn{n}", [P, CH], F32)) for n in range(2)]
        outp = ctx.enter_context(nc.psum_tensor("outp", [P, CH], F32))
        small = ctx.enter_context(nc.psum_tensor("small", [P, CH], F32))

        S = {}
        for name in ("consts wqk_in weights_in wv_hi_set wv_lo_set bcast_in blank_set blanks_out "
                     "turn_full turn_evac turn_low small_full small_read logits_read setup_done "
                     "x_in ctx_in0 ctx_in1 ctx_in2 ctx_in3 mask_in xres_in0 xres_in1 xres_in2 xres_in3 "
                     "scores_full mask_ready max_raw max_full max_neg exp_done sum_inv "
                     "out_full attn_ready ctx_hi_done ctx_lo_done xres_beta "
                     "bn1_set mv1_set var1 rstd1 scaled_set x1_done bn2_set mv2_set var2 rstd2 xn2_done "
                     "bnx_set mvx_set varx rstdx xnorm_done kb_prod_set kb_sum_set kb_set "
                     "best_set below_set gates_done tied_set pick_set onehot_done added_set count_set "
                     "countb_set place_set base_set over_set part_set slot_ready gsum_set gate_done "
                     "token_set token_next store0 store1 scatter0 scatter1").split():
            S[name] = sem(name)
        MET = (S["consts"], 13)
        store_done = [S["store0"], S["store1"]]
        scatter_done = [S["scatter0"], S["scatter1"]]
        ctx_in_done = [S[f"ctx_in{n}"] for n in range(QT)]
        xres_in = [S[f"xres_in{n}"] for n in range(4)]

        x_v = dram["x"].rearrange("b (i p) d -> b p i d", p=P)
        ctx_v = dram["ctx"]
        mask_v = dram["mask"].rearrange("b (i p) k -> (b i) p k", p=P)
        x_t = dram["x"].rearrange("b (i p) d -> (b i) p d", p=P)
        out_t = dram["out"].rearrange("b (i p) d -> (b i) p d", p=P)
        slots = dram["slots"]
        w1_v = dram["w1"].rearrange("e (k p) h -> e p k h", p=P)
        w2_v = dram["w2"].rearrange("e (h p) n -> e p h n", p=P)
        W = keep["weights_sems"]

        def piece_keys(q):
            j0, j1 = PIECES[q]
            return slice(j0 * P, min(j1 * P, SK))

        def piece_in(at, eng):
            loads = 2 if at.quarter == QT - 1 else 1
            eng.wait_ge(ctx_in_done[at.quarter], at.count(lambda t: 16 * loads * (t // QT + 2)))

        block = ctx.enter_context(nc.Block())

        @block.sync
        def _(sp):
            def load_piece(nb, q):
                j0, j1 = PIECES[q]
                full = min(j1, JF)
                sp.dma_start(ctx_in[:, j0:full, :], ctx_v[nb, j0 * P:full * P, :].rearrange("(j p) d -> p j d", p=P)) \
                    .then_inc(ctx_in_done[q], 16)
                if j1 == JT:
                    sp.dma_start(ctx_in[0:JR, JF, :], ctx_v[nb, JF * P:SK, :]).then_inc(ctx_in_done[q], 16)

            for dst, src in ((wq, "wq"), (wk, "wk")):
                sp.dma_start(dst[:], dram[src].rearrange("(k p) n -> p k n", p=P)).then_inc(S["wqk_in"], 16)
            for dst, src in ((bq, "bq"), (bk, "bk")):
                sp.dma_start(dst[:], dram[src].rearrange("(k p) -> p k", p=P), allow_slow_non_contiguous=True) \
                    .then_inc(S["wqk_in"], 16)
            load_piece(0, 0)
            sp.dma_start(xb[:], x_v[0]).then_inc(S["x_in"], 16)
            for dst, src in ((wv, "wv"), (wg, "wg")):
                sp.dma_start(dst[:], dram[src].rearrange("(k p) n -> p k n", p=P)).then_inc(S["weights_in"], 16)
            for dst, src in ((bv_all, "bv"), (gamma_all, "gamma"), (beta_all, "beta")):
                sp.dma_start(dst[:], dram[src].partition_broadcast(P)).then_inc(S["bcast_in"], 16)
            for q in range(1, QT):
                load_piece(0, q)

            def step(at):
                t, b, r = at.t, at.batch, at.quarter
                if tile_ok(t - 3):
                    x1_done, = at.ahead(sp, lambda t: t - 2)
                    sp.wait_ge(*MET)
                    sp.wait_ge(S["x1_done"], x1_done)
                    k = (t - 3) // QT % 2
                    sp.dma_start(out_t[at.value(lambda t: t - 3)], row[k][:, (t - 3) % QT, 0:D]) \
                        .then_inc(store_done[k], 16)
                if tile_ok(t + 1):
                    if t == -1:
                        sp.wait_ge(S["small_full"], 1)
                    if tile_ok(t):
                        mask_ready, = at.ahead(sp, lambda t: t + 1)
                        sp.wait_ge(*MET)
                        sp.wait_ge(S["mask_ready"], mask_ready)
                    sp.dma_start(mask_in[:], mask_v[at.value(lambda t: t + 1)]).then_inc(S["mask_in"], 16)
                if tile_ok(t):
                    if tile_ok(t - 4):
                        x1_done, = at.ahead(sp, lambda t: t - 3)
                        sp.wait_ge(*MET)
                        sp.wait_ge(S["x1_done"], x1_done)
                    sp.dma_start(xres[t % 4][:], x_t[at.value(lambda t: t)]).then_inc(xres_in[t % 4], 16)
                nb, q = (t - 2) // QT + 2, (t - 2) % QT
                if 0 < nb < NB:
                    turn_full, ctx_hi_done, ctx_lo_done = at.ahead(
                        sp, nth(TURN_NO, ("ctx", nb - 1, 2 * q + 1), t, QT),
                        lambda t: t + QT - 1, lambda t: t + QT - 1)
                    sp.wait_ge(*MET)
                    sp.wait_ge(S["turn_full"], turn_full)
                    sp.wait_ge(S["ctx_hi_done"], ctx_hi_done)
                    sp.wait_ge(S["ctx_lo_done"], ctx_lo_done)
                    load_piece(at.value(lambda t: (t - 2) // QT + 2), q)
                if 0 < b + 2 < NB and r == 3:
                    kb_sum_set, = at.ahead(sp, lambda t: QT * (t // QT + 2))
                    sp.wait_ge(*MET)
                    sp.wait_ge(S["kb_sum_set"], kb_sum_set)
                    sp.dma_start(xb[:], x_v[at.value(lambda t: t // QT + 2)]).then_inc(S["x_in"], 16)
                if t == W1_STEP:
                    sp.wait_ge(S["turn_full"], TURN_NO[("ctx", NB - 1, 2 * QT - 1)] + 1)
                    sp.wait_ge(S["ctx_hi_done"], NT)
                    sp.wait_ge(S["ctx_lo_done"], NT)
                    sp.dma_start(w1_in, w1_v[0]).then_inc(W["w1_arrived"], 16)
                if t == W1_STEP + 1:
                    sp.wait_ge(S["turn_full"], TURN_NO[("qk", NB - 1, KT - 1)] + 1)
                    sp.wait_ge(S["kb_sum_set"], QT * NB)
                    sp.dma_start(w2_in, w2_v[0]).then_inc(W["w2_arrived"], 16)
                if 0 <= t < 2 * QT:
                    if t == 0:
                        sp.wait_ge(S["blank_set"], 3)
                    sp.dma_start(slots.rearrange("(c p n) w -> c p n w", c=2 * QT, p=P)[t],
                                 blank[:].unsqueeze(1).broadcast_to([P, TOKENS // P // (2 * QT), ROW])) \
                        .then_inc(S["blanks_out"], 16)

            ATTENTION.run(sp, step)
            for n in range(2):
                sp.wait_ge(store_done[n], 16 * NT // 2)
                sp.wait_ge(scatter_done[n], 16 * NT // 2)

        @block.gpsimd
        def _(pool):
            g = nc.gpsimd
            g.memset(ident[:], 0.0).then_inc(S["consts"], 1)
            g.memset(tri[:], 0.0).then_inc(S["consts"], 1)
            g.memset(ones[:], 1.0).then_inc(S["consts"], 1)
            g.memset(halves[:], -0.5).then_inc(S["consts"], 1)
            g.memset(mask_add[:, SK:SKP], MASKED).then_inc(S["consts"], 1)
            for n in range(2):
                for part in (ctxT_hi[n], ctxT_lo[n]):
                    g.memset(part[:, :, SK:SKP].bitcast(F32), 0.0).then_inc(S["consts"], 1)
            g.iota(rank[:], pattern=[[0, QT], [-1, EXPERTS]], base=EXPERTS, channel_multiplier=0,
                   allow_small_or_imprecise_dtypes=True).then_inc(S["consts"], 1)
            g.iota(token[:], pattern=[[P, QT]], base=0, channel_multiplier=1,
                   allow_small_or_imprecise_dtypes=True).then_inc(S["consts"], 1)
            pool.wait_ge(S["consts"], 11)
            g.affine_select(out=ident[:], in_=ident[:], compare_op=ALU.not_equal, fill=1.0, base=0,
                            pattern=[[-1, P]], channel_multiplier=1).then_inc(S["consts"], 1)
            g.affine_select(out=tri[:], in_=tri[:], compare_op=ALU.is_ge, fill=1.0, base=0,
                            pattern=[[-1, P]], channel_multiplier=1).then_inc(S["consts"], 1)
            g.memset(blank[:, 0:D + 3], 0.0).then_inc(S["blank_set"], 1)
            g.memset(blank[:, D + 3:ROW], NOWHERE).then_inc(S["blank_set"], 1)
            g.memset(countb[:], 0.0).then_inc(S["blank_set"], 1)
            pool.wait_ge(S["wv_hi_set"], 1)
            g.tensor_tensor(out=wv_lo[:], in0=wv[:], in1=wv_hi[:].bitcast(F32), op=ALU.subtract) \
                .then_inc(S["wv_lo_set"], 1)
            pool.wait_ge(S["bcast_in"], 48)

            def low_part(at, b, r):
                j0, j1 = PIECES[r]
                full = min(j1, JF)
                par = b % 2
                pool.wait_ge(S["ctx_hi_done"], at.count(lambda t: t + QT + 1))
                last = g.tensor_tensor(out=ctx_lo[par][:, j0:full, :], in0=ctx_in[:, j0:full, :],
                                       in1=ctx_hi[par][:, j0:full, :].bitcast(F32), op=ALU.subtract)
                if j1 == JT:
                    last = g.tensor_tensor(out=ctx_lo[par][0:JR, JF, :], in0=ctx_in[0:JR, JF, :],
                                           in1=ctx_hi[par][0:JR, JF, :].bitcast(F32), op=ALU.subtract)
                last.then_inc(S["ctx_lo_done"], 1)

            def step(at):
                t, b, r = at.t, at.batch, at.quarter
                if tile_ok(t - 3):
                    pool.wait_ge(S["var2"], at.count(lambda t: t - 2))
                    k = (t - 3) // QT % 2
                    g.tensor_tensor(out=row[k][:, (t - 3) % QT, D + 1:D + 2], in0=ve2[:], in1=halves[:, 0:1],
                                    op=ALU.pow).then_inc(S["rstd2"], 1)
                if batch_ok(b + 1) and r == 0:
                    pool.wait_ge(S["varx"], at.count(lambda t: t // QT + 2))
                    g.tensor_tensor(out=rstdx[:], in0=vex[:], in1=halves[:], op=ALU.pow).then_inc(S["rstdx"], 1)
                if tile_ok(t - 2):
                    pool.wait_ge(S["var1"], at.count(lambda t: t - 1))
                    g.tensor_tensor(out=rstd1[:], in0=ve1[:], in1=halves[:, 0:1], op=ALU.pow).then_inc(S["rstd1"], 1)
                if batch_ok(b + 1) and r == 2:
                    pool.wait_ge(S["turn_full"], at.count(nth(TURN_NO, ("xn", b + 1, 1), t, QT)))
                    g.tensor_tensor(out=xb[:], in0=xb[:], in1=kbias[:].unsqueeze(1).broadcast_to([P, QT, D]),
                                    op=ALU.mult).then_inc(S["kb_prod_set"], 1)
                if batch_ok(b - 2):
                    k = b % 2
                    if r == 0:
                        slot_ready, gate_done, token_set = at.ahead(
                            pool, lambda t: t // QT - 1, lambda t: t // QT - 1, lambda t: t // QT - 1)
                        pool.wait_ge(*MET)
                        pool.wait_ge(S["slot_ready"], slot_ready)
                        pool.wait_ge(S["gate_done"], gate_done)
                        pool.wait_ge(S["token_set"], token_set)
                    if t == 2 * QT:
                        pool.wait_ge(S["blanks_out"], 2 * QT * 16)
                    for i in range(QT) if b - 2 == NB - 1 else SCATTERED[r]:
                        g.indirect_dma_start(
                            out=slots, out_offset=bass.IndirectOffsetOnAxis(ap=slot[k][:, i:i + 1], axis=0),
                            in_=row[k][:, i, :], in_offset=None, bounds_check=TOKENS - 1, oob_is_err=False) \
                            .then_inc(scatter_done[k], 16)
                if batch_ok(b + 1):
                    low_part(at, b + 1, r)
                if tile_ok(t - 1):
                    pool.wait_ge(xres_in[(t - 1) % 4], at.count(lambda t: 16 * ((t - 1) // 4 + 1)))
                    g.tensor_tensor(out=xres[(t - 1) % 4][:], in0=xres[(t - 1) % 4][:], in1=beta_all[:],
                                    op=ALU.add).then_inc(S["xres_beta"], 1)
                if t == W1_STEP + 2:
                    pool.wait_ge(W["w1_hi_set"], HB)
                    g.tensor_tensor(out=w1_lo, in0=w1_in, in1=w1_hi.bitcast(F32), op=ALU.subtract) \
                        .then_inc(W["w1_lo_set"], HB)
                if t == W1_STEP + 3:
                    pool.wait_ge(W["w2_hi_set"], HB)
                    g.tensor_tensor(out=w2_lo, in0=w2_in, in1=w2_hi.bitcast(F32), op=ALU.subtract) \
                        .then_inc(W["w2_lo_set"], HB)

            ATTENTION.run(pool, step)

        @block.scalar
        def _(act):
            a = nc.scalar

            def evac(at, group, t0, per, out, in_, **kw):
                act.wait_ge(S["turn_full"], at.count(nth(TURN_NO, group, t0, per)))
                a.activation(out, in_, kw.pop("func", ACT.Copy), **kw).then_inc(S["turn_evac"], 1)

            def ctx_high(at, i):
                par = (at.batch + 1) % 2
                g = ("ctx", at.batch + 1, i)
                keys = piece_keys(i // 2)
                evac(at, g, at.t, QT, ctxT_hi[par][:, i % 2, keys], turn[TURN_NO[g] % 2][:, 0:keys.stop - keys.start])

            def qk_high(at, m):
                g = ("qk", at.batch + 1, m)
                evac(at, g, at.t, QT, qkT_hi[(at.batch + 1) % 2][:, m, :], turn[TURN_NO[g] % 2][:],
                     func=ACT.Identity, bias=qbias[:, m:m + 1])

            for n, dst in enumerate((wq_t, wk_t, mqk_hi)):
                act.wait_ge(S["turn_full"], n + 1)
                a.activation(dst[:].rearrange("p k n -> p (k n)"), turn[n % 2][:], ACT.Copy).then_inc(S["turn_evac"], 1)
            act.wait_ge(S["weights_in"], 32)
            a.activation(wv_hi[:], wv[:], ACT.Copy).then_inc(S["wv_hi_set"], 1)

            def step(at):
                t, b, r = at.t, at.batch, at.quarter
                if tile_ok(t - 2):
                    g = ("attn", t - 2, 0)
                    evac(at, g, t, 1, attnT_hi[:].rearrange("p k q -> p (k q)"), turn[TURN_NO[g] % 2][:, 0:KT * P])
                for c in range(NC):
                    if tile_ok(t - 1):
                        g = ("probs", t - 1, c)
                        bank = turn[TURN_NO[g] % 2]
                        if c < NC - 1:
                            dst, src = probsT_hi[:, 4 * c:4 * c + 4, :].rearrange("p j q -> p (j q)"), bank[:]
                        else:
                            dst, src = probsT_hi[0:JR, JF, :], bank[0:JR, 0:P]
                        evac(at, g, t, 1, dst, src)
                    if batch_ok(b + 1) and r == 3:
                        act.wait_ge(S["kb_prod_set"], at.count(lambda t: t // QT + 2))
                        a.activation(xb[:, c, :], xb[:, c, :], ACT.Copy, accum_out=kb_sum[:, c:c + 1]) \
                            .then_inc(S["kb_sum_set"], 1)
                if batch_ok(b + 1):
                    ctx_high(at, 2 * r)
                if tile_ok(t):
                    act.wait_ge(S["max_neg"], at.count(lambda t: t + 1))
                    a.activation(probs[:], probs[:], ACT.Exp, bias=negmax[:, t % 2:t % 2 + 1], scale=SCALE,
                                 accum_out=rowsum[:, t % 2:t % 2 + 1]).then_inc(S["exp_done"], 1)
                if batch_ok(b - 1) and r == 3:
                    act.wait_ge(S["below_set"], at.count(lambda t: t // QT))
                    a.activation(gates[:].rearrange("p i e -> p (i e)"), below[:].rearrange("p i e -> p (i e)"),
                                 ACT.Exp).then_inc(S["gates_done"], 1)
                if tile_ok(t - 3):
                    g = ("xn2", t - 3, 0)
                    evac(at, g, t, 1, xn2T[:].rearrange("p k q -> p (k q)"), turn[TURN_NO[g] % 2][:, 0:KT * P])
                if batch_ok(b + 1):
                    ctx_high(at, 2 * r + 1)
                    par = (b + 1) % 2
                    piece_in(at, act)
                    j0, j1 = PIECES[r]
                    full = min(j1, JF)
                    last = a.activation(ctx_hi[par][:, j0:full, :], ctx_in[:, j0:full, :], ACT.Copy)
                    if j1 == JT:
                        last = a.activation(ctx_hi[par][0:JR, JF, :], ctx_in[0:JR, JF, :], ACT.Copy)
                    last.then_inc(S["ctx_hi_done"], 1)
                if tile_ok(t - 1):
                    act.wait_ge(S["sum_inv"], at.count(lambda t: t))
                    act.wait_ge(S["out_full"], at.count(lambda t: t))
                    a.activation(attn[:], outp[:, 0:D], ACT.Copy, scale=rsum[:, (t - 1) % 2:(t - 1) % 2 + 1]) \
                        .then_inc(S["attn_ready"], 1)
                if batch_ok(b + 1) and r == 2:
                    qk_high(at, 0)
                    qk_high(at, 1)
                if tile_ok(t - 3):
                    act.wait_ge(S["small_full"], at.count(nth(SMALL_NO, ("logits", t - 3), t)))
                    if (t - 3) % QT == 0 and t - 3 > 0:
                        act.wait_ge(S["below_set"], at.count(lambda t: (t - 3) // QT))
                    a.activation(logits[:, (t - 3) % QT, :], small[:, 0:EXPERTS], ACT.Copy) \
                        .then_inc(S["logits_read"], 1)
                if batch_ok(b + 1):
                    if r == 1:
                        for k in range(KT):
                            g = ("xn", b + 1, k)
                            evac(at, g, t, QT, xnT_hi[:, k, :], turn[TURN_NO[g] % 2][:])
                if t == W1_STEP + 1:
                    act.wait_ge(W["w1_arrived"], 16)
                    act.wait_ge(S["scores_full"], NT - QT)
                    a.activation(w1_hi, w1_in, ACT.Copy).then_inc(W["w1_hi_set"], HB)
                if t == W1_STEP + 2:
                    act.wait_ge(W["w2_arrived"], 16)
                    act.wait_ge(S["out_full"], NT - QT)
                    a.activation(w2_hi, w2_in, ACT.Copy).then_inc(W["w2_hi_set"], HB)

            ATTENTION.run(act, step)

        @block.vector
        def _(dve):
            v = nc.vector
            TT, TS, STT = v.tensor_tensor, v.tensor_scalar, v.scalar_tensor_tensor

            dve.wait_ge(S["consts"], 13)
            dve.wait_ge(S["blank_set"], 3)
            v.memset(count[:], 0.0).then_inc(S["count_set"], 1)
            dve.wait_ge(S["wqk_in"], 64)
            for k in range(KT):
                last = v.tensor_copy(bkw[:, k, :], bk[:, k:k + 1].broadcast_to([P, P]))
            last.then_inc(S["setup_done"], 1)
            flat = lambda a: a.rearrange("p k n -> p (k n)")
            dve.wait_ge(S["turn_evac"], 3)
            TT(out=flat(mqk_lo[:]), in0=turn[0][:], in1=flat(mqk_hi[:]).bitcast(F32), op=ALU.subtract) \
                .then_inc(S["turn_low"], 1)
            dve.wait_ge(S["small_full"], 1)
            v.tensor_copy(qbias[:], small[:, 0:KT])
            v.tensor_copy(kbias[:], small[:, D:2 * D])
            v.tensor_copy(bqk[:], small[:, KT:KT + 1]).then_inc(S["small_read"], 1)
            dve.wait_ge(S["small_read"], 1)
            dve.wait_ge(S["bcast_in"], 48)

            def low(at, group, t0, per, out, psum, hi, bias=None):
                dve.wait_ge(S["turn_evac"], at.count(nth(TURN_NO, group, t0, per)))
                if bias is None:
                    ins = TT(out=out, in0=psum, in1=hi.bitcast(F32), op=ALU.subtract)
                else:
                    ins = STT(out=out, in0=psum, scalar=bias, in1=hi.bitcast(F32), op0=ALU.add, op1=ALU.subtract)
                ins.then_inc(S["turn_low"], 1)

            def probs_low(at, c):
                t = at.t
                g = ("probs", t - 1, c)
                bank = turn[TURN_NO[g] % 2]
                if c < NC - 1:
                    sl = lambda a: a[:, 4 * c:4 * c + 4, :].rearrange("p j q -> p (j q)")
                    low(at, g, t, 1, sl(probsT_lo), bank[:], sl(probsT_hi))
                else:
                    low(at, g, t, 1, probsT_lo[0:JR, JF, :], bank[0:JR, 0:P], probsT_hi[0:JR, JF, :])

            def qk_low(at, m):
                par, g = (at.batch + 1) % 2, ("qk", at.batch + 1, m)
                low(at, g, at.t, QT, qkT_lo[par][:, m, :], turn[TURN_NO[g] % 2][:], qkT_hi[par][:, m, :],
                    bias=qbias[:, m:m + 1])

            def mask_prep(at):
                dve.wait_ge(S["mask_in"], at.count(lambda t: 16 * (t + 1)))
                TS(mask_add[:, 0:SK], mask_in[:], 0.0, MASKED, ALU.is_equal, ALU.mult) \
                    .then_inc(S["mask_ready"], 1)

            def ctx_low(at, i):
                par = (at.batch + 1) % 2
                g = ("ctx", at.batch + 1, i)
                keys = piece_keys(i // 2)
                low(at, g, at.t, QT, ctxT_lo[par][:, i % 2, keys], turn[TURN_NO[g] % 2][:, 0:keys.stop - keys.start],
                    ctxT_hi[par][:, i % 2, keys])

            def step(at):
                t, b, r = at.t, at.batch, at.quarter
                if tile_ok(t - 1):
                    dve.wait_ge(S["exp_done"], at.count(lambda t: t))
                    v.reciprocal(rsum[:, (t - 1) % 2:(t - 1) % 2 + 1], rowsum[:, (t - 1) % 2:(t - 1) % 2 + 1]) \
                        .then_inc(S["sum_inv"], 1)
                if tile_ok(t - 2):
                    g = ("attn", t - 2, 0)
                    flat = lambda a: a.rearrange("p k q -> p (k q)")
                    low(at, g, t, 1, flat(attnT_lo[:]), turn[TURN_NO[g] % 2][:, 0:KT * P], flat(attnT_hi[:]))
                if tile_ok(t):
                    mask_prep(at)
                if tile_ok(t - 1):
                    probs_low(at, 0)
                router(at, 0)
                if tile_ok(t - 3):
                    k, i = (t - 3) // QT % 2, (t - 3) % QT
                    x1 = row[k][:, i, 0:D]
                    dve.wait_ge(S["rstd1"], at.count(lambda t: t - 2))
                    dve.wait_ge(S["xres_beta"], at.count(lambda t: t - 2))
                    dve.wait_ge(S["scaled_set"], at.count(lambda t: t - 2))
                    if i == 0 and (t - 3) // QT >= 2:
                        dve.wait_ge(store_done[k], at.count(lambda t: 16 * QT * ((t - 3) // QT // 2)))
                        dve.wait_ge(scatter_done[k], at.count(lambda t: 16 * QT * ((t - 3) // QT // 2)))
                    STT(out=x1, in0=scaled[:], scalar=rstd1[:], in1=xres[(t - 3) % 4][:],
                        op0=ALU.mult, op1=ALU.add).then_inc(S["x1_done"], 1)
                if tile_ok(t - 1):
                    probs_low(at, 1)
                router(at, 1)
                if tile_ok(t - 3):
                    dve.wait_ge(S["x1_done"], at.count(lambda t: t - 2))
                    v.bn_stats(bn2[:], x1).then_inc(S["bn2_set"], 1)
                if tile_ok(t - 1):
                    probs_low(at, 2)
                router(at, 2)
                if tile_ok(t - 3):
                    bn2_set, = at.ahead(dve, lambda t: t - 2)
                    dve.wait_ge(*MET)
                    dve.wait_ge(S["bn2_set"], bn2_set)
                    v.bn_aggr(mv2[:], bn2[:]).then_inc(S["mv2_set"], 1)
                if tile_ok(t - 1):
                    probs_low(at, 3)
                router(at, 3)
                if tile_ok(t - 3):
                    dve.wait_ge(S["mv2_set"], at.count(lambda t: t - 2))
                    v.tensor_scalar_add(ve2[:], mv2[:, 1:2], EPS).then_inc(S["var2"], 1)
                    v.tensor_copy(row[k][:, i, D:D + 1], mv2[:, 0:1])
                router(at, 4)
                if tile_ok(t) and r == 0:
                    dve.wait_ge(S["kb_sum_set"], at.count(lambda t: QT * (t // QT + 1)))
                    TS(kb16[b % 2][:], kb_sum[:], bqk[:], SCALE, ALU.add, ALU.mult).then_inc(S["kb_set"], 1)
                if tile_ok(t):
                    o = t % 2
                    scores_full, mask_ready = at.ahead(dve, lambda t: t + 1, lambda t: t + 1)
                    dve.wait_ge(*MET)
                    dve.wait_ge(S["scores_full"], scores_full)
                    dve.wait_ge(S["mask_ready"], mask_ready)
                    v.tensor_tensor_reduce(out=probs[:].rearrange("p (c w) -> p c w", c=NC), in0=scores[:, :, 0:CW],
                                           in1=mask_add[:].rearrange("p (c w) -> p c w", c=NC), scale=1.0,
                                           scalar=-3e38, op0=ALU.add, op1=ALU.max,
                                           accum_out=rowmax[:, o:o + 1]).then_inc(S["max_raw"], 1)
                    kb = kb16[b % 2][:, r:r + 1]
                    if r == 0:
                        dve.wait_ge(S["kb_set"], at.count(lambda t: t // QT + 1))
                    dve.wait_ge(S["max_raw"], at.count(lambda t: t + 1))
                    STT(out=fullmax[:, o:o + 1], in0=rowmax[:, o:o + 1], scalar=SCALE, in1=kb,
                        op0=ALU.mult, op1=ALU.add).then_inc(S["max_full"], 1)
                    dve.wait_ge(S["max_full"], at.count(lambda t: t + 1))
                    TT(out=negmax[:, o:o + 1], in0=kb, in1=fullmax[:, o:o + 1], op=ALU.subtract) \
                        .then_inc(S["max_neg"], 1)
                if tile_ok(t - 2):
                    dve.wait_ge(S["small_full"], at.count(nth(SMALL_NO, ("value", t - 2), t)))
                    TT(out=value[:], in0=small[:, D:2 * D], in1=bv_all[:], op=ALU.add).then_inc(S["small_read"], 1)
                if tile_ok(t - 3):
                    k, i = (t - 3) // QT % 2, (t - 3) % QT
                    if tile_ok(t - 4):
                        dve.wait_ge(S["turn_full"], at.count(nth(TURN_NO, ("xn2", t - 4, 0), t)))
                    dve.wait_ge(S["rstd2"], at.count(lambda t: t - 2))
                    TS(xn2[:], row[k][:, i, 0:D], mv2[:, 0:1], row[k][:, i, D + 1:D + 2], ALU.subtract, ALU.mult) \
                        .then_inc(S["xn2_done"], 1)
                if batch_ok(b + 1):
                    ctx_low(at, 2 * r)
                if tile_ok(t - 2):
                    dve.wait_ge(S["small_read"], at.count(nth(SMALL_READ, ("value", t - 2), t)))
                    v.bn_stats(bn1[:], value[:]).then_inc(S["bn1_set"], 1)
                if batch_ok(b - 1) and r == 3:
                    places(at)
                if batch_ok(b + 1):
                    if r == 0:
                        dve.wait_ge(S["x_in"], at.count(lambda t: 16 * (t // QT + 2)))
                        for i in range(QT):
                            last = v.bn_stats(bnx[:, i, :], xb[:, i, :])
                        last.then_inc(S["bnx_set"], 1)
                    if r == 1:
                        dve.wait_ge(S["rstdx"], at.count(lambda t: t // QT + 2))
                        for i in range(QT):
                            last = TS(xb[:, i, :], xb[:, i, :], mvx[:, i, 0:1], rstdx[:, i:i + 1],
                                      ALU.subtract, ALU.mult)
                        last.then_inc(S["xnorm_done"], 1)
                if batch_ok(b + 1):
                    ctx_low(at, 2 * r + 1)
                if tile_ok(t - 2):
                    bn1_set, = at.ahead(dve, lambda t: t - 1)
                    dve.wait_ge(*MET)
                    dve.wait_ge(S["bn1_set"], bn1_set)
                    v.bn_aggr(mv1[:], bn1[:]).then_inc(S["mv1_set"], 1)
                    dve.wait_ge(S["mv1_set"], at.count(lambda t: t - 1))
                    v.tensor_scalar_add(ve1[:], mv1[:, 1:2], EPS).then_inc(S["var1"], 1)
                    STT(out=scaled[:], in0=value[:], scalar=mv1[:, 0:1], in1=gamma_all[:],
                        op0=ALU.subtract, op1=ALU.mult).then_inc(S["scaled_set"], 1)
                if batch_ok(b + 1):
                    if r == 0:
                        bnx_set, = at.ahead(dve, lambda t: t // QT + 2)
                        dve.wait_ge(*MET)
                        dve.wait_ge(S["bnx_set"], bnx_set)
                        for i in range(QT):
                            last = v.bn_aggr(mvx[:, i, :], bnx[:, i, :])
                        last.then_inc(S["mvx_set"], 1)
                        dve.wait_ge(S["mvx_set"], at.count(lambda t: t // QT + 2))
                        v.tensor_scalar_add(vex[:], mvx[:, :, 1], EPS).then_inc(S["varx"], 1)
                    if r == 1:
                        for k in range(KT):
                            g = ("xn", b + 1, k)
                            low(at, g, t, QT, xnT_lo[:, k, :], turn[TURN_NO[g] % 2][:], xnT_hi[:, k, :])
                    if r == 2:
                        qk_low(at, 0)
                        qk_low(at, 1)

            nbatch = lambda t: t // QT

            def router(at, part):
                if not (batch_ok(at.batch - 1) and at.quarter == 3):
                    return
                wide = lambda a: a.unsqueeze(2).broadcast_to([P, QT, EXPERTS])
                if part == 0:
                    dve.wait_ge(S["logits_read"], at.count(lambda t: t - 3))
                    v.tensor_reduce(best[:], logits[:], AX.X, ALU.max).then_inc(S["best_set"], 1)
                if part == 1:
                    dve.wait_ge(S["best_set"], at.count(nbatch))
                    TT(out=below[:], in0=logits[:], in1=wide(best[:]), op=ALU.subtract).then_inc(S["below_set"], 1)
                if part == 2:
                    dve.wait_ge(S["below_set"], at.count(nbatch))
                    STT(out=tied[:], in0=below[:], scalar=0.0, in1=rank[:], op0=ALU.is_equal, op1=ALU.mult) \
                        .then_inc(S["tied_set"], 1)
                if part == 3:
                    dve.wait_ge(S["tied_set"], at.count(nbatch))
                    v.tensor_reduce(pick[:], tied[:], AX.X, ALU.max).then_inc(S["pick_set"], 1)
                if part == 4:
                    dve.wait_ge(S["pick_set"], at.count(nbatch))
                    TT(out=onehot[:], in0=tied[:], in1=wide(pick[:]), op=ALU.is_equal).then_inc(S["onehot_done"], 1)

            def places(at):
                k = (at.batch - 1) % 2
                dve.wait_ge(S["small_full"], at.count(nth(SMALL_NO, ("places", at.batch - 1), at.t, QT)))
                TT(out=placed[:], in0=small[:, 32:32 + QT * EXPERTS].rearrange("p (i e) -> p i e", e=EXPERTS),
                   in1=onehot[:], op=ALU.mult).then_inc(S["small_read"], 1)
                v.tensor_reduce(added[:], onehot[:].rearrange("p i e -> p e i"), AX.X, ALU.add) \
                    .then_inc(S["added_set"], 1)
                dve.wait_ge(S["small_read"], at.count(nth(SMALL_READ, ("places", at.batch - 1), at.t, QT)))
                v.tensor_reduce(place[:], placed[:], AX.X, ALU.add).then_inc(S["place_set"], 1)
                if at.batch - 1 > 0:
                    dve.wait_ge(S["token_next"], at.count(lambda t: t // QT - 1))
                v.tensor_copy(row[k][:, :, D + 3], token[:]).then_inc(S["token_set"], 1)
                dve.wait_ge(S["added_set"], at.count(nbatch))
                TT(out=count[:], in0=count[:], in1=added[:], op=ALU.add).then_inc(S["count_set"], 1)
                dve.wait_ge(S["place_set"], at.count(nbatch))
                TS(base[:], pick[:], -float(CAP), float(EXPERTS * CAP), ALU.mult, ALU.add).then_inc(S["base_set"], 1)
                TS(over[:], place[:], float(CAP), NOWHERE, ALU.is_ge, ALU.mult).then_inc(S["over_set"], 1)
                dve.wait_ge(S["token_set"], at.count(nbatch))
                v.tensor_scalar_add(token[:], token[:], float(SQ)).then_inc(S["token_next"], 1)
                dve.wait_ge(S["count_set"], at.count(lambda t: t // QT + 1))
                v.tensor_copy(countb[:], count[:]).then_inc(S["countb_set"], 1)
                dve.wait_ge(S["base_set"], at.count(nbatch))
                TT(out=slotf[:], in0=base[:], in1=place[:], op=ALU.add).then_inc(S["part_set"], 1)
                dve.wait_ge(S["over_set"], at.count(nbatch))
                dve.wait_ge(S["part_set"], at.count(nbatch))
                TT(out=slot[k][:], in0=slotf[:], in1=over[:], op=ALU.add).then_inc(S["slot_ready"], 1)
                dve.wait_ge(S["gates_done"], at.count(nbatch))
                v.tensor_reduce(gsum[:], gates[:], AX.X, ALU.add).then_inc(S["gsum_set"], 1)
                dve.wait_ge(S["gsum_set"], at.count(nbatch))
                v.reciprocal(row[k][:, :, D + 2], gsum[:]).then_inc(S["gate_done"], 1)

            ATTENTION.run(dve, step)

        @block.tensor
        def _(pe):
            mm = nc.tensor.matmul

            def turn_bank(at, group, t0, per):
                n = TURN_NO[group]
                before = TURNS[n - 2]

                def shifted(table):
                    def f(t):
                        kind, of, *rest = group
                        return table(TURNS[TURN_NO[(kind, of + (t - t0) // per, *rest)] - 2])
                    return f
                if before[0] in SPLIT_KINDS:
                    pe.wait_ge(S["turn_low"], at.count(shifted(lambda g: SPLITS[g] + 1)))
                else:
                    pe.wait_ge(S["turn_evac"], at.count(shifted(lambda g: TURN_NO[g] + 1)))
                return turn[n % 2]

            def small_free(at, group, t0, per=1):
                before = SMALLS[SMALL_NO[group] - 1]

                def prior(t):
                    g = SMALLS[nth(SMALL_NO, group, t0, per)(t) - 2]
                    assert g[0] == before[0]
                    return g[1] + 1 if g[0] in READ_BY_ACT else SMALL_READ[g] + 1
                pe.wait_ge(S["logits_read" if before[0] in READ_BY_ACT else "small_read"], at.count(prior))

            def three(out, w_hi, w_lo, m_hi, m_lo, first, last):
                mm(out, w_hi, m_hi, start=first, stop=False)
                mm(out, w_hi, m_lo, start=False, stop=False)
                return mm(out, w_lo, m_hi, start=False, stop=last)

            pe.wait_ge(S["consts"], 13)
            pe.wait_ge(S["wqk_in"], 64)
            for n, w in enumerate((wq, wk)):
                for k in range(KT):
                    for m in range(KT):
                        last = nc.tensor.transpose(turn[n][:, k * D + m * P:k * D + m * P + P],
                                                   w[:, m, k * P:k * P + P], ident[:])
                last.then_inc(S["turn_full"], 1)
            pe.wait_ge(S["turn_evac"], 2)
            for m in range(KT):
                for k in range(KT):
                    last = mm(turn[0][:, m * D:m * D + D], wq_t[:, k, m * P:m * P + P], wk_t[:, k, :],
                              start=(k == 0), stop=(k == KT - 1))
            last.then_inc(S["turn_full"], 1)
            pe.wait_ge(S["setup_done"], 1)
            for m in range(KT):
                for k in range(KT):
                    mm(small[:, m:m + 1], wk_t[:, k, m * P:m * P + P], bq[:, k:k + 1], start=(k == 0), stop=(k == KT - 1))
            for k in range(KT):
                mm(small[:, KT:KT + 1], bkw[:, k, :], bq[:, k:k + 1], start=(k == 0), stop=(k == KT - 1))
            for k in range(KT):
                last = mm(small[:, D:2 * D], bkw[:, k, :], wq_t[:, k, :], start=(k == 0), stop=(k == KT - 1))
            last.then_inc(S["small_full"], 1)

            def score_chunk(at, c):
                t, b, r = at.t, at.batch, at.quarter
                par = b % 2
                if c == 0:
                    if tile_ok(t - 1):
                        pe.wait_ge(S["max_raw"], at.count(lambda t: t))
                    if r == 0:
                        pe.wait_ge(S["turn_low"], at.count(nth(SPLITS, ("qk", b, 1), t, QT)))
                if r == 0 and c == NC - 1:
                    pe.wait_ge(S["turn_low"], at.count(nth(SPLITS, ("ctx", b, 2 * c + 1), t, QT)))
                sl = slice(c * CW, c * CW + CW)
                q = slice(r * P, r * P + P)
                for k in range(KT):
                    last = three(scores[:, c, 0:CW], qkT_hi[par][:, k, q], qkT_lo[par][:, k, q],
                                 ctxT_hi[par][:, k, sl], ctxT_lo[par][:, k, sl], k == 0, k == KT - 1)
                if c == NC - 1:
                    last.then_inc(S["scores_full"], 1)

            def probs_turn(at, c):
                t = at.t
                if c == 0:
                    pe.wait_ge(S["exp_done"], at.count(lambda t: t))
                bank = turn_bank(at, ("probs", t - 1, c), t, 1)
                for j in range(4 * c, min(4 * c + 4, JT)):
                    n = P if j < JF else JR
                    o = (j - 4 * c) * P
                    last = nc.tensor.transpose(bank[0:n, o:o + P], probs[:, j * P:j * P + n], ident[:])
                last.then_inc(S["turn_full"], 1)

            def attend(at, j0, j1):
                t = at.t
                par = (t - 1) // QT % 2
                if j0 == 0:
                    if tile_ok(t - 2):
                        pe.wait_ge(S["attn_ready"], at.count(lambda t: t - 1))
                    if (t - 1) % QT == 0:
                        pe.wait_ge(S["ctx_lo_done"], at.count(lambda t: (t - 1) + QT))
                for j in range(j0, j1):
                    n = P if j < JF else JR
                    if j % 4 == 0:
                        pe.wait_ge(S["turn_low"], at.count(nth(SPLITS, ("probs", t - 1, j // 4), t)))
                    last = three(outp[:, 0:D], probsT_hi[0:n, j, :], probsT_lo[0:n, j, :],
                                 ctx_hi[par][0:n, j, :], ctx_lo[par][0:n, j, :], j == 0, j == JT - 1)
                if j1 == JT:
                    last.then_inc(S["out_full"], 1)

            def ctx_turn(at, i):
                bank = turn_bank(at, ("ctx", at.batch + 1, i), at.t, QT)
                k, (j0, j1) = i % 2, PIECES[i // 2]
                for j in range(j0, j1):
                    n = P if j < JF else JR
                    o = (j - j0) * P
                    last = nc.tensor.transpose(bank[:, o:o + n], ctx_in[0:n, j, k * P:k * P + P], ident[0:n, 0:n])
                last.then_inc(S["turn_full"], 1)

            def qk_product(at, m):
                if m == 0:
                    pe.wait_ge(S["turn_low"], at.count(nth(SPLITS, ("xn", at.batch + 1, 1), at.t, QT)))
                bank = turn_bank(at, ("qk", at.batch + 1, m), at.t, QT)
                sl = slice(m * P, m * P + P)
                for k in range(KT):
                    last = three(bank[:], mqk_hi[:, k, sl], mqk_lo[:, k, sl],
                                 xnT_hi[:, k, :], xnT_lo[:, k, :], k == 0, k == KT - 1)
                last.then_inc(S["turn_full"], 1)

            def attn_turn(at):
                t = at.t
                pe.wait_ge(S["attn_ready"], at.count(lambda t: t - 1))
                bank = turn_bank(at, ("attn", t - 2, 0), t, 1)
                for k in range(KT):
                    last = nc.tensor.transpose(bank[:, k * P:k * P + P], attn[:, k * P:k * P + P], ident[:])
                last.then_inc(S["turn_full"], 1)

            def step(at):
                t, b, r = at.t, at.batch, at.quarter
                for c in range(NC):
                    if tile_ok(t):
                        score_chunk(at, c)
                    if c == 0 and tile_ok(t - 2):
                        attn_turn(at)
                    if tile_ok(t - 1):
                        probs_turn(at, c)
                if tile_ok(t - 1):
                    attend(at, 0, 2)
                if batch_ok(b + 1):
                    piece_in(at, pe)
                    ctx_turn(at, 2 * r)
                if tile_ok(t - 1):
                    attend(at, 2, 4)
                if tile_ok(t - 2):
                    pe.wait_ge(S["turn_low"], at.count(nth(SPLITS, ("attn", t - 2, 0), t)))
                    small_free(at, ("value", t - 2), t)
                    for k in range(KT):
                        last = three(small[:, D:2 * D], attnT_hi[:, k, :], attnT_lo[:, k, :],
                                     wv_hi[:, k, :], wv_lo[:, k, :], k == 0, k == KT - 1)
                    last.then_inc(S["small_full"], 1)
                if tile_ok(t - 1):
                    attend(at, 4, 10)
                if batch_ok(b - 1) and r == 3:
                    pe.wait_ge(S["onehot_done"], at.count(lambda t: t // QT))
                    if b - 1 > 0:
                        pe.wait_ge(S["countb_set"], at.count(lambda t: t // QT - 1))
                    small_free(at, ("places", b - 1), t, QT)
                    flat = lambda a: a.rearrange("p i e -> p (i e)")
                    region = small[:, 32:32 + QT * EXPERTS]
                    mm(region, tri[:], flat(onehot[:]), start=True, stop=False)
                    for back in range(1, QT):
                        mm(region[:, back * EXPERTS:], ones[:], flat(onehot[:, 0:QT - back, :]),
                           start=False, stop=False)
                    mm(region, ones[:], countb[:].unsqueeze(1).broadcast_to([P, QT, EXPERTS]), start=False, stop=True) \
                        .then_inc(S["small_full"], 1)
                if tile_ok(t - 3):
                    pe.wait_ge(S["xn2_done"], at.count(lambda t: t - 2))
                    bank = turn_bank(at, ("xn2", t - 3, 0), t, 1)
                    for k in range(KT):
                        last = nc.tensor.transpose(bank[:, k * P:k * P + P], xn2[:, k * P:k * P + P], ident[:])
                    last.then_inc(S["turn_full"], 1)
                if batch_ok(b + 1):
                    ctx_turn(at, 2 * r + 1)
                if tile_ok(t - 1):
                    attend(at, 10, JT)
                if batch_ok(b + 1) and r == 2:
                    qk_product(at, 0)
                    qk_product(at, 1)
                if tile_ok(t - 3):
                    pe.wait_ge(S["turn_evac"], at.count(nth(TURN_NO, ("xn2", t - 3, 0), t)))
                    small_free(at, ("logits", t - 3), t)
                    for k in range(KT):
                        last = mm(small[:, 0:EXPERTS], xn2T[:, k, :], wg[:, k, :], start=(k == 0), stop=(k == KT - 1))
                    last.then_inc(S["small_full"], 1)
                if batch_ok(b + 1):
                    if r == 1:
                        pe.wait_ge(S["xnorm_done"], at.count(lambda t: t // QT + 2))
                        for k in range(KT):
                            bank = turn_bank(at, ("xn", b + 1, k), t, QT)
                            for i in range(QT):
                                last = nc.tensor.transpose(bank[:, i * P:i * P + P], xb[:, i, k * P:k * P + P],
                                                           ident[:])
                            last.then_inc(S["turn_full"], 1)

            pe.wait_ge(S["weights_in"], 32)
            pe.wait_ge(S["wv_lo_set"], 1)
            ATTENTION.run(pe, step)


LAG = 2
HB = HID // P
SG = 512
GROUPS = CAP // SG
ST = SG // P
UNITS = EXPERTS * GROUPS * HB
PER = GROUPS * HB
EXPERT_PIPE = Pipeline("experts", -HB, PER, PER, EXPERTS - 2, UNITS + LAG + 1)


WEIGHTS_SEMS = "w1_arrived w2_arrived w1_hi_set w1_lo_set w2_hi_set w2_lo_set".split()


def weight_places(keep):
    n1 = KT * HID // D
    w2_in = keep["room"][:, n1:n1 + HB, :]
    w1_in = keep["room"][:, 0:n1, :].rearrange("p (k a) d -> p k (a d)", k=KT)
    return (w1_in, w2_in, keep["ctxT_hi0"][:, :, 0:HID], keep["ctxT_lo0"][:, :, 0:HID],
            keep["ctx_hi0"][:, 0:HB, :], keep["ctx_lo0"][:, 0:HB, :])


def experts(nc, dram, keep):
    with ExitStack() as ctx:
        def sb(name, shape, dt=F32):
            return ctx.enter_context(nc.sbuf_tensor(name, shape, dt))

        def sem(name):
            return ctx.enter_context(nc.semaphore(name))

        ident = keep["ident"]
        w1_in, w2_in, w1_hi, w1_lo, w2_hi, w2_lo = weight_places(keep)
        b1_in = sb("b1_in", [EXPERTS * HB, P])
        b1_t = sb("b1_t", [P, EXPERTS * HB])
        b2_all = sb("b2_all", [P, EXPERTS, D])
        rows = [sb(f"rows{n}", [P, ST, ROW]) for n in range(2)]
        token_of = [sb(f"token_of{n}", [P, ST], U32) for n in range(2)]
        xn = sb("xn", [P, ST, D])
        xT_hi = [sb(f"xT_hi{n}", [P, KT, SG], F32R) for n in range(2)]
        xT_lo = [sb(f"xT_lo{n}", [P, KT, SG], F32R) for n in range(2)]
        hid = [sb(f"hid{n}", [P, SG]) for n in range(4)]
        hid_hi = [sb(f"hid_hi{n}", [P, SG], F32R) for n in range(4)]
        hid_lo = [sb(f"hid_lo{n}", [P, SG], F32R) for n in range(4)]
        base = [sb(f"base{n}", [P, ST, D]) for n in range(2)]
        gate_of = [sb(f"gate_of{n}", [P, ST]) for n in range(2)]
        result = [sb(f"result{n}", [P, ST, D]) for n in range(2)]

        hps = [ctx.enter_context(nc.psum_tensor(f"hps{n}", [P, SG], F32)) for n in range(2)]
        xps = [ctx.enter_context(nc.psum_tensor(f"xps{n}", [P, SG], F32)) for n in range(KT)]
        acc = [ctx.enter_context(nc.psum_tensor(f"acc{n}", [P, SG], F32)) for n in range(ST)]

        S = {}
        for name in ("b1_in b2_in b1_full b1_set rows_in0 rows_in1 xn_set token_of_set "
                     "x_turned x_hi x_lo hid_full hid_set hid_hi_set hid_lo_set "
                     "hid_used acc_full base_set result_set out0 out1").split():
            S[name] = sem("e_" + name)
        S.update(keep["weights_sems"])
        MET = (S["b1_in"], 16)
        rows_in = [S["rows_in0"], S["rows_in1"]]
        out_done = [S["out0"], S["out1"]]
        slots_v = dram["slots"].rearrange("(g p n) w -> g p n w", g=EXPERTS * GROUPS, p=P)
        w1_v = dram["w1"].rearrange("e (k p) h -> e p k h", p=P)
        w2_v = dram["w2"].rearrange("e (h p) n -> e p h n", p=P)
        out_rows = dram["out"].rearrange("b q d -> (b q) d")

        unit_ok = lambda n: 0 <= n < UNITS
        group_ok = lambda g: 0 <= g < EXPERTS * GROUPS
        refresh_ok = lambda n: n >= 0 and n // HB % 2 == 1 and 0 <= n // PER + 1 < EXPERTS
        refreshed = lambda n: (n // PER + 1) * HB + n % HB + 1

        block = ctx.enter_context(nc.Block())

        @block.sync
        def _(sp):
            def load(at, dst, src, arrived, split, e_of):
                blocks_split, = at.ahead(sp, lambda n: HB * e_of(n))
                sp.wait_ge(*MET)
                sp.wait_ge(split, blocks_split)
                sp.dma_start(dst, src[at.value(e_of)]).then_inc(arrived, 16)

            def load_rows(at, g_of):
                g = g_of(at.t)
                if g >= 2:
                    base_set, = at.ahead(sp, lambda n: ST * (g_of(n) - 1))
                    sp.wait_ge(*MET)
                    sp.wait_ge(S["base_set"], base_set)
                sp.dma_start(rows[g % 2][:], slots_v[at.value(g_of)]).then_inc(rows_in[g % 2], 16)

            def step(at):
                n = at.t
                g, hb = n // HB, n % HB
                if n == -HB:
                    load_rows(at, lambda n: 0)
                    sp.dma_start(b1_in[:], dram["b1"].rearrange("e (h p) -> (e h) p", p=P)).then_inc(S["b1_in"], 16)
                    sp.dma_start(b2_all[:], dram["b2"].partition_broadcast(P)).then_inc(S["b2_in"], 16)
                new_expert = n >= 0 and n // PER + 1 < EXPERTS
                if new_expert and n % PER == 0:
                    load(at, w1_in, w1_v, S["w1_arrived"], S["w1_lo_set"], lambda n: n // PER + 1)
                if new_expert and n % PER == LAG:
                    load(at, w2_in, w2_v, S["w2_arrived"], S["w2_lo_set"], lambda n: n // PER + 1)
                if hb == 6 and group_ok(g + 2):
                    load_rows(at, lambda n: n // HB + 2)

            EXPERT_PIPE.run(sp, step)
            for n in range(2):
                sp.wait_ge(out_done[n], 16 * ST * EXPERTS * GROUPS // 2)

        @block.gpsimd
        def _(pool):
            g_ = nc.gpsimd

            def step(at):
                n = at.t
                grp, hb = n // HB, n % HB
                if refresh_ok(n):
                    blk = slice(hb * P, hb * P + P)
                    pool.wait_ge(S["w1_hi_set"], at.count(refreshed))
                    g_.tensor_tensor(out=w1_lo[:, :, blk], in0=w1_in[:, :, blk], in1=w1_hi[:, :, blk].bitcast(F32),
                                     op=ALU.subtract).then_inc(S["w1_lo_set"], 1)
                if refresh_ok(n - LAG):
                    b2 = (n - LAG) % HB
                    pool.wait_ge(S["w2_hi_set"], at.count(lambda n: refreshed(n - LAG)))
                    g_.tensor_tensor(out=w2_lo[:, b2, :], in0=w2_in[:, b2, :], in1=w2_hi[:, b2, :].bitcast(F32),
                                     op=ALU.subtract).then_inc(S["w2_lo_set"], 1)
                if group_ok(grp - 1) and hb in (LAG, LAG + 1):
                    k = (grp - 1) % 2
                    for s in ((0, 1), (2, 3))[hb - LAG]:
                        result_set, = at.ahead(pool, lambda n: ST * (n // HB - 1) + s + 1)
                        pool.wait_ge(*MET)
                        pool.wait_ge(S["result_set"], result_set)
                        g_.indirect_dma_start(
                            out=out_rows, out_offset=bass.IndirectOffsetOnAxis(ap=token_of[k][:, s:s + 1], axis=0),
                            in_=result[k][:, s, :], in_offset=None, bounds_check=TOKENS - 1, oob_is_err=False) \
                            .then_inc(out_done[k], 16)

            EXPERT_PIPE.run(pool, step)

        @block.scalar
        def _(act):
            a = nc.scalar

            def step(at):
                n = at.t
                grp, hb = n // HB, n % HB
                if group_ok(grp + 1) and hb >= HB - KT:
                    k = hb - (HB - KT)
                    act.wait_ge(S["x_turned"], at.count(lambda n: KT * (n // HB + 1) + k + 1))
                    a.activation(xT_hi[(grp + 1) % 2][:, k, :], xps[k][:], ACT.Copy).then_inc(S["x_hi"], 1)
                if unit_ok(n):
                    act.wait_ge(S["hid_set"], at.count(lambda n: n + 1))
                    a.activation(hid_hi[n % 4][:], hid[n % 4][:], ACT.Copy).then_inc(S["hid_hi_set"], 1)
                if refresh_ok(n):
                    blk = slice(hb * P, hb * P + P)
                    act.wait_ge(S["w1_arrived"], at.count(lambda n: 16 * (n // PER + 2)))
                    if n >= 0:
                        act.wait_ge(S["hid_full"], at.count(lambda n: n + 1))
                    a.activation(w1_hi[:, :, blk], w1_in[:, :, blk], ACT.Copy).then_inc(S["w1_hi_set"], 1)
                if refresh_ok(n - LAG):
                    b2 = (n - LAG) % HB
                    act.wait_ge(S["w2_arrived"], at.count(lambda n: 16 * ((n - LAG) // PER + 2)))
                    if n - LAG >= 0:
                        act.wait_ge(S["hid_used"], at.count(lambda n: n - LAG + 1))
                    a.activation(w2_hi[:, b2, :], w2_in[:, b2, :], ACT.Copy).then_inc(S["w2_hi_set"], 1)

            EXPERT_PIPE.run(act, step)

        @block.vector
        def _(dve):
            v = nc.vector
            TT, TS, STT = v.tensor_tensor, v.tensor_scalar, v.scalar_tensor_tensor
            dve.wait_ge(S["b1_full"], 1)
            v.tensor_copy(b1_t[:], xps[0][:, 0:EXPERTS * HB]).then_inc(S["b1_set"], 1)
            dve.wait_ge(S["b1_set"], 1)

            def step(at):
                n = at.t
                grp, hb = n // HB, n % HB
                if group_ok(grp - 1) and hb == LAG:
                    k = (grp - 1) % 2
                    dve.wait_ge(S["token_of_set"], at.count(lambda n: 2 * (n // HB)))
                    dve.wait_ge(S["base_set"], at.count(lambda n: ST * (n // HB)))
                    for s in range(ST):
                        if s < ST - 1:
                            dve.wait_ge(S["acc_full"], at.count(lambda n: (ST - 1) * (n // HB - 1) + s + 1))
                        else:
                            dve.wait_ge(S["hid_used"], at.count(lambda n: n // HB * HB))
                        STT(out=result[k][:, s, :], in0=acc[s][:, 0:D], scalar=gate_of[k][:, s:s + 1],
                            in1=base[k][:, s, :], op0=ALU.mult, op1=ALU.add).then_inc(S["result_set"], 1)
                if group_ok(grp + 1) and hb >= HB - KT:
                    k = hb - (HB - KT)
                    dve.wait_ge(S["x_hi"], at.count(lambda n: KT * (n // HB + 1) + k + 1))
                    TT(out=xT_lo[(grp + 1) % 2][:, k, :], in0=xps[k][:], in1=xT_hi[(grp + 1) % 2][:, k, :].bitcast(F32),
                       op=ALU.subtract).then_inc(S["x_lo"], 1)
                if unit_ok(n):
                    dve.wait_ge(S["hid_full"], at.count(lambda n: n + 1))
                    col = at.value(lambda n: n // PER * HB + n % HB)
                    if n >= 4:
                        dve.wait_ge(S["hid_used"], at.count(lambda n: n - 3))
                    TS(hid[n % 4][:], hps[n % 2][:], b1_t[:, bass.ds(col, 1)], 0.0, ALU.add, ALU.max) \
                        .then_inc(S["hid_set"], 1)
                if unit_ok(n - 1):
                    dve.wait_ge(S["hid_hi_set"], at.count(lambda n: n))
                    j = (n - 1) % 4
                    TT(out=hid_lo[j][:], in0=hid[j][:], in1=hid_hi[j][:].bitcast(F32), op=ALU.subtract) \
                        .then_inc(S["hid_lo_set"], 1)
                k = grp % 2
                if group_ok(grp) and hb in (4, 5):
                    if n == 4:
                        dve.wait_ge(S["b2_in"], 16)
                    if hb == 4:
                        if grp >= 2:
                            dve.wait_ge(out_done[k], at.count(lambda n: 16 * ST * (n // HB // 2)))
                        v.tensor_copy(token_of[k][:], rows[k][:, :, D + 3]).then_inc(S["token_of_set"], 1)
                        v.tensor_copy(gate_of[k][:], rows[k][:, :, D + 2]).then_inc(S["token_of_set"], 1)
                    e = at.value(lambda n: n // PER)
                    for s in ((0, 1), (2, 3))[hb - 4]:
                        STT(out=base[k][:, s, :], in0=b2_all[:, bass.ds(e, 1), :].rearrange("p o d -> p (o d)"),
                            scalar=rows[k][:, s, D + 2:D + 3], in1=rows[k][:, s, 0:D],
                            op0=ALU.mult, op1=ALU.add).then_inc(S["base_set"], 1)
                if group_ok(grp + 1) and hb == HB - KT - 3:
                    k = (grp + 1) % 2
                    dve.wait_ge(rows_in[k], at.count(lambda n: 16 * ((n // HB + 1) // 2 + 1)))
                    if grp >= 0:
                        dve.wait_ge(S["x_turned"], at.count(lambda n: KT * (n // HB + 1)))
                    for i in range(ST):
                        last = TS(xn[:, i, :], rows[k][:, i, 0:D], rows[k][:, i, D:D + 1],
                                  rows[k][:, i, D + 1:D + 2], ALU.subtract, ALU.mult)
                    last.then_inc(S["xn_set"], 1)

            EXPERT_PIPE.run(dve, step)

        @block.tensor
        def _(pe):
            mm = nc.tensor.matmul

            def three(out, w_hi, w_lo, m_hi, m_lo, first, last):
                mm(out, w_hi, m_hi, start=first, stop=False)
                mm(out, w_hi, m_lo, start=False, stop=False)
                return mm(out, w_lo, m_hi, start=False, stop=last)

            pe.wait_ge(S["b1_in"], 16)
            nc.tensor.transpose(xps[0][:, 0:EXPERTS * HB], b1_in[:], ident[0:EXPERTS * HB, 0:EXPERTS * HB]) \
                .then_inc(S["b1_full"], 1)
            pe.wait_ge(S["b1_set"], 1)

            def step(at):
                n = at.t
                grp, hb = n // HB, n % HB
                if unit_ok(n):
                    if hb == 0:
                        pe.wait_ge(S["x_lo"], at.count(lambda n: KT * (n // HB + 1)))
                    if grp % 2 == 0:
                        pe.wait_ge(S["w1_lo_set"], at.count(lambda n: n // PER * HB + n % HB + 1))
                    if n >= 2:
                        pe.wait_ge(S["hid_set"], at.count(lambda n: n - 1))
                    blk = slice(hb * P, hb * P + P)
                    for k in range(KT):
                        last = three(hps[n % 2][:], w1_hi[:, k, blk], w1_lo[:, k, blk],
                                     xT_hi[grp % 2][:, k, :], xT_lo[grp % 2][:, k, :], k == 0, k == KT - 1)
                    last.then_inc(S["hid_full"], 1)
                if group_ok(grp + 1) and HB - KT - 1 <= hb < HB - 1:
                    k = hb - (HB - KT - 1)
                    if k == 0:
                        pe.wait_ge(S["xn_set"], at.count(lambda n: n // HB + 2))
                        if grp >= 0:
                            pe.wait_ge(S["x_lo"], at.count(lambda n: KT * (n // HB + 1)))
                    for i in range(ST):
                        last = nc.tensor.transpose(xps[k][:, i * P:i * P + P], xn[:, i, k * P:k * P + P], ident[:])
                    last.then_inc(S["x_turned"], 1)
                u = n - LAG
                if unit_ok(u):
                    ub = u % HB
                    if u // HB % 2 == 0:
                        pe.wait_ge(S["w2_lo_set"], at.count(lambda n: (n - LAG) // PER * HB + (n - LAG) % HB + 1))
                    pe.wait_ge(S["hid_lo_set"], at.count(lambda n: n - LAG + 1))
                    for s in range(ST):
                        if ub == 0 and u >= HB:
                            pe.wait_ge(S["result_set"], at.count(lambda n: ST * ((n - LAG) // HB - 1) + s + 1))
                        q = slice(s * P, s * P + P)
                        last = three(acc[s][:, 0:D], hid_hi[u % 4][:, q], hid_lo[u % 4][:, q],
                                     w2_hi[:, ub, :], w2_lo[:, ub, :], ub == 0, ub == HB - 1)
                        if ub == HB - 1 and s < ST - 1:
                            last.then_inc(S["acc_full"], 1)
                    last.then_inc(S["hid_used"], 1)

            EXPERT_PIPE.run(pe, step)


def build(nc, x, ctx_in, mask, wq, bq, wk, bk, wv, bv, gamma, beta, wg, w1, b1, w2, b2, out):
    dram = dict(x=x, ctx=ctx_in, mask=mask, wq=wq, bq=bq, wk=wk, bk=bk, wv=wv, bv=bv, gamma=gamma, beta=beta,
                wg=wg, w1=w1, b1=b1, w2=w2, b2=b2, out=out,
                slots=nc.dram_tensor("slots", [TOKENS, ROW], F32, kind="Internal").ap())
    with ExitStack() as ctx:
        keep = {name: ctx.enter_context(nc.sbuf_tensor(name, shape, dt)) for name, shape, dt in (
            ("ident", [P, P], F32), ("room", [P, JT + QT, D], F32),
            ("ctx_hi0", [P, JT, D], F32R), ("ctx_lo0", [P, JT, D], F32R),
            ("ctxT_hi0", [P, KT, SKP], F32R), ("ctxT_lo0", [P, KT, SKP], F32R))}
        keep["weights_sems"] = {name: ctx.enter_context(nc.semaphore(name)) for name in WEIGHTS_SEMS}
        attention(nc, dram, keep)
        experts(nc, dram, keep)


_INS = ["x", "ctx_1024", "mask_BxSxS2_ik1", "L0_xattn_Wq", "L0_xattn_bq", "L0_xattn_Wk", "L0_xattn_bk",
        "L0_xattn_Wv", "L0_xattn_bv", "L0_xattn_ln_gamma", "L0_xattn_ln_beta", "L0_ffn_wg", "L0_ffn_w1",
        "L0_ffn_b1", "L0_ffn_w2", "L0_ffn_b2"]


def kernel(**inputs):
    import numpy as _np
    import concourse.bacc as _bacc
    from concourse.bass_utils import run_bass_kernel_spmd as _run

    nc = _bacc.Bacc("TRN2", target_bir_lowering=False, num_devices=1)
    arrays, args = {}, []
    for name in _INS:
        a = _np.ascontiguousarray(inputs[name])
        arrays[f"in_{name}"] = a
        args.append(nc.dram_tensor(f"in_{name}", a.shape, mybir.dt.from_np(a.dtype), kind="ExternalInput").ap())
    out = nc.dram_tensor("out", (NB, SQ, D), F32, kind="ExternalOutput").ap()
    build(nc, *args, out)
    r = _run(nc, [arrays], core_ids=[0])
    return r.results[0]["out"]
```
